# Optimizing a Trainium2 kernel written in Bass

```python
import numpy as np
import jax
import jax.numpy as jnp

def _softmax(x, axis=-1):
    return jax.nn.softmax(x, axis=axis)

def _gelu(x):
    return jax.nn.gelu(x, approximate=True)

def _silu(x):
    return jax.nn.silu(x)

def _sigmoid(x):
    return jax.nn.sigmoid(x)

def _layernorm(x, axis=-1, eps=1e-05):
    m = jnp.mean(x, axis=axis, keepdims=True)
    v = jnp.var(x, axis=axis, keepdims=True)
    return (x - m) / jnp.sqrt(v + eps)

def _scatter_add(tgt, idx, src, axis=0):
    return tgt.at[idx].add(src)

def _segment_sum(src, seg, n):
    return jax.ops.segment_sum(src, seg, n)
kernel_name = 'mk_lm_tower_d1_tok_ids512_r4_b9d835'

def setup_inputs(seed: int=0):
    np.random.seed(seed)
    _w = jnp.asarray

    def _rec_inputs():
        import jax
        import jax.numpy as jnp
        _rk = jax.random.key(seed)
        x = jax.random.randint(jax.random.fold_in(_rk, 1), (16, 256), 0, 64, jnp.int32)
        return x
    x = _rec_inputs()

    def _L0_tok_setup():
        import jax, jax.numpy as jnp
        import numpy as np
        NGRAM_SIZES = (2, 3, 4)
        HASH_VOCAB = 25000
        EMBED_DIM = 128
        BATCH, SEQ = (8, 1024)

        def _ngram_hash_ids(byte_sequence, n):
            L = byte_sequence.shape[1] - n + 1
            h = jnp.zeros((byte_sequence.shape[0], L), dtype=jnp.int64)
            for j in range(n):
                h = (h * 64 + byte_sequence[:, j:j + L]) % HASH_VOCAB
            return h

        def _ngram_embed(byte_sequence, table, n):
            B, S = byte_sequence.shape
            ids = _ngram_hash_ids(byte_sequence, n)
            emb = table[ids]
            out = jnp.zeros((B, S, table.shape[1]), dtype=table.dtype)
            c = n // 2
            return out.at[:, c:c + emb.shape[1]].set(emb)
        key = jax.random.key(seed)
        ks = jax.random.split(key, 6)
        return {'byte_sequence': jax.random.randint(ks[0], (BATCH, SEQ), 0, 64, dtype=jnp.int64), 'emb_2': jax.random.normal(ks[1], (HASH_VOCAB, EMBED_DIM), dtype=jnp.float32), 'emb_3': jax.random.normal(ks[2], (HASH_VOCAB, EMBED_DIM), dtype=jnp.float32), 'emb_4': jax.random.normal(ks[3], (HASH_VOCAB, EMBED_DIM), dtype=jnp.float32), 'proj_w': jax.random.normal(ks[4], (EMBED_DIM, len(NGRAM_SIZES) * EMBED_DIM), dtype=jnp.float32) * 0.02, 'proj_b': jax.random.normal(ks[5], (EMBED_DIM,), dtype=jnp.float32) * 0.02}
    _L0_tok_all = _L0_tok_setup()
    _L0_tok_in = {k: v for k, v in _L0_tok_all.items() if k in ('emb_2', 'emb_3', 'emb_4', 'proj_w', 'proj_b')}
    del _L0_tok_all

    def _L0_attn_setup():
        import jax, jax.numpy as jnp
        import numpy as np
        THRE = 4.0
        EPS = 1e-05

        @jax.custom_vjp
        def spike(x):
            return jnp.floor(jnp.clip(x, 0.0, THRE) + 0.5)

        def _spike_fwd(x):
            return (spike(x), x)

        def _spike_bwd(x, g):
            return (g * ((x > 0) & (x < THRE)).astype(g.dtype),)
        spike.defvjp(_spike_fwd, _spike_bwd)
        key = jax.random.key(seed)
        k0, k1, k2 = jax.random.split(key, 3)
        B, N, C = (4, 256, 128)
        x = jax.random.normal(k0, (B, N, C), jnp.float32)
        Wqkv = jax.random.normal(k1, (3 * C, C), jnp.float32) * C ** (-0.5)
        gamma = jnp.ones((3 * C,), jnp.float32)
        beta = jnp.zeros((3 * C,), jnp.float32)
        Wproj = jax.random.normal(k2, (C, C), jnp.float32) * C ** (-0.5)
        bproj = jnp.zeros((C,), jnp.float32)
        return {'x': x, 'Wqkv': Wqkv, 'gamma': gamma, 'beta': beta, 'Wproj': Wproj, 'bproj': bproj}
    _L0_attn_all = _L0_attn_setup()
    _L0_attn_in = {k: v for k, v in _L0_attn_all.items() if k in ('Wqkv', 'gamma', 'beta', 'Wproj', 'bproj')}
    del _L0_attn_all

    def _L0_ffn_setup():
        import jax, jax.numpy as jnp
        import numpy as np
        H = 128
        I = 256
        E = 32
        K = 2
        key = jax.random.key(seed)
        ks = jax.random.split(key, 9)
        s = 0.02
        return {'hidden_states': jax.random.normal(ks[0], (2, 1024, H), dtype=jnp.float32), 'Wgate': jax.random.normal(ks[1], (H, E), dtype=jnp.float32) * s, 'bgate': jnp.zeros((E,), dtype=jnp.float32), 'Wg': jax.random.normal(ks[2], (E, H, I), dtype=jnp.float32) * s, 'bg': jnp.zeros((E, I), dtype=jnp.float32), 'Wu': jax.random.normal(ks[3], (E, H, I), dtype=jnp.float32) * s, 'bu': jnp.zeros((E, I), dtype=jnp.float32), 'Wd': jax.random.normal(ks[4], (E, I, H), dtype=jnp.float32) * s, 'bd': jnp.zeros((E, H), dtype=jnp.float32)}
    _L0_ffn_all = _L0_ffn_setup()
    _L0_ffn_in = {k: v for k, v in _L0_ffn_all.items() if k in ('Wgate', 'bgate', 'Wg', 'bg', 'Wu', 'bu', 'Wd', 'bd')}
    del _L0_ffn_all
    return {'x': x, 'L0_tok_emb_2': _L0_tok_in['emb_2'], 'L0_tok_emb_3': _L0_tok_in['emb_3'], 'L0_tok_emb_4': _L0_tok_in['emb_4'], 'L0_tok_proj_w': _L0_tok_in['proj_w'], 'L0_tok_proj_b': _L0_tok_in['proj_b'], 'L0_attn_Wqkv': _L0_attn_in['Wqkv'], 'L0_attn_gamma': _L0_attn_in['gamma'], 'L0_attn_beta': _L0_attn_in['beta'], 'L0_attn_Wproj': _L0_attn_in['Wproj'], 'L0_attn_bproj': _L0_attn_in['bproj'], 'L0_ffn_Wgate': _L0_ffn_in['Wgate'], 'L0_ffn_bgate': _L0_ffn_in['bgate'], 'L0_ffn_Wg': _L0_ffn_in['Wg'], 'L0_ffn_bg': _L0_ffn_in['bg'], 'L0_ffn_Wu': _L0_ffn_in['Wu'], 'L0_ffn_bu': _L0_ffn_in['bu'], 'L0_ffn_Wd': _L0_ffn_in['Wd'], 'L0_ffn_bd': _L0_ffn_in['bd']}

def reference(x, L0_tok_emb_2, L0_tok_emb_3, L0_tok_emb_4, L0_tok_proj_w, L0_tok_proj_b, L0_attn_Wqkv, L0_attn_gamma, L0_attn_beta, L0_attn_Wproj, L0_attn_bproj, L0_ffn_Wgate, L0_ffn_bgate, L0_ffn_Wg, L0_ffn_bg, L0_ffn_Wu, L0_ffn_bu, L0_ffn_Wd, L0_ffn_bd):
    import jax
    import jax.numpy as jnp

    def _L0_tok_ref(byte_sequence, emb_2, emb_3, emb_4, proj_w, proj_b):
        import jax, jax.numpy as jnp
        import numpy as np
        NGRAM_SIZES = (2, 3, 4)
        HASH_VOCAB = 25000
        EMBED_DIM = 128
        BATCH, SEQ = (8, 1024)

        def _ngram_hash_ids(byte_sequence, n):
            L = byte_sequence.shape[1] - n + 1
            h = jnp.zeros((byte_sequence.shape[0], L), dtype=jnp.int64)
            for j in range(n):
                h = (h * 64 + byte_sequence[:, j:j + L]) % HASH_VOCAB
            return h

        def _ngram_embed(byte_sequence, table, n):
            B, S = byte_sequence.shape
            ids = _ngram_hash_ids(byte_sequence, n)
            emb = table[ids]
            out = jnp.zeros((B, S, table.shape[1]), dtype=table.dtype)
            c = n // 2
            return out.at[:, c:c + emb.shape[1]].set(emb)
        tables = (emb_2, emb_3, emb_4)
        combined = jnp.concatenate([_ngram_embed(byte_sequence, t, n) for t, n in zip(tables, NGRAM_SIZES)], axis=-1)
        return jnp.einsum('bsk,dk->bsd', combined, proj_w) + proj_b

    def _L0_attn_ref(x, Wqkv, gamma, beta, Wproj, bproj):
        import jax, jax.numpy as jnp
        import numpy as np
        THRE = 4.0
        EPS = 1e-05

        @jax.custom_vjp
        def spike(x):
            return jnp.floor(jnp.clip(x, 0.0, THRE) + 0.5)

        def _spike_fwd(x):
            return (spike(x), x)

        def _spike_bwd(x, g):
            return (g * ((x > 0) & (x < THRE)).astype(g.dtype),)
        spike.defvjp(_spike_fwd, _spike_bwd)
        B, N, C = x.shape
        H = 8
        hd = C // H
        scale = hd ** (-0.5)
        xs = spike(x)
        qkv = jnp.einsum('bnc,dc->bnd', xs, Wqkv)
        mu = qkv.mean(axis=(0, 1))
        var = qkv.var(axis=(0, 1))
        qkv = (qkv - mu) * jax.lax.rsqrt(var + EPS) * gamma + beta
        qkv = qkv.reshape(B, N, 3, H, hd).transpose(2, 0, 3, 1, 4)
        q = spike(qkv[0])
        k = spike(qkv[1])
        v = spike(qkv[2])
        attn = jnp.einsum('bhnd,bhmd->bhnm', q, k)
        attn = spike(attn)
        out = jnp.einsum('bhnm,bhmd->bhnd', attn, v) * scale
        out = out.transpose(0, 2, 1, 3).reshape(B, N, C)
        out = spike(out)
        return jnp.einsum('bnc,dc->bnd', out, Wproj) + bproj

    def _L0_ffn_ref(hidden_states, Wgate, bgate, Wg, bg, Wu, bu, Wd, bd):
        import jax, jax.numpy as jnp
        import numpy as np
        H = 128
        I = 256
        E = 32
        K = 2
        B, S, Hs = hidden_states.shape
        x = hidden_states.reshape(-1, Hs)
        probs = jax.nn.softmax(x @ Wgate + bgate, axis=-1)
        router_w, sel = jax.lax.top_k(probs, K)
        comb = (jax.nn.one_hot(sel, E, dtype=x.dtype) * router_w[..., None]).sum(axis=1)

        def body(acc, xs):
            Wg_e, bg_e, Wu_e, bu_e, Wd_e, bd_e, w_e = xs
            h = jax.nn.silu(x @ Wg_e + bg_e) * (x @ Wu_e + bu_e)
            acc = acc + w_e[:, None] * (h @ Wd_e + bd_e)
            return (acc, None)
        acc0 = jnp.zeros_like(x)
        acc, _ = jax.lax.scan(body, acc0, (Wg, bg, Wu, bu, Wd, bd, comb.T))
        return acc.reshape(B, S, Hs)
    h = _L0_tok_ref(x, L0_tok_emb_2, L0_tok_emb_3, L0_tok_emb_4, L0_tok_proj_w, L0_tok_proj_b)
    h = h + _L0_attn_ref(_layernorm(h, axis=-1), L0_attn_Wqkv, L0_attn_gamma, L0_attn_beta, L0_attn_Wproj, L0_attn_bproj)
    h = h + _L0_ffn_ref(_layernorm(h, axis=-1), L0_ffn_Wgate, L0_ffn_bgate, L0_ffn_Wg, L0_ffn_bg, L0_ffn_Wu, L0_ffn_bu, L0_ffn_Wd, L0_ffn_bd)
    return h

_drawn_inputs = setup_inputs


def setup_inputs(seed=0):
    import zlib

    import numpy as np

    out = dict(_drawn_inputs(seed))
    spreads = {'L0_attn_gamma': (1.0, 0.2),
     'L0_attn_beta': (0.0, 0.1),
     'L0_attn_bproj': (0.0, 0.291),
     'L0_ffn_bgate': (0.0, 0.8),
     'L0_ffn_bg': (0.0, 0.8),
     'L0_ffn_bu': (0.0, 0.8),
     'L0_ffn_bd': (0.0, 0.8)}
    factors = {'L0_ffn_Wgate': 8.0, 'L0_ffn_Wg': 8.0, 'L0_ffn_Wu': 8.0, 'L0_ffn_Wd': 8.0}
    for name, (base, spread) in spreads.items():
        noise = np.random.default_rng([zlib.crc32(name.encode()), seed]).standard_normal(out[name].shape)
        drawn = base * np.exp(spread * noise) if base else spread * noise
        out[name] = jnp.asarray(drawn.astype(out[name].dtype))
    for name, factor in factors.items():
        out[name] = (out[name] * factor).astype(out[name].dtype)
    return out
```

```python
from contextlib import ExitStack

import concourse.bass as bass
from concourse import mybir

F32 = mybir.dt.float32
BF16 = mybir.dt.bfloat16
I16 = mybir.dt.int16
I32 = mybir.dt.int32
U32 = mybir.dt.uint32
ALU = mybir.AluOpType
ACT = mybir.ActivationFunctionType
AX = mybir.AxisListType.X

P = 128
B, S = 16, 256
NTOK = B * S
TPB = S // P
NT = NTOK // P
C = 128
NG = 3
VOCAB = 64
HASHED = 25000
HALO = 2
EPS = 1e-5
CAP = 4.0
HALF_UP = 2.0 ** -22
NE = 32
TOPK = 2
FF = 256
FC = FF // P
REGION = NTOK + P
ROW = C + 4
NPAIR = TOPK * NTOK
NTILE = 96
NO_PAIR = 1 << 30
ROUNDS = 4
BIG = 8388608.0
FG = 4
NFG = NT // FG


def live(b, n=B):
    return not isinstance(b, int) or 0 <= b < n


def upto(b, n=B):
    return min(b, n) if isinstance(b, int) else b


def after(eng, sem, count):
    if not isinstance(count, int) or count > 0:
        eng.wait_ge(sem, count)


def hold(eng, sem, count):
    if not isinstance(count, int) or count > 0:
        eng.wait_ge(sem, count)
        eng.nop(nofuse=True)


def steps(eng, first, steady, pairs, unroll, last, step):
    for b in range(first, steady):
        step(b, b % unroll)
    with eng.Fori(0, pairs) as i:
        for u in range(unroll):
            step(unroll * i + (steady + u), (steady + u) % unroll)
    for b in range(steady + pairs * unroll, last + 1):
        step(b, b % unroll)


def build(nc, x, emb, proj_w, proj_b, Wqkv, gamma, beta, Wproj, bproj, Wgate, bgate,
          Wg, bg, Wu, bu, Wd, bd, out):
    ctx = ExitStack()
    with ctx:
        def sb(name, shape, dt):
            return ctx.enter_context(nc.sbuf_tensor(name, shape, dt))

        sems = {}

        def sem(name):
            if name not in sems:
                sems[name] = ctx.enter_context(nc.semaphore(name))
            return sems[name]

        regions = nc.dram_tensor("regions", [NE * REGION, ROW], F32, kind="Internal").ap()
        results = nc.dram_tensor("results", [NPAIR, C], F32, kind="Internal").ap()

        ident = sb("ident", [P, P], F32)
        identb = sb("identb", [P, P], BF16)
        before = sb("before", [P, P], F32)
        beforeb = sb("beforeb", [P, P], BF16)
        onesb = sb("onesb", [P, P], BF16)
        onesf = sb("onesf", [P, NE], F32)
        iota_e = sb("iota_e", [P, NE], F32)
        region0 = sb("region0", [P, NE], F32)
        part_i = sb("part_i", [P, 1], I32)
        part_f = sb("part_f", [P, 1], F32)
        par_i = sb("par_i", [P, 2], I32)
        even_odd = sb("even_odd", [P, 2], F32)
        upper = sb("upper", [P, 1], F32)
        o_scale = sb("o_scale", [P, 1], F32)
        eps = sb("eps", [P, 1], F32)
        four = sb("four", [P, 1], F32)
        pair_no = sb("pair_no", [P, TOPK, NT], I32)
        pad_row = sb("pad_row", [P, ROW], F32)
        projb_bc = sb("projb_bc", [P, C], F32)
        bgate_bc = sb("bgate_bc", [P, NE], F32)
        wgate = sb("wgate", [P, NE], F32)
        wqkv = sb("wqkv", [P, 3, C], F32)
        wproj = sb("wproj", [P, C], F32)
        wemb = sb("wemb", [P, NG * C], F32)
        rows7 = sb("rows7", [7, C], F32)
        cols7 = sb("cols7", [P, 7], F32)
        wembT = sb("wembT", [P, NG, C], F32)
        wT = sb("wT", [P, 3 * C], F32)
        wprojT = sb("wprojT", [P, C], F32)
        qkT3 = sb("qkT3", [P, 3, 2 * C], BF16)
        vT3 = sb("vT3", [P, 3, C], BF16)
        prT3 = sb("prT3", [P, 3, C], BF16)
        rest = sb("rest", [P, 2 * C], F32)
        rest2 = sb("rest2", [P, 2 * C], F32)
        col3 = sb("col3", [P, 2, 3], BF16)
        rest_c = sb("rest_c", [P, 2, 2], F32)
        bp3 = sb("bp3", [3, C], BF16)
        bv3 = sb("bv3", [3, C], BF16)

        tok_i = sb("tok_i", [NT, HALO + P + 2], I32)
        tok_f = sb("tok_f", [NT, HALO + P + 2], F32)
        hsh = sb("hsh", [NT, NG, P], F32)
        h_t = sb("h_t", [NT, P], F32)
        h_q = sb("h_q", [NT, P], F32)
        ids = sb("ids", [P, NT, NG], U32)
        id_ring = sb("id_ring", [P, 2, TPB * NG], U32)

        grams_mem = sb("grams_mem", [P, 2 * TPB * NG * C], F32)
        grams = grams_mem[:, :].rearrange("p (v t n c) -> p v t n c", v=2, t=TPB, n=NG)
        gramsT_mem = sb("gramsT_mem", [P, 2 * NG * S], F32)
        gramsT = gramsT_mem[:, :].rearrange("p (v n s) -> p v n s", v=2, n=NG)
        h_all = sb("h_all", [P, NT, C], F32)
        st = sb("st", [P, 2, TPB, 6], F32)
        mv = sb("mv", [P, 2, TPB, 2], F32)
        sd = sb("sd", [P, 2, TPB], F32)
        rstd = sb("rstd", [P, 2, TPB], F32)
        nmr = sb("nmr", [P, 2, TPB], F32)
        xi = sb("xi", [P, 2, TPB, C], I16)
        xs = sb("xs", [P, 2, TPB, C + 1], BF16)
        xsT = sb("xsT", [P, NTOK], BF16)

        gn = sb("gn", [P, C + 1], F32)
        mrow = sb("mrow", [1, C], F32)
        cov = sb("cov", [P, C], F32)
        wtc = sb("wtc", [P, 3 * C], F32)
        muvar = sb("muvar", [P, 2, 3], F32)
        bn_sd = sb("bn_sd", [P, 3], F32)
        bn_r = sb("bn_r", [P, 3], F32)
        bn_a = sb("bn_a", [P, 3], F32)
        bn_ma = sb("bn_ma", [P, 3], F32)
        bn_b = sb("bn_b", [P, 3], F32)
        bn_bh = sb("bn_bh", [P, 3], F32)
        wv = sb("wv", [P, C], F32)

        qi = sb("qi", [P, 2, S], I16)
        ki = sb("ki", [P, 2, S], I16)
        vi = sb("vi", [P, 2, TPB, C], I16)
        qeo = sb("qeo", [P, 2, 2, S], BF16)
        kT = sb("kT", [P, 2, S], BF16)
        veo = sb("veo", [P, 2, 2, TPB, C], BF16)
        att_mem = sb("att_mem", [P, 2 * ROUNDS * 4 * S], BF16)
        att = att_mem[:, :].rearrange("p (v r i a n) -> p v r i a n", v=2, r=ROUNDS, i=2, a=2)
        o_bias = sb("o_bias", [P, 2], F32)
        oi = sb("oi", [P, 2, S], I16)
        oT = sb("oT", [P, 2, S], BF16)
        row = sb("row", [P, 2, TOPK, TPB, ROW], F32)
        x2T = sb("x2T", [P, S], F32)
        lg = sb("lg", [P, TPB, NE + 8], F32)
        lg_all = sb("lg_all", [P, NT, NE + 8], F32)
        topi = sb("topi", [P, TPB, 8], U32)
        topf = sb("topf", [P, TPB, TOPK], F32)
        chosen = sb("chosen", [P, 2, TPB, TOPK, NE], F32)
        picks = sb("picks", [P, 2, TPB, NE], BF16)
        seen = sb("seen", [P, 2, TPB, NE], BF16)
        place = sb("place", [P, TPB, NE], F32)
        placed = sb("placed", [P, TPB, TOPK, NE], F32)
        slot = sb("slot", [P, 2, TPB * TOPK], U32)

        wgu = sb("wgu", [P, NE, 2 * FF], F32)
        wd = sb("wd", [P, NE, FC, C], F32)
        bias_f = sb("bias_f", [NE, 2 * FF + C], F32)
        bias3 = sb("bias3", [3 * NE, 2 * FF + C], BF16)
        sel3 = sb("sel3", [3 * NE, NE], BF16)
        total = sb("total", [P, NE], BF16)
        count = sb("count", [P, NE], F32)
        ntile_i = sb("ntile_i", [P, NE], I16)
        ntile = sb("ntile", [P, NE], F32)
        upto_t = sb("upto_t", [P, NE], F32)
        prev_t = sb("prev_t", [P, NE], F32)
        origin = sb("origin", [P, NE], F32)
        passed = sb("passed", [P, NE], F32)
        owner = sb("owner", [P, NE], F32)
        mapc = sb("mapc", [P, 2], F32)
        mapf = sb("mapf", [P, 2], F32)
        tmap = sb("tmap", [1, 2 * P], I32)
        den = sb("den", [P, NT], F32)
        e2 = sb("e2", [P, NT], F32)
        w12 = sb("w12", [P, TOPK, NT], F32)
        XR = 4
        pair_i = sb("pair_i", [P, XR, 1], U32)
        xg = grams_mem[:, 0:XR * ROW].rearrange("p (r c) -> p r c", r=XR)
        yy = grams_mem[:, XR * ROW:XR * (ROW + C)].rearrange("p (r c) -> p r c", r=XR)
        xgT = grams_mem[:, XR * (ROW + C):XR * (ROW + C) + 2 * P].rearrange("p (r c) -> p r c", r=2)
        sg, hh, hhT = [gramsT_mem[:, i * 2 * FF:(i + 1) * 2 * FF] for i in range(3)]
        sg = sg.rearrange("p (r n) -> p r n", r=2)
        hh = hh.rearrange("p (r n) -> p r n", r=2)
        hhT = hhT.rearrange("p (r c n) -> p r c n", r=2, c=FC)
        late = att_mem[:, :].bitcast(F32)
        y_fin = late[:, 0:2 * TOPK * FG * C].rearrange("p (g k t c) -> p g k t c", g=2, k=TOPK, t=FG)
        e_all = late[:, 2 * TOPK * FG * C:2 * TOPK * FG * C + NT * NE].rearrange("p (t e) -> p t e", e=NE)
        spare = 2 * TOPK * FG * C + NT * NE
        bias_r = late[0:NE, spare:spare + 2 * FF + C]
        spare = 2 * (spare + 2 * FF + C)
        bias_m = att_mem[0:NE, spare:spare + 2 * FF + C]

        bank = [ctx.enter_context(nc.psum_tensor(f"bank{i}", [P, 512], F32)) for i in range(8)]

        block = ctx.enter_context(nc.Block())

        @block.sync
        def _(sp):
            xr = x.rearrange("b (t p) -> (b t) p", p=P)
            sp.wait_ge(sem("tok_clear"), 1)
            sp.dma_start(tok_i[:, HALO:HALO + P], xr).then_inc(sem("tok_in"), 16)
            sp.dma_start(tok_i[1:NT, 0:HALO], xr[0:NT - 1, P - HALO:P]).then_inc(sem("tok_in"), 16)
            sp.dma_start(tok_i[0:NT - 1, HALO + P:], xr[1:NT, 0:2]).then_inc(sem("tok_in"), 16)
            sp.dma_start(wemb[:, :], proj_w).then_inc(sem("wemb_in"), 16)
            sp.dma_start(projb_bc[:, :], proj_b.rearrange("(a n) -> a n", a=1).to_broadcast([P, C]))\
                .then_inc(sem("projb_in"), 16)
            sp.dma_start(wqkv[:, :, :], Wqkv.rearrange("(g p) c -> p g c", p=P)).then_inc(sem("wattn_in"), 16)
            sp.dma_start(wproj[:, :], Wproj).then_inc(sem("wattn_in"), 16)
            sp.dma_start(rows7[0:3, :], gamma.rearrange("(g p) -> g p", p=P)).then_inc(sem("wattn_in"), 16)
            sp.dma_start(rows7[3:6, :], beta.rearrange("(g p) -> g p", p=P)).then_inc(sem("wattn_in"), 16)
            sp.dma_start(rows7[6:7, :], bproj.rearrange("(a p) -> a p", a=1)).then_inc(sem("wattn_in"), 16)
            sp.dma_start(wgate[:, :], Wgate).then_inc(sem("wgate_in"), 16)
            sp.dma_start(bgate_bc[:, :], bgate.rearrange("(a n) -> a n", a=1).to_broadcast([P, NE]))\
                .then_inc(sem("wgate_in"), 16)
            sp.dma_start(bias_f[:, 0:FF], bg).then_inc(sem("bias_in"), 16)
            sp.dma_start(bias_f[:, FF:2 * FF], bu).then_inc(sem("bias_in"), 16)
            sp.dma_start(bias_f[:, 2 * FF:], bd).then_inc(sem("bias_in"), 16)
            sp.wait_ge(sem("pad_made"), 1)
            sp.dma_start(regions.rearrange("(e r) c -> r e c", e=NE)[0:P],
                         pad_row[:, :].rearrange("p (a c) -> p a c", a=1).to_broadcast([P, NE, ROW]))\
                .then_inc(sem("pads_in"), 16)
            for e in range(0, NE, 4):
                sp.dma_start(wgu[:, e:e + 4, 0:FF], Wg[e:e + 4].rearrange("e h i -> h e i")).then_inc(sem("experts_in"), 16)
                sp.dma_start(wgu[:, e:e + 4, FF:], Wu[e:e + 4].rearrange("e h i -> h e i")).then_inc(sem("experts_in"), 16)
                sp.dma_start(wd[:, e:e + 4], Wd[e:e + 4].rearrange("e (c p) h -> p e c h", p=P)).then_inc(sem("experts_in"), 16)

            sp.wait_ge(sem("map_made"), 1)
            for u in range(2):
                sp.wait_ge(sem(f"rows_sent{u}"), 16 * TPB * TOPK * B // 2)

            def load_tile(j, u):
                start = sp.value_load(tmap[0:1, bass.ds(P + j, 1)], min_val=0, max_val=NE * REGION - P)
                after(sp, sem("x_turned"), j - XR + 1)
                after(sp, sem("pair_kept"), j - XR + 1)
                sp.dma_start(xg[:, u, :], regions[bass.ds(start, P), :]).then_inc(sem(f"x_in{u}"), 16)

            steps(sp, 0, 4, 23, XR, NTILE - 1, load_tile)

            for u in range(XR):
                sp.wait_ge(sem(f"y_sent{u}"), 16 * NTILE // XR)
            res = results.rearrange("(k t p) c -> k p t c", k=TOPK, p=P)
            for g in range(NFG):
                if g >= 2:
                    sp.wait_ge(sem("fin_used"), g - 1)
                for k in range(TOPK):
                    sp.dma_start(y_fin[:, g % 2, k], res[k][:, g * FG:(g + 1) * FG, :]).then_inc(sem(f"fin_in{g % 2}"), 16)

        @block.gpsimd
        def _(pool):
            pool.memset(tok_i[:, :], 0).then_inc(sem("tok_clear"), 1)
            pool.memset(ident[:, :], 0.0).then_inc(sem("pool_c"), 1)
            pool.memset(before[:, :], 0.0).then_inc(sem("pool_c"), 1)
            pool.memset(pad_row[:, :], 0.0).then_inc(sem("pool_c"), 1)
            pool.wait_ge(sem("pool_c"), 3)
            pool.affine_select(out=ident[:, :], in_=ident[:, :], compare_op=ALU.not_equal, fill=1.0,
                               base=0, pattern=[[-1, P]], channel_multiplier=1).then_inc(sem("ident_made"), 1)
            pool.affine_select(out=before[:, :], in_=before[:, :], compare_op=ALU.is_ge, fill=1.0,
                               base=0, pattern=[[-1, P]], channel_multiplier=1).then_inc(sem("before_made"), 1)
            pool.memset(pad_row[:, C:C + 1].bitcast(I32), NO_PAIR).then_inc(sem("pad_made"), 1)
            pool.iota(part_i[:, :], pattern=[[0, 1]], base=0, channel_multiplier=1).then_inc(sem("iotas"), 1)
            pool.iota(pair_no[:, :, :], pattern=[[NTOK, TOPK], [P, NT]], base=0, channel_multiplier=1)\
                .then_inc(sem("iotas"), 1)
            pool.iota(iota_e[:, :], pattern=[[1, NE]], base=0, channel_multiplier=0,
                      allow_small_or_imprecise_dtypes=True).then_inc(sem("iotas"), 1)
            pool.iota(region0[:, :], pattern=[[REGION, NE]], base=P, channel_multiplier=0,
                      allow_small_or_imprecise_dtypes=True).then_inc(sem("iotas"), 1)

            pool.wait_ge(sem("ids_made"), 1)

            def gather(b, u):
                hold(pool, sem(f"grams_in{u}"), 16 * TPB * NG * ((b - u) // 2) if isinstance(b, int)
                      else 8 * TPB * NG * (b - u))
                pool.tensor_copy(id_ring[:, u, :].rearrange("p (t n) -> p t n", n=NG),
                                 ids[:, bass.ds(b * TPB, TPB), :]).then_inc(sem("ids_staged"), 1)
                hold(pool, sem("ids_staged"), b + 1)
                hold(pool, sem("grams_used"), b - 1)
                for t in range(TPB):
                    for n in range(NG):
                        k = t * NG + n
                        pool.indirect_dma_start(grams[:, u, t, n, :], None, emb[n],
                                                bass.IndirectOffsetOnAxis(ap=id_ring[:, u, k:k + 1], axis=0))\
                            .then_inc(sem(f"grams_in{u}"), 16)

            steps(pool, 0, 2, 7, 2, B - 1, gather)

            pool.wait_ge(sem("pads_in"), 16)

            def dispatch(s, u):
                b, v = s - 3, (u + 1) % 2
                if live(b):
                    hold(pool, sem("slot_made"), b + 1)
                    hold(pool, sem("row_copied"), b + 1)
                    for t in range(TPB):
                        for k in range(TOPK):
                            i = t * TOPK + k
                            pool.indirect_dma_start(
                                regions, bass.IndirectOffsetOnAxis(ap=slot[:, v, i:i + 1], axis=0),
                                row[:, v, k, t, :], None).then_inc(sem(f"rows_sent{v}"), 16)
                b, v = s - 2, u
                if live(b):
                    hold(pool, sem(f"rows_sent{v}"), 16 * TPB * TOPK * ((b - v) // 2) if isinstance(b, int)
                          else 8 * TPB * TOPK * (b - v))
                    for k in range(TOPK):
                        pool.tensor_copy(row[:, v, k, :, C:C + 1].bitcast(I32),
                                         pair_no[:, k, bass.ds(b * TPB, TPB)].rearrange("p (t a) -> p t a", a=1))
                    hold(pool, sem("row_made"), b + 1)
                    pool.tensor_copy(row[:, v, 1, :, 0:C], row[:, v, 0, :, 0:C]).then_inc(sem("row_copied"), 1)

            steps(pool, 2, 5, 5, 2, B + 2, dispatch)

            def collect(j, u):
                hold(pool, sem("y_made"), j + 1)
                pool.indirect_dma_start(
                    results, bass.IndirectOffsetOnAxis(ap=pair_i[:, u, :], axis=0), yy[:, u, :], None,
                    bounds_check=NPAIR - 1, oob_is_err=False).then_inc(sem(f"y_sent{u}"), 16)

            steps(pool, 0, 4, 23, XR, NTILE - 1, collect)

        @block.tensor
        def _(pe):
            pe.wait_ge(sem("ident_made"), 1)
            pe.wait_ge(sem("hashed"), 1)
            for n in range(NG):
                last = pe.transpose(bank[0][:, n * NT:(n + 1) * NT], hsh[:, n, :], ident[0:NT, 0:NT])
            last.then_inc(sem("ids_turned"), 1)
            pe.wait_ge(sem("wemb_in"), 16)
            for n in range(NG):
                last = pe.transpose(bank[1][:, n * C:(n + 1) * C], wemb[:, n * C:(n + 1) * C], ident[:, :])
            last.then_inc(sem("wemb_turned"), 1)
            pe.wait_ge(sem("wattn_in"), 80)
            for g in range(3):
                pe.transpose(bank[2][:, g * C:(g + 1) * C], wqkv[:, g, :], ident[:, :])
            pe.transpose(bank[3][:, 0:C], wproj[:, :], ident[:, :])
            pe.transpose(bank[3][:, C:C + 7], rows7[:, :], ident[0:7, 0:7]).then_inc(sem("wattn_turned"), 1)
            pe.wait_ge(sem("identb_made"), 1)
            pe.wait_ge(sem("bp_split"), 1)
            pe.transpose(bank[4][0:3, 0:C // 2].bitcast(BF16), col3[:, 0, :], identb[:, :]).then_inc(sem("bp_turned"), 1)
            pe.wait_ge(sem("setup_done"), 1)

            def embed(s, u):
                b, v = s, u
                if live(b):
                    pe.wait_ge(sem(f"grams_in{v}"), 8 * TPB * NG * (b - v) + 16 * TPB * NG)
                    after(pe, sem("gramsT_a"), b - 1)
                    after(pe, sem("gramsT_b"), b - 1)
                    for n in range(NG):
                        for t in range(TPB):
                            dst = bank[2 * v + n // 2][:, (n % 2) * S + t * P:(n % 2) * S + (t + 1) * P]
                            last = pe.transpose(dst, grams[:, v, t, n, :], ident[:, :])
                    last.then_inc(sem("grams_used"), 1)
                b, v = s - 1, 1 - u
                if live(b):
                    pe.wait_ge(sem("gramsT_a"), b + 1)
                    pe.wait_ge(sem("gramsT_b"), b + 1)
                    after(pe, sem("h_made"), b - 1)
                    for t in range(TPB):
                        for n in range(NG):
                            last = pe.matmul(bank[4 + v][:, t * C:(t + 1) * C], gramsT[:, v, n, t * P:(t + 1) * P],
                                             wembT[:, n, :], start=(n == 0), stop=(n == NG - 1))
                    last.then_inc(sem("projected"), 1)
                b, v = s - 2, u
                if live(b):
                    pe.wait_ge(sem("xs_made"), b + 1)
                    after(pe, sem("xsT_made"), b)
                    for t in range(TPB):
                        pe.transpose(bank[6][:, t * C // 2:(t + 1) * C // 2].bitcast(BF16), xs[:, v, t, 0:C], identb[:, :])
                    for t in range(TPB):
                        last = pe.matmul(bank[7][:, 0:C + 1], xs[:, v, t, 0:C], xs[:, v, t, :],
                                         start=(isinstance(b, int) and b == 0 and t == 0),
                                         stop=(isinstance(b, int) and b == B - 1 and t == TPB - 1))
                    last.then_inc(sem("xs_turned"), 1)

            steps(pe, 0, 4, 6, 2, B + 1, embed)

            pe.wait_ge(sem("mean_made"), 1)
            pe.transpose(bank[0][0:1, 0:P], gn[:, C:C + 1], ident[:, :]).then_inc(sem("mean_turned"), 1)
            pe.wait_ge(sem("mrow_made"), 1)
            pe.matmul(bank[1][:, 0:C], mrow[:, :], mrow[:, :], start=True, stop=True).then_inc(sem("mm_made"), 1)
            for g in range(3):
                last = pe.matmul(bank[3][:, g:g + 1], wT[:, g * C:(g + 1) * C], gn[:, C:C + 1], start=True, stop=True)
            pe.wait_ge(sem("cov_made"), 1)
            pe.matmul(bank[2][:, 0:3 * C], cov[:, :], wT[:, :], start=True, stop=True).then_inc(sem("covw"), 1)
            pe.wait_ge(sem("wtc_made"), 1)
            for g in range(3):
                last = pe.matmul(bank[3][:, 3 + g:4 + g], wtc[:, g * C:(g + 1) * C], onesf[:, 0:1], start=True, stop=True)
            last.then_inc(sem("muvar_made"), 1)
            pe.wait_ge(sem("wv_made"), 1)
            pe.transpose(bank[0][:, 0:C], wv[:, :], ident[:, :])
            pe.transpose(bank[1][0:3, 0:C // 2].bitcast(BF16), col3[:, 1, :], identb[:, :]).then_inc(sem("wv_turned"), 1)

            pe.wait_ge(sem("vT_made"), 1)

            def scores(b, v, r):
                c, half = r // 2, r % 2
                if r == 0:
                    pe.wait_ge(sem("qk_made"), b + 1)
                after(pe, sem(f"att_made{half}"), 2 * b + c)
                for par in range(2):
                    for i in range(2):
                        g = 32 * (2 * half + i)
                        last = pe.matmul(bank[2 * half + i][:, par * S:(par + 1) * S],
                                         kT[g:g + 32, v, c * P:(c + 1) * P], qeo[g:g + 32, v, par, :],
                                         start=True, stop=True)
                last.then_inc(sem(f"scored{half}"), 1)

            def attend(s, u):
                b, v = s - 1, 1 - u
                if live(b):
                    pe.wait_ge(sem("att_made0"), 2 * b + 2)
                    pe.wait_ge(sem("att_made1"), 2 * b + 2)
                    pe.wait_ge(sem("v_made"), b + 1)
                    after(pe, sem("o_read"), b)
                    for i, (par, c) in enumerate([(0, 0), (0, 1), (1, 0), (1, 1)]):
                        pe.matmul(bank[6][:, S:S + 1], veo[:, v, par, c, :], onesb[:, 0:1], start=(i == 0), stop=(i == 3))
                    for i, (par, c) in enumerate([(0, 0), (0, 1), (1, 0), (1, 1)]):
                        for g in range(4):
                            last = pe.matmul(bank[6][32 * g:32 * g + 32, 0:S], veo[:, v, par, c, 32 * g:32 * g + 32],
                                             att[:, v, 2 * c + g // 2, g % 2, par, :],
                                             start=(i == 0), stop=(i == 3))
                    last.then_inc(sem("attended"), 1)
                b = s + 1
                if live(b):
                    after(pe, sem("qk_read"), b)
                    after(pe, sem("slot_read"), b - 4)
                    for g in range(2):
                        for part in range(3):
                            last = pe.matmul(bank[4][:, g * S:(g + 1) * S], qkT3[:, part, g * C:(g + 1) * C],
                                             xsT[:, bass.ds(b * S, S)], start=(part == 0), stop=(part == 2))
                    last.then_inc(sem("qk_out"), 1)
                if live(s):
                    scores(s, u, 0)
                b, v = s - 3, 1 - u
                if live(b):
                    pe.wait_ge(sem("row_made"), b + 1)
                    after(pe, sem("logits_made"), b)
                    for t in range(TPB):
                        last = pe.transpose(bank[7][:, t * P:(t + 1) * P], row[:, v, 0, t, 0:C], ident[:, :])
                    last.then_inc(sem("x2_turned"), 1)
                b = s + 1
                if live(b):
                    after(pe, sem("v_read"), b)
                    after(pe, sem("h2_made"), b - 2)
                    for t in range(TPB):
                        for part in range(3):
                            pe.matmul(bank[5][:, t * C:(t + 1) * C], xsT[:, bass.ds(b * S + t * P, P)],
                                      vT3[:, part, :], start=(part == 0), stop=False)
                        last = pe.matmul(bank[5][:, t * C:(t + 1) * C], onesb[0:3, :], bv3[:, :], start=False, stop=True)
                    last.then_inc(sem("v_out"), 1)
                if live(s):
                    scores(s, u, 1)
                b, v = s - 1, 1 - u
                if live(b):
                    pe.wait_ge(sem("oT_made"), b + 1)
                    pe.wait_ge(sem("v_read"), upto(b + 3))
                    for t in range(TPB):
                        for part in range(3):
                            pe.matmul(bank[5][:, t * C:(t + 1) * C], oT[:, v, t * P:(t + 1) * P], prT3[:, part, :],
                                      start=(part == 0), stop=False)
                        last = pe.matmul(bank[5][:, t * C:(t + 1) * C], onesb[0:3, :], bp3[:, :], start=False, stop=True)
                    last.then_inc(sem("proj_out"), 1)
                if live(s):
                    scores(s, u, 2)
                b = s - 3
                if live(b):
                    pe.wait_ge(sem("x2T_made"), b + 1)
                    for t in range(TPB):
                        last = pe.matmul(bank[7][:, S + t * NE:S + (t + 1) * NE], x2T[:, t * P:(t + 1) * P], wgate[:, :],
                                         start=True, stop=True)
                    last.then_inc(sem("routed"), 1)
                if live(s):
                    scores(s, u, 3)
                b, v = s - 3, 1 - u
                if live(b):
                    pe.wait_ge(sem("picks_made"), b + 1)
                    pe.wait_ge(sem("qk_read"), upto(b + 5))
                    pe.matmul(bank[4][:, 0:TPB * NE], beforeb[:, :], picks[:, v].rearrange("p t e -> p (t e)"),
                              start=True, stop=False)
                    pe.matmul(bank[4][:, 0:TPB * NE], onesb[:, :], seen[:, v].rearrange("p t e -> p (t e)"),
                              start=False, stop=True).then_inc(sem("ranked"), 1)

            steps(pe, -1, 3, 6, 2, B + 2, attend)

            pe.wait_ge(sem("total_made"), 1)
            pe.matmul(bank[0][:, 0:NE], onesb[:, :], total[:, :], start=True, stop=True).then_inc(sem("counted"), 1)
            pe.wait_ge(sem("map_cols"), 1)
            for i in range(2):
                last = pe.matmul(bank[1][0:1, i * P:(i + 1) * P], mapf[:, i:i + 1], ident[:, :], start=True, stop=True)
            last.then_inc(sem("map_turned"), 1)

            pe.wait_ge(sem("map_made"), 1)
            pe.wait_ge(sem("bias3_made"), 1)
            pe.wait_ge(sem("experts_in"), 16 * 3 * NE // 4)
            pe.wait_ge(sem("slot_read"), B)

            def expert_tile(j, u):
                if live(j, NTILE):
                    e = pe.value_load(tmap[0:1, bass.ds(j, 1)], min_val=0, max_val=NE - 1)
                    pe.wait_ge(sem("xgT_made"), j + 1)
                    after(pe, sem("hh_made"), j - 1)
                    gu = bank[u % 2]
                    pe.matmul(gu[:, 0:2 * FF], sel3[:, bass.ds(e, 1)].to_broadcast([3 * NE, P]),
                              bias3[:, 0:2 * FF], start=True, stop=False)
                    pe.matmul(gu[:, 0:2 * FF], xgT[:, u % 2, :],
                              wgu[:, bass.ds(e, 1), :].rearrange("p a n -> p (a n)"), start=False, stop=True)\
                        .then_inc(sem("gu_out"), 1)
                i = j - 2
                if live(i, NTILE):
                    w = u % 2
                    e2_ = pe.value_load(tmap[0:1, bass.ds(i, 1)], min_val=0, max_val=NE - 1)
                    pe.wait_ge(sem("hhT_made"), i + 1)
                    after(pe, sem("y_made"), i - 1)
                    yb = bank[6 + w]
                    pe.matmul(yb[:, 0:C], sel3[:, bass.ds(e2_, 1)].to_broadcast([3 * NE, P]),
                              bias3[:, 2 * FF:], start=True, stop=False)
                    for c in range(FC):
                        last = pe.matmul(yb[:, 0:C], hhT[:, w, c, :],
                                         wd[:, bass.ds(e2_, 1), c, :].rearrange("p a n -> p (a n)"),
                                         start=False, stop=(c == FC - 1))
                    last.then_inc(sem("y_out"), 1)
                i = j - 1
                if live(i, NTILE):
                    w = (u - 1) % 2
                    pe.wait_ge(sem("hh_made"), i + 1)
                    after(pe, sem("hhT_made"), i - 1)
                    for c in range(FC):
                        last = pe.transpose(bank[4 + w][:, c * P:(c + 1) * P], hh[:, w, c * P:(c + 1) * P], ident[:, :])
                    last.then_inc(sem("hh_turned"), 1)
                i = j + 1
                if live(i, NTILE):
                    w = (u + 1) % 4
                    pe.wait_ge(sem(f"x_in{w}"), 16 * (i // XR + 1) if isinstance(i, int) else 4 * (i - w) + 16)
                    after(pe, sem("xgT_made"), i - 1)
                    pe.transpose(bank[2 + w % 2][:, 0:P], xg[:, w, 0:C], ident[:, :]).then_inc(sem("x_turned"), 1)

            steps(pe, -1, 3, 23, XR, NTILE + 1, expert_tile)

        @block.scalar
        def _(act):
            act.wait_ge(sem("cols_made"), 1)

            def embed(s, u):
                b, v = s, u
                if live(b):
                    act.wait_ge(sem("grams_used"), b + 1)
                    after(act, sem("projected"), b - 1)
                    act.activation(gramsT[:, v, 2, 2:S - 1], bank[2 * v + 1][:, 2:S - 1], ACT.Copy)\
                        .then_inc(sem("gramsT_b"), 1)
                b, v = s - 1, 1 - u
                if live(b):
                    act.wait_ge(sem("stats_made"), b + 1)
                    act.activation(sd[:, v, :], mv[:, v, :, 1], ACT.Sqrt, bias=eps[:, :]).then_inc(sem("sd_made"), 1)
                    act.wait_ge(sem("nmr_made"), b + 1)
                    after(act, sem("xs_made"), b - 1)
                    for t in range(TPB):
                        last = act.activation(xi[:, v, t, :],
                                              h_all[:, bass.ds(b * TPB + t, 1), :].rearrange("p a c -> p (a c)"),
                                              ACT.Relu, scale=rstd[:, v, t:t + 1], bias=nmr[:, v, t:t + 1])
                    last.then_inc(sem("xi_made"), 1)
                b = s - 2
                if live(b):
                    act.wait_ge(sem("xs_turned"), b + 1)
                    act.activation(xsT[:, bass.ds(b * S, S)], bank[6][:, 0:S // 2].bitcast(BF16), ACT.Copy)\
                        .then_inc(sem("xsT_made"), 1)

            steps(act, 0, 4, 6, 2, B + 1, embed)

            act.wait_ge(sem("bn_var"), 1)
            act.activation(bn_sd[:, :], muvar[:, 1, :], ACT.Sqrt, bias=eps[:, :]).then_inc(sem("bn_sd"), 1)
            act.wait_ge(sem("bn_made"), 1)

            def att_odd(b, v, c):
                act.wait_ge(sem("scored1"), 2 * b + c + 1)
                if c == 0:
                    after(act, sem("attended"), b - 1)
                for i in range(2):
                    last = act.activation(att[:, v, 2 * c + 1, i].rearrange("p a n -> p (a n)"), bank[2 + i][:, :],
                                          ACT.Relu, scale=-1.0, bias=four[:, :])
                last.then_inc(sem("att_made1"), 1)

            def attend(s, u):
                b, v = s - 1, 1 - u
                if live(b):
                    act.wait_ge(sem("o_bias_made"), b + 1)
                    after(act, sem("oT_made"), b - 1)
                    act.activation(oi[:, v, :], bank[6][:, 0:S], ACT.Identity, scale=o_scale[:, :], bias=o_bias[:, v:v + 1])\
                        .then_inc(sem("o_read"), 1)
                b, v = s + 1, 1 - u
                if live(b):
                    act.wait_ge(sem("qk_out"), b + 1)
                    after(act, sem("qk_made"), b - 1)
                    act.activation(qi[:, v, :], bank[4][:, 0:S], ACT.Relu, scale=bn_a[:, 0:1], bias=bn_bh[:, 0:1])
                    act.activation(ki[:, v, :], bank[4][:, S:2 * S], ACT.Relu, scale=bn_a[:, 1:2], bias=bn_bh[:, 1:2])\
                        .then_inc(sem("qk_read"), 1)
                b = s - 3
                if live(b):
                    act.wait_ge(sem("x2_turned"), b + 1)
                    after(act, sem("routed"), b)
                    act.activation(x2T[:, :], bank[7][:, 0:S], ACT.Copy).then_inc(sem("x2T_made"), 1)
                b, v = s + 1, 1 - u
                if live(b):
                    act.wait_ge(sem("v_out"), b + 1)
                    after(act, sem("v_made"), b - 1)
                    act.activation(vi[:, v].rearrange("p t c -> p (t c)"), bank[5][:, 0:S], ACT.Relu).then_inc(sem("v_read"), 1)
                if live(s):
                    att_odd(s, u, 0)
                b, v = s - 2, u
                if live(b):
                    act.wait_ge(sem("nmr2_made"), b + 1)
                    after(act, sem(f"rows_sent{v}"), 16 * TPB * TOPK * ((b - v) // 2) if isinstance(b, int)
                          else 8 * TPB * TOPK * (b - v))
                    for t in range(TPB):
                        last = act.activation(row[:, v, 0, t, 0:C],
                                              h_all[:, bass.ds(b * TPB + t, 1), :].rearrange("p a c -> p (a c)"),
                                              ACT.Identity, scale=rstd[:, v, t:t + 1], bias=nmr[:, v, t:t + 1])
                    last.then_inc(sem("row_made"), 1)
                if live(s):
                    att_odd(s, u, 1)
                b, v = s - 1, 1 - u
                if live(b):
                    act.wait_ge(sem("stats2_made"), b + 1)
                    act.activation(sd[:, v, :], mv[:, v, :, 1], ACT.Sqrt, bias=eps[:, :]).then_inc(sem("sd2_made"), 1)

            steps(act, -1, 3, 6, 2, B + 2, attend)

            act.wait_ge(sem("shifted"), 1)
            act.activation(e_all[:, :, :], e_all[:, :, :], ACT.Exp)
            act.activation(e2[:, :], e2[:, :], ACT.Exp).then_inc(sem("exps_made"), 1)

            def expert_tile(j, u):
                if live(j, NTILE):
                    act.wait_ge(sem("gu_out"), j + 1)
                    after(act, sem("hh_made"), j - 1)
                    act.activation(sg[:, u % 2, :], bank[u % 2][:, 0:FF], ACT.Silu).then_inc(sem("silu_made"), 1)
                i, w = j - 1, (u - 1) % 2
                if live(i, NTILE):
                    act.wait_ge(sem("hh_turned"), i + 1)
                    after(act, sem("y_out"), i - 1)
                    act.activation(hhT[:, w].rearrange("p c n -> p (c n)"), bank[4 + w][:, 0:FF], ACT.Copy)\
                        .then_inc(sem("hhT_made"), 1)

            steps(act, 0, 4, 23, XR, NTILE, expert_tile)

            o = out.rearrange("b (t p) c -> p (b t) c", p=P)
            for g in range(NFG):
                act.wait_ge(sem("fin_made"), g + 1)
                act.dma_start(o[:, g * FG:(g + 1) * FG, :], h_all[:, g * FG:(g + 1) * FG, :]).then_inc(sem("out_written"), 16)
            act.wait_ge(sem("out_written"), 16 * NFG)

        @block.vector
        def _(dve):
            chained = [0]

            def chain(ins):
                chained[0] += 1
                ins.then_inc(sem("dve_chain"), 1)
                dve.wait_ge(sem("dve_chain"), chained[0])

            dve.memset(onesb[:, :], 1.0)
            dve.memset(onesf[:, :], 1.0)
            dve.memset(eps[:, :], EPS)
            dve.memset(four[:, :], CAP)
            dve.memset(gramsT[:, :, :, :], 0.0)
            dve.memset(xs[:, :, :, :], 1.0)
            dve.memset(veo[:, :, :, :, :], 0.0)
            dve.memset(row[:, :, :, :, :], 0.0)
            dve.memset(seen[:, :, :, :], 0.0)
            chain(dve.memset(picks[:, :, :, :], 0.0))
            dve.wait_ge(sem("tok_in"), 48)
            chain(dve.tensor_copy(tok_f[:, :], tok_i[:, :]))

            def at(j):
                return tok_f[:, HALO + j:HALO + j + P]

            def modulo(dst, t):
                chain(dve.tensor_scalar(h_q[:, :], t, 1.0 / HASHED, BIG, ALU.mult, ALU.add))
                chain(dve.tensor_scalar(h_q[:, :], h_q[:, :], -BIG, -float(HASHED), ALU.add, ALU.mult))
                chain(dve.tensor_tensor(dst, t, h_q[:, :], ALU.add))
                chain(dve.tensor_scalar(h_q[:, :], dst, 0.0, float(HASHED), ALU.is_lt, ALU.mult))
                chain(dve.tensor_tensor(dst, dst, h_q[:, :], ALU.add))

            def push(dst, h, token):
                chain(dve.scalar_tensor_tensor(out=h_t[:, :], in0=h, scalar=float(VOCAB), in1=token, op0=ALU.mult, op1=ALU.add))
                modulo(dst, h_t[:, :])

            push(hsh[:, 0, :], at(-1), at(0))
            push(hsh[:, 1, :], hsh[:, 0, :], at(1))
            push(hsh[:, 2, :], at(-2), at(-1))
            push(hsh[:, 2, :], hsh[:, 2, :], at(0))
            push(hsh[:, 2, :], hsh[:, 2, :], at(1))
            dve.sem_inc(sem("hashed"), 1)
            dve.wait_ge(sem("ids_turned"), 1)
            dve.tensor_copy(ids[:, :, :].rearrange("p t n -> p n t"),
                            bank[0][:, 0:NG * NT].rearrange("p (n t) -> p n t", n=NG)).then_inc(sem("ids_made"), 1)

            dve.wait_ge(sem("ident_made"), 1)
            dve.tensor_copy(identb[:, :], ident[:, :]).then_inc(sem("identb_made"), 1)
            dve.wait_ge(sem("before_made"), 1)
            dve.tensor_copy(beforeb[:, :], before[:, :])
            dve.wait_ge(sem("iotas"), 4)
            chain(dve.tensor_copy(part_f[:, :], part_i[:, :]))
            chain(dve.tensor_scalar(par_i[:, 0:1], part_i[:, :], 16, None, ALU.bitwise_and))
            dve.tensor_scalar(even_odd[:, 0:1], par_i[:, 0:1], 0.0, None, ALU.is_equal)
            dve.tensor_scalar(even_odd[:, 1:2], par_i[:, 0:1], 0.0, None, ALU.is_gt)
            chain(dve.tensor_scalar(upper[:, :], part_f[:, :], float(P // 2), None, ALU.is_ge))
            chain(dve.tensor_scalar(o_scale[:, :], upper[:, :], -0.5, 0.25, ALU.mult, ALU.add))

            def split(part0, part1, part2, w, r1, r2):
                chain(dve.tensor_copy(part0, w))
                chain(dve.tensor_tensor(r1, w, part0, ALU.subtract))
                chain(dve.tensor_copy(part1, r1))
                chain(dve.tensor_tensor(r2, r1, part1, ALU.subtract))
                chain(dve.tensor_copy(part2, r2))

            dve.wait_ge(sem("wemb_turned"), 1)
            dve.tensor_copy(wembT[:, :, :].rearrange("p n c -> p (n c)"), bank[1][:, 0:NG * C])
            dve.wait_ge(sem("wattn_turned"), 1)
            dve.tensor_copy(wT[:, :], bank[2][:, 0:3 * C])
            dve.tensor_copy(wprojT[:, :], bank[3][:, 0:C])
            chain(dve.tensor_copy(cols7[:, :], bank[3][:, C:C + 7]))
            split(qkT3[:, 0, :], qkT3[:, 1, :], qkT3[:, 2, :], wT[:, 0:2 * C], rest[:, :], rest2[:, :])
            split(prT3[:, 0, :], prT3[:, 1, :], prT3[:, 2, :], wprojT[:, :], rest[:, 0:C], rest2[:, 0:C])
            split(col3[:, 0, 0:1], col3[:, 0, 1:2], col3[:, 0, 2:3], cols7[:, 6:7], rest_c[:, 0, 0:1], rest_c[:, 0, 1:2])
            dve.sem_inc(sem("bp_split"), 1)
            dve.wait_ge(sem("bp_turned"), 1)
            chain(dve.tensor_copy(bp3[:, :], bank[4][0:3, 0:C // 2].bitcast(BF16)))
            dve.sem_inc(sem("setup_done"), 1)
            dve.sem_inc(sem("cols_made"), 1)
            dve.wait_ge(sem("projb_in"), 16)

            def embed(s, u):
                b, v = s - 2, u
                if live(b):
                    dve.wait_ge(sem("xi_made"), b + 1)
                    after(dve, sem("xs_turned"), b - 1)
                    dve.tensor_scalar(xs[:, v, :, 0:C], xi[:, v], CAP, None, ALU.min).then_inc(sem("xs_made"), 1)
                b, v = s, u
                if live(b):
                    dve.wait_ge(sem("grams_used"), b + 1)
                    after(dve, sem("projected"), b - 1)
                    dve.tensor_copy(gramsT[:, v, 0, 1:S], bank[2 * v][:, 1:S])
                    dve.tensor_copy(gramsT[:, v, 1, 1:S - 1], bank[2 * v][:, S + 1:2 * S - 1]).then_inc(sem("gramsT_a"), 1)
                b, v = s - 1, 1 - u
                if live(b):
                    dve.wait_ge(sem("projected"), b + 1)
                    hb = h_all[:, bass.ds(b * TPB, TPB), :]
                    dve.tensor_tensor(hb, bank[4 + v][:, 0:S].rearrange("p (t c) -> p t c", c=C),
                                      projb_bc[:, :].rearrange("p (a c) -> p a c", a=1).to_broadcast([P, TPB, C]),
                                      ALU.add).then_inc(sem("h_made"), 1)
                    hold(dve, sem("h_made"), b + 1)
                    for t in range(TPB):
                        last = dve.bn_stats(st[:, v, t, :], h_all[:, bass.ds(b * TPB + t, 1), :].rearrange("p a c -> p (a c)"))
                    last.then_inc(sem("halves_made"), 1)
                    hold(dve, sem("halves_made"), b + 1)
                    for t in range(TPB):
                        last = dve.bn_aggr(mv[:, v, t, :], st[:, v, t, :])
                    last.then_inc(sem("stats_made"), 1)
                    dve.wait_ge(sem("sd_made"), b + 1)
                    dve.reciprocal(rstd[:, v, :], sd[:, v, :]).then_inc(sem("rstd_made"), 1)
                    dve.wait_ge(sem("rstd_made"), b + 1)
                    dve.scalar_tensor_tensor(out=nmr[:, v, :], in0=mv[:, v, :, 0], scalar=-1.0, in1=rstd[:, v, :],
                                             op0=ALU.mult, op1=ALU.mult).then_inc(sem("nmr_made"), 1)

            steps(dve, 0, 4, 6, 2, B + 1, embed)

            dve.wait_ge(sem("xs_turned"), B)
            dve.tensor_scalar(gn[:, :], bank[7][:, 0:C + 1], 1.0 / NTOK, None, ALU.mult).then_inc(sem("mean_made"), 1)
            dve.wait_ge(sem("mean_turned"), 1)
            dve.tensor_copy(mrow[:, :], bank[0][0:1, 0:P]).then_inc(sem("mrow_made"), 1)
            dve.wait_ge(sem("mm_made"), 1)
            dve.tensor_tensor(cov[:, :], gn[:, 0:C], bank[1][:, 0:C], ALU.subtract).then_inc(sem("cov_made"), 1)
            dve.wait_ge(sem("covw"), 1)
            dve.tensor_tensor(wtc[:, :], wT[:, :], bank[2][:, 0:3 * C], ALU.mult).then_inc(sem("wtc_made"), 1)
            dve.wait_ge(sem("muvar_made"), 1)
            dve.tensor_copy(muvar[:, :, :].rearrange("p a g -> p (a g)"), bank[3][:, 0:6]).then_inc(sem("bn_var"), 1)
            dve.wait_ge(sem("bn_sd"), 1)
            chain(dve.reciprocal(bn_r[:, :], bn_sd[:, :]))
            chain(dve.tensor_tensor(bn_a[:, :], bn_r[:, :], cols7[:, 0:3], ALU.mult))
            chain(dve.tensor_tensor(bn_ma[:, :], muvar[:, 0, :], bn_a[:, :], ALU.mult))
            chain(dve.tensor_tensor(bn_b[:, :], cols7[:, 3:6], bn_ma[:, :], ALU.subtract))
            chain(dve.tensor_scalar(bn_bh[:, :], bn_b[:, :], HALF_UP, None, ALU.add))
            dve.sem_inc(sem("bn_made"), 1)
            dve.tensor_scalar(wv[:, :], wqkv[:, 2, :], bn_a[:, 2:3], None, ALU.mult)
            split(col3[:, 1, 0:1], col3[:, 1, 1:2], col3[:, 1, 2:3], bn_bh[:, 2:3], rest_c[:, 1, 0:1], rest_c[:, 1, 1:2])
            dve.sem_inc(sem("wv_made"), 1)
            dve.wait_ge(sem("wv_turned"), 1)
            dve.tensor_copy(bv3[:, :], bank[1][0:3, 0:C // 2].bitcast(BF16))
            split(vT3[:, 0, :], vT3[:, 1, :], vT3[:, 2, :], bank[0][:, 0:C], rest[:, 0:C], rest2[:, 0:C])
            dve.sem_inc(sem("vT_made"), 1)
            dve.wait_ge(sem("wgate_in"), 32)

            def att_even(b, v, c):
                dve.wait_ge(sem("scored0"), 2 * b + c + 1)
                if c == 0:
                    after(dve, sem("attended"), b - 1)
                for i in range(2):
                    last = dve.tensor_scalar(att[:, v, 2 * c, i].rearrange("p a n -> p (a n)"), bank[i][:, :],
                                             CAP, None, ALU.min)
                last.then_inc(sem("att_made0"), 1)

            def attend(s, u):
                b, v = s - 1, 1 - u
                if live(b):
                    dve.wait_ge(sem("attended"), b + 1)
                    after(dve, sem("o_read"), b - 1)
                    dve.tensor_scalar(o_bias[:, v:v + 1], bank[6][:, S:S + 1], upper[:, 0:1], 0.0625, ALU.mult, ALU.add)\
                        .then_inc(sem("o_bias_made"), 1)
                b, v = s + 1, 1 - u
                if live(b):
                    dve.wait_ge(sem("qk_read"), b + 1)
                    after(dve, sem("scored1"), 2 * (b - 1))
                    for par in range(2):
                        dve.tensor_scalar(qeo[:, v, par, :], qi[:, v, :], CAP, even_odd[:, par:par + 1], ALU.min, ALU.mult)
                    dve.tensor_scalar(kT[:, v, :], ki[:, v, :], CAP, None, ALU.min).then_inc(sem("qk_made"), 1)
                if live(s):
                    att_even(s, u, 0)
                b, v = s - 1, 1 - u
                if live(b):
                    dve.wait_ge(sem("o_read"), b + 1)
                    after(dve, sem("proj_out"), b - 1)
                    dve.tensor_scalar(oT[:, v, :], oi[:, v, :], CAP, None, ALU.min).then_inc(sem("oT_made"), 1)
                b, v = s + 1, 1 - u
                if live(b):
                    dve.wait_ge(sem("v_read"), b + 1)
                    after(dve, sem("attended"), b - 1)
                    vh = vi[:, v].rearrange("p t (g a d) -> p (t g) a d", a=2, d=16)
                    for par in range(2):
                        dst = veo[:, v, par].rearrange("p t (g a d) -> p (t g) a d", a=2, d=16)
                        last = dve.tensor_scalar(dst[:, :, par, :], vh[:, :, par, :], CAP, None, ALU.min)
                    last.then_inc(sem("v_made"), 1)
                b, v = s - 1, 1 - u
                if live(b):
                    dve.wait_ge(sem("proj_out"), b + 1)
                    hb = h_all[:, bass.ds(b * TPB, TPB), :]
                    dve.tensor_tensor(hb, bank[5][:, 0:S].rearrange("p (t c) -> p t c", c=C), hb, ALU.add)\
                        .then_inc(sem("h2_made"), 1)
                    hold(dve, sem("h2_made"), b + 1)
                    for t in range(TPB):
                        last = dve.bn_stats(st[:, v, t, :], h_all[:, bass.ds(b * TPB + t, 1), :].rearrange("p a c -> p (a c)"))
                    last.then_inc(sem("halves2_made"), 1)
                    after(dve, sem("row_made"), b - 1)
                    hold(dve, sem("halves2_made"), b + 1)
                    for t in range(TPB):
                        last = dve.bn_aggr(mv[:, v, t, :], st[:, v, t, :])
                    last.then_inc(sem("stats2_made"), 1)
                if live(s):
                    att_even(s, u, 1)
                b, v = s - 3, 1 - u
                if live(b):
                    dve.wait_ge(sem("routed"), b + 1)
                    after(dve, sem("lg_kept"), b)
                    dve.tensor_tensor(lg[:, :, 0:NE],
                                      bank[7][:, S:S + TPB * NE].rearrange("p (t e) -> p t e", e=NE),
                                      bgate_bc[:, :].rearrange("p (a e) -> p a e", a=1).to_broadcast([P, TPB, NE]),
                                      ALU.add).then_inc(sem("logits_made"), 1)
                    hold(dve, sem("logits_made"), b + 1)
                    for t in range(TPB):
                        last = dve.max(lg[:, t, NE:], lg[:, t, 0:NE])
                    last.then_inc(sem("top_made"), 1)
                    hold(dve, sem("top_made"), b + 1)
                    for t in range(TPB):
                        last = dve.max_index(topi[:, t, :], lg[:, t, NE:], lg[:, t, 0:NE])
                    last.then_inc(sem("topi_made"), 1)
                    dve.tensor_copy(lg_all[:, bass.ds(b * TPB, TPB), :], lg[:, :, :]).then_inc(sem("lg_kept"), 1)
                    dve.wait_ge(sem("topi_made"), b + 1)
                    dve.tensor_copy(topf[:, :, :], topi[:, :, 0:TOPK]).then_inc(sem("topf_made"), 1)
                    dve.wait_ge(sem("topf_made"), b + 1)
                    dve.tensor_tensor(chosen[:, v].rearrange("p t k e -> p (t k) e"),
                                      iota_e[:, :].rearrange("p (a e) -> p a e", a=1).to_broadcast([P, TPB * TOPK, NE]),
                                      topf[:, :, :].rearrange("p t (k a) -> p (t k) a", a=1).to_broadcast([P, TPB * TOPK, NE]),
                                      ALU.is_equal).then_inc(sem("chosen_made"), 1)
                    dve.wait_ge(sem("chosen_made"), b + 1)
                    after(dve, sem("ranked"), b)
                    dve.tensor_tensor(seen[:, v, 0, :], seen[:, 1 - v, 1, :], picks[:, 1 - v, 1, :], ALU.add)
                    dve.tensor_tensor(picks[:, v], chosen[:, v, :, 0, :], chosen[:, v, :, 1, :], ALU.add)\
                        .then_inc(sem("picked"), 1)
                    dve.wait_ge(sem("picked"), b + 1)
                    dve.tensor_tensor(seen[:, v, 1, :], seen[:, v, 0, :], picks[:, v, 0, :], ALU.add)\
                        .then_inc(sem("picks_made"), 1)
                b, v = s - 1, 1 - u
                if live(b):
                    dve.wait_ge(sem("sd2_made"), b + 1)
                    dve.reciprocal(rstd[:, v, :], sd[:, v, :]).then_inc(sem("rstd2_made"), 1)
                    dve.wait_ge(sem("rstd2_made"), b + 1)
                    dve.scalar_tensor_tensor(out=nmr[:, v, :], in0=mv[:, v, :, 0], scalar=-1.0, in1=rstd[:, v, :],
                                             op0=ALU.mult, op1=ALU.mult).then_inc(sem("nmr2_made"), 1)
                b, v = s - 3, 1 - u
                if live(b):
                    dve.wait_ge(sem("ranked"), b + 1)
                    dve.tensor_tensor(place[:, :, :], bank[4][:, 0:TPB * NE].rearrange("p (t e) -> p t e", e=NE),
                                      region0[:, :].rearrange("p (a e) -> p a e", a=1).to_broadcast([P, TPB, NE]),
                                      ALU.add).then_inc(sem("slot_read"), 1)
                    dve.wait_ge(sem("slot_read"), b + 1)
                    for k in range(TOPK):
                        last = dve.tensor_tensor(placed[:, :, k, :], place[:, :, :], chosen[:, v, :, k, :], ALU.mult)
                    last.then_inc(sem("placed_made"), 1)
                    dve.wait_ge(sem("placed_made"), b + 1)
                    after(dve, sem(f"rows_sent{v}"), 16 * TPB * TOPK * ((b - v) // 2) if isinstance(b, int)
                          else 8 * TPB * TOPK * (b - v))
                    with nc.allow_low_precision(reason="one term of a sum isn't zero, an integer below 2^24"):
                        dve.tensor_reduce(slot[:, v, :], placed[:, :, :, :].rearrange("p t k e -> p (t k) e"), AX, ALU.add)\
                            .then_inc(sem("slot_made"), 1)

            steps(dve, -1, 3, 6, 2, B + 2, attend)

            v = (B - 1) % 2
            chain(dve.tensor_tensor(total[:, :], seen[:, v, 1, :], picks[:, v, 1, :], ALU.add))
            dve.sem_inc(sem("total_made"), 1)
            dve.wait_ge(sem("counted"), 1)
            chain(dve.tensor_copy(count[:, :], bank[0][:, 0:NE]))
            chain(dve.tensor_scalar(ntile_i[:, :], count[:, :], P / 2 - 0.5, 1.0 / P, ALU.add, ALU.mult))
            chain(dve.tensor_copy(ntile[:, :], ntile_i[:, :]))
            chain(dve.tensor_tensor_scan(upto_t[:, :], onesf[:, :], ntile[:, :], 0.0, ALU.mult, ALU.add))
            chain(dve.tensor_tensor(prev_t[:, :], upto_t[:, :], ntile[:, :], ALU.subtract))
            chain(dve.scalar_tensor_tensor(out=origin[:, :], in0=prev_t[:, :], scalar=float(P), in1=count[:, :],
                                           op0=ALU.mult, op1=ALU.add))
            chain(dve.scalar_tensor_tensor(out=origin[:, :], in0=region0[:, :], scalar=-float(P), in1=origin[:, :],
                                           op0=ALU.add, op1=ALU.add))
            chain(dve.tensor_scalar(passed[:, :], upto_t[:, :], part_f[:, 0:1], None, ALU.is_le))
            chain(dve.tensor_reduce(mapc[:, 0:1], passed[:, :], AX, ALU.add))
            chain(dve.tensor_scalar(owner[:, :], iota_e[:, :], mapc[:, 0:1], None, ALU.is_equal))
            chain(dve.tensor_tensor(owner[:, :], owner[:, :], origin[:, :], ALU.mult))
            chain(dve.tensor_reduce(mapc[:, 1:2], owner[:, :], AX, ALU.add))
            chain(dve.scalar_tensor_tensor(out=mapf[:, 1:2], in0=part_f[:, :], scalar=-float(P), in1=mapc[:, 1:2],
                                           op0=ALU.mult, op1=ALU.add))
            chain(dve.tensor_scalar(mapf[:, 1:2], mapf[:, 1:2], 0.0, None, ALU.max))
            chain(dve.tensor_scalar(mapf[:, 0:1], mapc[:, 0:1], float(NE - 1), None, ALU.min))
            dve.sem_inc(sem("map_cols"), 1)
            dve.wait_ge(sem("map_turned"), 1)
            dve.tensor_copy(tmap[:, :], bank[1][0:1, 0:2 * P]).then_inc(sem("map_made"), 1)

            dve.wait_ge(sem("bias_in"), 48)
            chain(dve.tensor_copy(bias3[0:NE, :], bias_f[:, :]))
            chain(dve.tensor_tensor(bias_r[:, :], bias_f[:, :], bias3[0:NE, :], ALU.subtract))
            chain(dve.tensor_copy(bias_m[:, :], bias_r[:, :]))
            chain(dve.tensor_copy(bias3[NE:2 * NE, :], bias_m[:, :]))
            chain(dve.tensor_tensor(bias_r[:, :], bias_r[:, :], bias_m[:, :], ALU.subtract))
            chain(dve.tensor_copy(bias3[2 * NE:3 * NE, :], bias_r[:, :]))
            for i in range(3):
                chain(dve.tensor_copy(sel3[i * NE:(i + 1) * NE, :], identb[0:NE, 0:NE]))
            dve.sem_inc(sem("bias3_made"), 1)

            dve.tensor_tensor(e2[:, :], lg_all[:, :, NE + 1], lg_all[:, :, NE], ALU.subtract)
            chain(dve.tensor_tensor(e_all[:, :, :], lg_all[:, :, 0:NE], lg_all[:, :, NE:NE + 1].to_broadcast([P, NT, NE]), ALU.subtract))
            dve.sem_inc(sem("shifted"), 1)
            dve.wait_ge(sem("exps_made"), 1)
            chain(dve.tensor_reduce(den[:, :], e_all[:, :, :], AX, ALU.add))
            chain(dve.reciprocal(w12[:, 0, :], den[:, :]))
            chain(dve.tensor_tensor(w12[:, 1, :], w12[:, 0, :], e2[:, :], ALU.mult))

            def expert_tile(j, u):
                i = j - 1
                if live(i, NTILE):
                    w = (u - 1) % 2
                    dve.wait_ge(sem("silu_made"), i + 1)
                    after(dve, sem("hh_turned"), i - 1)
                    dve.tensor_tensor(hh[:, w, :], sg[:, w, :], bank[w][:, FF:2 * FF], ALU.mult).then_inc(sem("hh_made"), 1)
                i = j - 3
                if live(i, NTILE):
                    w = (u - 3) % XR
                    dve.wait_ge(sem("y_out"), i + 1)
                    after(dve, sem(f"y_sent{w}"), 16 * (i // XR) if isinstance(i, int) else 4 * (i - w))
                    dve.tensor_copy(yy[:, w, :], bank[6 + w % 2][:, 0:C]).then_inc(sem("y_made"), 1)
                if live(j, NTILE):
                    dve.wait_ge(sem("x_turned"), j + 1)
                    after(dve, sem("gu_out"), j - 1)
                    dve.tensor_copy(xgT[:, u % 2, :], bank[2 + u % 2][:, 0:P]).then_inc(sem("xgT_made"), 1)
                    after(dve, sem(f"y_sent{u}"), 16 * (j // XR) if isinstance(j, int) else 4 * (j - u))
                    dve.tensor_copy(pair_i[:, u, :], xg[:, u, C:C + 1].bitcast(U32)).then_inc(sem("pair_kept"), 1)

            steps(dve, 0, 4, 23, XR, NTILE + 2, expert_tile)

            for g in range(NFG):
                dve.wait_ge(sem(f"fin_in{g % 2}"), 16 * TOPK * (g // 2 + 1))
                for k in range(TOPK):
                    for t in range(FG):
                        tt = g * FG + t
                        last = dve.scalar_tensor_tensor(out=h_all[:, tt, :], in0=y_fin[:, g % 2, k, t, :],
                                                        scalar=w12[:, k, tt:tt + 1], in1=h_all[:, tt, :],
                                                        op0=ALU.mult, op1=ALU.add)
                    last.then_inc(sem("fin_part"), 1)
                    dve.wait_ge(sem("fin_part"), TOPK * g + k + 1)
                dve.sem_inc(sem("fin_used"), 1)
                dve.sem_inc(sem("fin_made"), 1)


_INS = ['x', 'L0_tok_emb_2', 'L0_tok_emb_3', 'L0_tok_emb_4', 'L0_tok_proj_w', 'L0_tok_proj_b', 'L0_attn_Wqkv',
        'L0_attn_gamma', 'L0_attn_beta', 'L0_attn_Wproj', 'L0_attn_bproj', 'L0_ffn_Wgate', 'L0_ffn_bgate',
        'L0_ffn_Wg', 'L0_ffn_bg', 'L0_ffn_Wu', 'L0_ffn_bu', 'L0_ffn_Wd', 'L0_ffn_bd']


def kernel(**inputs):
    import numpy as _np
    import concourse.bacc as _bacc
    from concourse import mybir as _mybir
    from concourse.bass_utils import run_bass_kernel_spmd as _run

    nc = _bacc.Bacc("TRN2", target_bir_lowering=False, num_devices=1)
    arrays, aps = {}, {}
    for name in _INS:
        a = _np.ascontiguousarray(inputs[name])
        arrays[f"in_{name}"] = a
        aps[name] = nc.dram_tensor(f"in_{name}", a.shape, _mybir.dt.from_np(a.dtype), kind="ExternalInput").ap()
    out = nc.dram_tensor("out_h", (B, S, C), F32, kind="ExternalOutput").ap()
    a = [aps[n] for n in _INS]
    build(nc, a[0], a[1:4], *a[4:], out)
    r = _run(nc, [arrays], core_ids=[0])
    return r.results[0]["out_h"]
```

```python
from contextlib import ExitStack

import concourse.bass as bass
from concourse import mybir

F32 = mybir.dt.float32
BF16 = mybir.dt.bfloat16
I16 = mybir.dt.int16
I32 = mybir.dt.int32
U32 = mybir.dt.uint32
ALU = mybir.AluOpType
ACT = mybir.ActivationFunctionType
AX = mybir.AxisListType.X

P = 128
B, S = 16, 256
NTOK = B * S
TPB = S // P
NT = NTOK // P
C = 128
NG = 3
VOCAB = 64
HASHED = 25000
HALO = 2
EPS = 1e-5
CAP = 4.0
HALF_UP = 2.0 ** -22
NE = 32
TOPK = 2
EPR = NE // B
FF = 256
FC = FF // P
REGION = NTOK + P
ROW = C + 4
NPAIR = TOPK * NTOK
NTILE = 96
NO_PAIR = 2.0 ** 30
ROUNDS = 4
RR = 4
BIG = 1.5 * 2.0 ** 23
FG = 4
NFG = NT // FG
FILL = (1, 2, 8, 10)


def live(b, n=B):
    return not isinstance(b, int) or 0 <= b < n


def upto(b, n=B):
    return min(b, n) if isinstance(b, int) else b


def after(eng, sem, count):
    if not isinstance(count, int) or count > 0:
        eng.wait_ge(sem, count)


def hold(eng, sem, count):
    if not isinstance(count, int) or count > 0:
        eng.wait_ge(sem, count)
        eng.nop(nofuse=True)


def steps(eng, first, steady, pairs, unroll, last, step):
    for b in range(first, steady):
        step(b, b % unroll)
    with eng.Fori(0, pairs) as i:
        for u in range(unroll):
            step(unroll * i + (steady + u), (steady + u) % unroll)
    for b in range(steady + pairs * unroll, last + 1):
        step(b, b % unroll)


def build(nc, x, emb, proj_w, proj_b, Wqkv, gamma, beta, Wproj, bproj, Wgate, bgate,
          Wg, bg, Wu, bu, Wd, bd, out):
    ctx = ExitStack()
    with ctx:
        def sb(name, shape, dt):
            return ctx.enter_context(nc.sbuf_tensor(name, shape, dt))

        sems = {}

        def sem(name):
            if name not in sems:
                sems[name] = ctx.enter_context(nc.semaphore(name))
            return sems[name]

        regions = nc.dram_tensor("regions", [NE * REGION, ROW], F32, kind="Internal").ap()
        results = nc.dram_tensor("results", [NPAIR, C], F32, kind="Internal").ap()

        ident = sb("ident", [P, P], F32)
        identb = sb("identb", [P, P], BF16)
        before = sb("before", [P, P], F32)
        beforeb = sb("beforeb", [P, P], BF16)
        onesb = sb("onesb", [P, P], BF16)
        onesf = sb("onesf", [P, NE], F32)
        iota_e = sb("iota_e", [P, NE], F32)
        region0 = sb("region0", [P, NE], F32)
        part_i = sb("part_i", [P, 1], I32)
        part_f = sb("part_f", [P, 1], F32)
        head_i = sb("head_i", [P, 1], I32)
        head = sb("head", [P, 4], F32)
        upper = sb("upper", [P, 1], F32)
        o_scale = sb("o_scale", [P, 1], F32)
        eps = sb("eps", [P, 1], F32)
        four = sb("four", [P, 1], F32)
        number = sb("number", [P, NT], F32)
        pad_row = sb("pad_row", [P, ROW], F32)
        projb_bc = sb("projb_bc", [P, C], F32)
        bgate_bc = sb("bgate_bc", [P, NE], F32)
        wgate = sb("wgate", [P, NE], F32)
        wqkv = sb("wqkv", [P, 3, C], F32)
        wproj = sb("wproj", [P, C], F32)
        wemb = sb("wemb", [P, NG * C], F32)
        rows7 = sb("rows7", [7, C], F32)
        cols7 = sb("cols7", [P, 7], F32)
        wembT = sb("wembT", [P, NG, C], F32)
        wT = sb("wT", [P, 3 * C], F32)
        wprojT = sb("wprojT", [P, C], F32)
        qkT3 = sb("qkT3", [P, 3, 2 * C], BF16)
        vT3 = sb("vT3", [P, 3, C], BF16)
        prT3 = sb("prT3", [P, 3, C], BF16)
        rest = sb("rest", [P, 2 * C], F32)
        rest2 = sb("rest2", [P, 2 * C], F32)
        col3 = sb("col3", [P, 2, 3], BF16)
        rest_c = sb("rest_c", [P, 2, 2], F32)
        bp3 = sb("bp3", [3, C], BF16)
        bv3 = sb("bv3", [3, C], BF16)

        tok_i = sb("tok_i", [NT, HALO + P + 2], I32)
        tok_f = sb("tok_f", [NT, HALO + P + 2], F32)
        hsh = sb("hsh", [NT, NG, P + 1], F32)
        h_t = sb("h_t", [NT, P + 1], F32)
        h_q = sb("h_q", [NT, NG, P + 1], F32)
        ids = sb("ids", [P, NT, NG], U32)
        id_ring = sb("id_ring", [P, 2, TPB * NG], U32)

        grams_mem = sb("grams_mem", [P, 2 * TPB * NG * C], F32)
        grams = grams_mem[:, :].rearrange("p (v t n c) -> p v t n c", v=2, t=TPB, n=NG)
        gramsT_mem = sb("gramsT_mem", [P, 2 * NG * S], F32)
        gramsT = gramsT_mem[:, :].rearrange("p (v n s) -> p v n s", v=2, n=NG)
        h_all = sb("h_all", [P, NT, C], F32)
        st = sb("st", [P, 2, TPB, 6], F32)
        mv = sb("mv", [P, 2, TPB, 2], F32)
        sd = sb("sd", [P, 2, TPB], F32)
        rstd = sb("rstd", [P, 2, TPB], F32)
        nmr = sb("nmr", [P, 2, TPB], F32)
        xi = sb("xi", [P, 2, TPB, C], I16)
        xs = sb("xs", [P, 2, TPB, C + 1], BF16)
        xsT = sb("xsT", [P, NTOK], BF16)

        gn = sb("gn", [P, C + 1], F32)
        mrow = sb("mrow", [1, C], F32)
        cov = sb("cov", [P, C], F32)
        wtc = sb("wtc", [P, 3 * C], F32)
        muvar = sb("muvar", [P, 2, 3], F32)
        bn_sd = sb("bn_sd", [P, 3], F32)
        bn_r = sb("bn_r", [P, 3], F32)
        bn_a = sb("bn_a", [P, 3], F32)
        bn_ma = sb("bn_ma", [P, 3], F32)
        bn_b = sb("bn_b", [P, 3], F32)
        bn_bh = sb("bn_bh", [P, 3], F32)
        wv = sb("wv", [P, C], F32)

        qi = sb("qi", [P, 2, S], I16)
        ki = sb("ki", [P, 2, S], I16)
        vi = sb("vi", [P, 2, TPB, C], I16)
        qh = gramsT_mem[:, 0:4 * S].bitcast(BF16).rearrange("p (v j s) -> p v j s", v=2, j=4)
        kT = sb("kT", [P, 2, S], BF16)
        veo = sb("veo", [P, 2, 2, TPB, C], BF16)
        att_mem = sb("att_mem", [P, 2 * ROUNDS * 4 * S], BF16)
        att = att_mem[:, :].rearrange("p (v r i a n) -> p v r i a n", v=2, r=ROUNDS, i=2, a=2)
        o_bias = sb("o_bias", [P, 2], F32)
        oi = sb("oi", [P, 2, S], I16)
        oT = sb("oT", [P, 2, S], BF16)
        row_mem = sb("row_mem", [P, RR * TPB * ROW], F32)
        row = row_mem[:, :].rearrange("p (v t c) -> p v t c", v=RR, t=TPB)
        x2T = sb("x2T", [P, S], F32)
        lg = sb("lg", [P, TPB, NE + 8], F32)
        lg_all = sb("lg_all", [P, NT, NE + 8], F32)
        topi = sb("topi", [P, TPB, 8], U32)
        topf = sb("topf", [P, TPB, TOPK], F32)
        chosen = sb("chosen", [P, 2, TPB, TOPK, NE], F32)
        picks = sb("picks", [P, 2, TPB, NE], BF16)
        seen = sb("seen", [P, 2, TPB, NE], BF16)
        place = sb("place", [P, TPB, NE], F32)
        placed = sb("placed", [P, TPB, TOPK, NE], F32)
        slot = sb("slot", [P, RR, TPB * TOPK], U32)

        wgu = sb("wgu", [P, NE, 2 * FF], F32)
        wd = sb("wd", [P, NE, FC, C], F32)
        bias_f = sb("bias_f", [NE, 2 * FF + C], F32)
        bias3 = sb("bias3", [3 * NE, 2 * FF + C], BF16)
        sel3 = sb("sel3", [3 * NE, NE], BF16)
        total = sb("total", [P, NE], BF16)
        count = sb("count", [P, NE], F32)
        ntile_i = sb("ntile_i", [P, NE], I16)
        ntile = sb("ntile", [P, NE], F32)
        upto_t = sb("upto_t", [P, NE], F32)
        prev_t = sb("prev_t", [P, NE], F32)
        origin = sb("origin", [P, NE], F32)
        passed = sb("passed", [P, NE], F32)
        owner = sb("owner", [P, NE], F32)
        mapc = sb("mapc", [P, 2], F32)
        mapf = sb("mapf", [P, 2], F32)
        tmap = sb("tmap", [1, 2 * P], I32)
        den = sb("den", [P, NT], F32)
        e2 = sb("e2", [P, NT], F32)
        w12 = sb("w12", [P, TOPK, NT], F32)
        XR = 8
        YR = 4
        pair_i = sb("pair_i", [P, XR, 1], U32)
        xg = grams_mem[:, 0:XR * ROW].rearrange("p (r c) -> p r c", r=XR)
        tile_e = grams_mem[:, XR * ROW:XR * ROW + P]
        yy = row_mem[:, 0:YR * C].rearrange("p (r c) -> p r c", r=YR)
        xgT = row_mem[:, YR * C:YR * C + 2 * P].rearrange("p (r c) -> p r c", r=2)
        sg, hh, hhT = [gramsT_mem[:, i * 2 * FF:(i + 1) * 2 * FF] for i in range(3)]
        sg = sg.rearrange("p (r n) -> p r n", r=2)
        hh = hh.rearrange("p (r n) -> p r n", r=2)
        hhT = hhT.rearrange("p (r c n) -> p r c n", r=2, c=FC)
        y_fin = wgu[:, 0:NPAIR * C // P // (2 * FF), :].rearrange("p e n -> p (e n)")\
            .rearrange("p (g t k c) -> p g t k c", g=NFG, k=TOPK, t=FG)
        late = att_mem[:, :].bitcast(F32)
        e_all = late[:, 0:NT * NE].rearrange("p (t e) -> p t e", e=NE)
        spare = NT * NE
        bias_r = late[0:NE, spare:spare + 2 * FF + C]
        spare = 2 * (spare + 2 * FF + C)
        bias_m = att_mem[0:NE, spare:spare + 2 * FF + C]

        bank = [ctx.enter_context(nc.psum_tensor(f"bank{i}", [P, 512], F32)) for i in range(8)]

        def rows_sent(b, w):
            return 16 * TPB * TOPK * (b - w) // RR if isinstance(b, int) else 16 * TPB * TOPK // RR * (b - w)

        block = ctx.enter_context(nc.Block())

        @block.sync
        def _(sp):
            xr = x.rearrange("b (t p) -> (b t) p", p=P)
            sp.wait_ge(sem("tok_clear"), 1)
            sp.dma_start(tok_i[:, HALO:HALO + P], xr).then_inc(sem("tok_in"), 16)
            sp.dma_start(tok_i[1:NT, 0:HALO], xr[0:NT - 1, P - HALO:P]).then_inc(sem("tok_in"), 16)
            sp.dma_start(tok_i[0:NT - 1, HALO + P:], xr[1:NT, 0:2]).then_inc(sem("tok_in"), 16)
            sp.dma_start(wemb[:, :], proj_w).then_inc(sem("wemb_in"), 16)
            sp.dma_start(projb_bc[:, :], proj_b.rearrange("(a n) -> a n", a=1).to_broadcast([P, C]))\
                .then_inc(sem("projb_in"), 16)
            sp.dma_start(wqkv[:, :, :], Wqkv.rearrange("(g p) c -> p g c", p=P)).then_inc(sem("wattn_in"), 16)
            sp.dma_start(wproj[:, :], Wproj).then_inc(sem("wattn_in"), 16)
            sp.dma_start(rows7[0:3, :], gamma.rearrange("(g p) -> g p", p=P)).then_inc(sem("wattn_in"), 16)
            sp.dma_start(rows7[3:6, :], beta.rearrange("(g p) -> g p", p=P)).then_inc(sem("wattn_in"), 16)
            sp.dma_start(rows7[6:7, :], bproj.rearrange("(a p) -> a p", a=1)).then_inc(sem("wattn_in"), 16)
            sp.dma_start(wgate[:, :], Wgate).then_inc(sem("wgate_in"), 16)
            sp.dma_start(bgate_bc[:, :], bgate.rearrange("(a n) -> a n", a=1).to_broadcast([P, NE]))\
                .then_inc(sem("wgate_in"), 16)
            sp.dma_start(bias_f[:, 0:FF], bg).then_inc(sem("bias_in"), 16)
            sp.dma_start(bias_f[:, FF:2 * FF], bu).then_inc(sem("bias_in"), 16)
            sp.dma_start(bias_f[:, 2 * FF:], bd).then_inc(sem("bias_in"), 16)
            with sp.Fori(0, B) as b:
                sp.wait_ge(sem("grams_used"), b + 1)
                e = b * EPR
                sp.dma_start(wgu[:, bass.ds(e, EPR), 0:FF], Wg[bass.ds(e, EPR)].rearrange("e h i -> h e i"))\
                    .then_inc(sem("experts_in"), 16)
                sp.dma_start(wgu[:, bass.ds(e, EPR), FF:], Wu[bass.ds(e, EPR)].rearrange("e h i -> h e i"))\
                    .then_inc(sem("experts_in"), 16)
                sp.dma_start(wd[:, bass.ds(e, EPR)], Wd[bass.ds(e, EPR)].rearrange("e (c p) h -> p e c h", p=P))\
                    .then_inc(sem("experts_in"), 16)
            sp.wait_ge(sem("pad_made"), 1)
            sp.dma_start(regions.rearrange("(e r) c -> r e c", e=NE)[0:P],
                         pad_row[:, :].rearrange("p (a c) -> p a c", a=1).to_broadcast([P, NE, ROW]))\
                .then_inc(sem("pads_in"), 16)

            sp.wait_ge(sem("map_made"), 1)
            for w in range(RR):
                sp.wait_ge(sem(f"rows_sent{w}"), 16 * TPB * TOPK * B // RR)

            def load_tile(j, u):
                start = sp.value_load(tmap[0:1, bass.ds(P + j, 1)], min_val=0, max_val=NE * REGION - P)
                after(sp, sem("x_turned"), j - XR + 1)
                after(sp, sem("pair_kept"), j - XR + 1)
                sp.dma_start(xg[:, u, :], regions[bass.ds(start, P), :]).then_inc(sem(f"x_in{u}"), 16)

            steps(sp, 0, 8, 11, XR, NTILE - 1, load_tile)

            for u in range(XR):
                sp.wait_ge(sem(f"y_sent{u}"), 16 * NTILE // XR)
            res = results.rearrange("(t p k) c -> p t k c", k=TOPK, p=P)
            for g in range(NFG):
                sp.dma_start(y_fin[:, g], res[:, g * FG:(g + 1) * FG]).then_inc(sem(f"fin_in{g}"), 16)

        @block.gpsimd
        def _(pool):
            pool.memset(tok_i[:, :], 0).then_inc(sem("tok_clear"), 1)
            pool.memset(ident[:, :], 0.0).then_inc(sem("pool_c"), 1)
            pool.memset(before[:, :], 0.0).then_inc(sem("pool_c"), 1)
            pool.memset(pad_row[:, :], 0.0).then_inc(sem("pool_c"), 1)
            pool.wait_ge(sem("pool_c"), 3)
            pool.affine_select(out=ident[:, :], in_=ident[:, :], compare_op=ALU.not_equal, fill=1.0,
                               base=0, pattern=[[-1, P]], channel_multiplier=1).then_inc(sem("ident_made"), 1)
            pool.affine_select(out=before[:, :], in_=before[:, :], compare_op=ALU.is_ge, fill=1.0,
                               base=0, pattern=[[-1, P]], channel_multiplier=1).then_inc(sem("before_made"), 1)
            pool.memset(pad_row[:, C:C + 1], NO_PAIR).then_inc(sem("pad_made"), 1)
            pool.iota(part_i[:, :], pattern=[[0, 1]], base=0, channel_multiplier=1).then_inc(sem("iotas"), 1)
            pool.iota(number[:, :], pattern=[[TOPK * P, NT]], base=0, channel_multiplier=TOPK,
                      allow_small_or_imprecise_dtypes=True).then_inc(sem("iotas"), 1)
            pool.iota(iota_e[:, :], pattern=[[1, NE]], base=0, channel_multiplier=0,
                      allow_small_or_imprecise_dtypes=True).then_inc(sem("iotas"), 1)
            pool.iota(region0[:, :], pattern=[[REGION, NE]], base=P, channel_multiplier=0,
                      allow_small_or_imprecise_dtypes=True).then_inc(sem("iotas"), 1)

            pool.wait_ge(sem("ids_made"), 1)

            def gather(b, u):
                hold(pool, sem(f"grams_in{u}"), 16 * TPB * NG * ((b - u) // 2) if isinstance(b, int)
                      else 8 * TPB * NG * (b - u))
                pool.tensor_copy(id_ring[:, u, :].rearrange("p (t n) -> p t n", n=NG),
                                 ids[:, bass.ds(b * TPB, TPB), :]).then_inc(sem("ids_staged"), 1)
                hold(pool, sem("ids_staged"), b + 1)
                hold(pool, sem("grams_used"), b - 1)
                for t in range(TPB):
                    for n in range(NG):
                        k = t * NG + n
                        pool.indirect_dma_start(grams[:, u, t, n, :], None, emb[n],
                                                bass.IndirectOffsetOnAxis(ap=id_ring[:, u, k:k + 1], axis=0))\
                            .then_inc(sem(f"grams_in{u}"), 16)

            steps(pool, 0, 2, 7, 2, B - 1, gather)

            pool.wait_ge(sem("pads_in"), 16)

            def dispatch(s, u):
                b, w = s - 3, (u - 3) % RR
                if live(b):
                    hold(pool, sem(f"rows_sent{w}"), rows_sent(b, w))
                    pool.tensor_copy(row[:, w, :, C:C + 1],
                                     number[:, bass.ds(b * TPB, TPB)].rearrange("p (t a) -> p t a", a=1))\
                        .then_inc(sem("numbered"), 1)
                b, w = s - 5, (u - 5) % RR
                if live(b):
                    hold(pool, sem("numbered"), b + 1)
                    hold(pool, sem("slot_made"), b + 1)
                    for i in range(TPB * TOPK):
                        pool.indirect_dma_start(
                            regions, bass.IndirectOffsetOnAxis(ap=slot[:, w, i:i + 1], axis=0),
                            row[:, w, i // TOPK, :], None).then_inc(sem(f"rows_sent{w}"), 16)

            steps(pool, 3, 5, 2, 4, B + 4, dispatch)

            def collect(j, u):
                hold(pool, sem("y_made"), j + 1)
                pool.indirect_dma_start(
                    results, bass.IndirectOffsetOnAxis(ap=pair_i[:, u, :], axis=0), yy[:, u % YR, :], None,
                    bounds_check=NPAIR - 1, oob_is_err=False).then_inc(sem(f"y_sent{u}"), 16)

            steps(pool, 0, 4, 11, XR, NTILE - 1, collect)

        @block.tensor
        def _(pe):
            pe.wait_ge(sem("ident_made"), 1)
            pe.wait_ge(sem("hashed"), 1)
            for n in range(NG):
                last = pe.transpose(bank[0][:, n * NT:(n + 1) * NT], hsh[:, n, 1:], ident[0:NT, 0:NT])
            last.then_inc(sem("ids_turned"), 1)
            pe.wait_ge(sem("wemb_in"), 16)
            for n in range(NG):
                last = pe.transpose(bank[1][:, n * C:(n + 1) * C], wemb[:, n * C:(n + 1) * C], ident[:, :])
            last.then_inc(sem("wemb_turned"), 1)
            pe.wait_ge(sem("wattn_in"), 80)
            for g in range(3):
                pe.transpose(bank[2][:, g * C:(g + 1) * C], wqkv[:, g, :], ident[:, :])
            pe.transpose(bank[3][:, 0:C], wproj[:, :], ident[:, :])
            pe.transpose(bank[3][:, C:C + 7], rows7[:, :], ident[0:7, 0:7]).then_inc(sem("wattn_turned"), 1)
            pe.wait_ge(sem("identb_made"), 1)
            pe.wait_ge(sem("bp_split"), 1)
            pe.transpose(bank[4][0:3, 0:C // 2].bitcast(BF16), col3[:, 0, :], identb[:, :]).then_inc(sem("bp_turned"), 1)
            pe.wait_ge(sem("setup_done"), 1)

            def embed(s, u):
                b, v = s, u
                if live(b):
                    pe.wait_ge(sem(f"grams_in{v}"), 8 * TPB * NG * (b - v) + 16 * TPB * NG)
                    after(pe, sem("gramsT_a"), b - 1)
                    after(pe, sem("gramsT_b"), b - 1)
                    for n in range(NG):
                        for t in range(TPB):
                            dst = bank[2 * v + n // 2][:, (n % 2) * S + t * P:(n % 2) * S + (t + 1) * P]
                            last = pe.transpose(dst, grams[:, v, t, n, :], ident[:, :])
                    last.then_inc(sem("grams_used"), 1)
                b, v = s - 1, 1 - u
                if live(b):
                    pe.wait_ge(sem("gramsT_a"), b + 1)
                    pe.wait_ge(sem("gramsT_b"), b + 1)
                    after(pe, sem("h_made"), b - 1)
                    for t in range(TPB):
                        for n in range(NG):
                            last = pe.matmul(bank[4 + v][:, t * C:(t + 1) * C], gramsT[:, v, n, t * P:(t + 1) * P],
                                             wembT[:, n, :], start=(n == 0), stop=(n == NG - 1))
                    last.then_inc(sem("projected"), 1)
                b, v = s - 2, u
                if live(b):
                    pe.wait_ge(sem("xs_made"), b + 1)
                    after(pe, sem("xsT_made"), b)
                    for t in range(TPB):
                        pe.transpose(bank[6][:, t * C // 2:(t + 1) * C // 2].bitcast(BF16), xs[:, v, t, 0:C], identb[:, :])
                    for t in range(TPB):
                        last = pe.matmul(bank[7][:, 0:C + 1], xs[:, v, t, 0:C], xs[:, v, t, :],
                                         start=(isinstance(b, int) and b == 0 and t == 0),
                                         stop=(isinstance(b, int) and b == B - 1 and t == TPB - 1))
                    last.then_inc(sem("xs_turned"), 1)

            steps(pe, 0, 4, 6, 2, B + 1, embed)

            def keep_clock(n):
                for _ in range(n):
                    pe.matmul(bank[5][:, :], onesb[:, :], xsT[:, 0:512], start=True, stop=True)

            pe.wait_ge(sem("mean_made"), 1)
            pe.transpose(bank[0][0:1, 0:P], gn[:, C:C + 1], ident[:, :]).then_inc(sem("mean_turned"), 1)
            keep_clock(FILL[0])
            pe.wait_ge(sem("mrow_made"), 1)
            pe.matmul(bank[1][:, 0:C], mrow[:, :], mrow[:, :], start=True, stop=True).then_inc(sem("mm_made"), 1)
            for g in range(3):
                last = pe.matmul(bank[3][:, g:g + 1], wT[:, g * C:(g + 1) * C], gn[:, C:C + 1], start=True, stop=True)
            pe.wait_ge(sem("cov_made"), 1)
            pe.matmul(bank[2][:, 0:3 * C], cov[:, :], wT[:, :], start=True, stop=True).then_inc(sem("covw"), 1)
            keep_clock(FILL[1])
            pe.wait_ge(sem("wtc_made"), 1)
            for g in range(3):
                last = pe.matmul(bank[3][:, 3 + g:4 + g], wtc[:, g * C:(g + 1) * C], onesf[:, 0:1], start=True, stop=True)
            last.then_inc(sem("muvar_made"), 1)
            keep_clock(FILL[2])
            pe.wait_ge(sem("wv_made"), 1)
            pe.transpose(bank[0][:, 0:C], wv[:, :], ident[:, :])
            pe.transpose(bank[1][0:3, 0:C // 2].bitcast(BF16), col3[:, 1, :], identb[:, :]).then_inc(sem("wv_turned"), 1)

            keep_clock(FILL[3])
            pe.wait_ge(sem("vT_made"), 1)

            def scores(b, v, q):
                c, i = q // 2, q % 2
                if q == 0:
                    pe.wait_ge(sem("qk_made"), b + 1)
                for half in range(2):
                    after(pe, sem(f"att_made{half}"), 4 * b + (q - 1))
                    g = half * (P // 2)
                    for par in range(2):
                        last = pe.matmul(bank[2 * half + i][:, par * S:(par + 1) * S],
                                         kT[g:g + P // 2, v, c * P:(c + 1) * P], qh[g:g + P // 2, v, 2 * i + par, :],
                                         start=True, stop=True)
                    last.then_inc(sem(f"scored{half}"), 1)

            def attend(s, u):
                if live(s):
                    scores(s, u % 2, 0)
                b = s - 4
                if live(b):
                    pe.wait_ge(sem("x2T_made"), b + 1)
                    for t in range(TPB):
                        last = pe.matmul(bank[7][:, t * NE:(t + 1) * NE], x2T[:, t * P:(t + 1) * P], wgate[:, :],
                                         start=True, stop=True)
                    last.then_inc(sem("routed"), 1)
                b, v = s - 1, (u - 1) % 2
                if live(b):
                    pe.wait_ge(sem("v_made"), b + 1)
                    after(pe, sem("o_read"), b)
                    for i, (par, c) in enumerate([(0, 0), (0, 1), (1, 0), (1, 1)]):
                        last = pe.matmul(bank[6][:, S:S + 1], veo[:, v, par, c, :], onesb[:, 0:1], start=(i == 0), stop=(i == 3))
                    last.then_inc(sem("v_summed"), 1)
                if live(s):
                    scores(s, u % 2, 1)
                b, v = s - 5, (u - 5) % 2
                if live(b):
                    pe.wait_ge(sem("picks_made"), b + 1)
                    after(pe, sem("slot_read"), b)
                    ranks = bank[7][:, TPB * NE:2 * TPB * NE]
                    pe.matmul(ranks, beforeb[:, :], picks[:, v].rearrange("p t e -> p (t e)"), start=True, stop=False)
                    pe.matmul(ranks, onesb[:, :], seen[:, v].rearrange("p t e -> p (t e)"), start=False, stop=True)\
                        .then_inc(sem("ranked"), 1)
                b, v = s - 2, (u - 2) % 2
                if live(b):
                    pe.wait_ge(sem("oT_made"), b + 1)
                    pe.wait_ge(sem("v_read"), upto(b + 3))
                    for t in range(TPB):
                        for part in range(3):
                            pe.matmul(bank[5][:, t * C:(t + 1) * C], oT[:, v, t * P:(t + 1) * P], prT3[:, part, :],
                                      start=(part == 0), stop=False)
                        last = pe.matmul(bank[5][:, t * C:(t + 1) * C], onesb[0:3, :], bp3[:, :], start=False, stop=True)
                    last.then_inc(sem("proj_out"), 1)
                b = s + 1
                if live(b):
                    after(pe, sem("qk_read"), b)
                    for g in range(2):
                        for part in range(3):
                            last = pe.matmul(bank[4][:, g * S:(g + 1) * S], qkT3[:, part, g * C:(g + 1) * C],
                                             xsT[:, bass.ds(b * S, S)], start=(part == 0), stop=(part == 2))
                    last.then_inc(sem("qk_out"), 1)
                if live(s):
                    scores(s, u % 2, 2)
                b, v = s - 1, (u - 1) % 2
                if live(b):
                    pe.wait_ge(sem("att_made0"), 4 * b + 4)
                    pe.wait_ge(sem("att_made1"), 4 * b + 4)
                    pe.wait_ge(sem("o_bias_made"), b + 1)
                    for i, (par, c) in enumerate([(0, 0), (0, 1), (1, 0), (1, 1)]):
                        for g in range(4):
                            last = pe.matmul(bank[6][32 * g:32 * g + 32, 0:S], veo[:, v, par, c, 32 * g:32 * g + 32],
                                             att[:, v, 2 * c + g // 2, g % 2, par, :],
                                             start=(i == 0), stop=(i == 3))
                    last.then_inc(sem("attended"), 1)
                b, w = s - 3, (u - 3) % RR
                if live(b):
                    pe.wait_ge(sem("row_made"), b + 1)
                    after(pe, sem("logits_made"), b)
                    after(pe, sem("slot_read"), b - 1)
                    for t in range(TPB):
                        last = pe.transpose(bank[7][:, t * P:(t + 1) * P], row[:, w, t, 0:C], ident[:, :])
                    last.then_inc(sem("x2_turned"), 1)
                if live(s):
                    scores(s, u % 2, 3)
                b = s + 1
                if live(b):
                    after(pe, sem("v_read"), b)
                    after(pe, sem("h2_made"), b - 2)
                    for t in range(TPB):
                        for part in range(3):
                            pe.matmul(bank[5][:, t * C:(t + 1) * C], xsT[:, bass.ds(b * S + t * P, P)],
                                      vT3[:, part, :], start=(part == 0), stop=False)
                        last = pe.matmul(bank[5][:, t * C:(t + 1) * C], onesb[0:3, :], bv3[:, :], start=False, stop=True)
                    last.then_inc(sem("v_out"), 1)

            steps(pe, -1, 5, 2, 4, B + 4, attend)

            pe.wait_ge(sem("total_made"), 1)
            pe.matmul(bank[0][:, 0:NE], onesb[:, :], total[:, :], start=True, stop=True).then_inc(sem("counted"), 1)
            pe.wait_ge(sem("map_cols"), 1)
            for i in range(2):
                pe.matmul(bank[1][0:1, i * P:(i + 1) * P], mapf[:, i:i + 1], ident[:, :], start=True, stop=True)
            pe.matmul(bank[1][:, 2 * P:3 * P], mapf[:, 0:1].to_broadcast([P, P]), ident[:, :], start=True, stop=True)\
                .then_inc(sem("map_turned"), 1)

            pe.wait_ge(sem("map_made"), 1)
            pe.wait_ge(sem("bias3_made"), 1)
            pe.wait_ge(sem("experts_in"), 16 * 3 * B)
            pe.wait_ge(sem("slot_read"), B)

            TURN0 = 3
            expert = {}
            earlier = [pe.alloc_register(f"earlier{k}") for k in range(2)]

            def expert_tile(j, u):
                if live(j, NTILE):
                    expert[u] = e = pe.value_load(tmap[0:1, bass.ds(j, 1)], min_val=0, max_val=NE - 1)
                    pe.wait_ge(sem("xgT_made"), j + 1)
                    after(pe, sem("hh_made"), j - 1)
                    gu = bank[u % 2]
                    pe.matmul(gu[:, 0:2 * FF], sel3[:, bass.ds(e, 1)].to_broadcast([3 * NE, P]),
                              bias3[:, 0:2 * FF], start=True, stop=False)
                    pe.matmul(gu[:, 0:2 * FF], xgT[:, u % 2, :],
                              wgu[:, bass.ds(e, 1), :].rearrange("p a n -> p (a n)"), start=False, stop=True)\
                        .then_inc(sem("gu_out"), 1)
                i = j - 2
                if live(i, NTILE):
                    w = u % 2
                    if isinstance(j, int):
                        e = pe.value_load(tmap[0:1, bass.ds(i, 1)], min_val=0, max_val=NE - 1)
                    else:
                        e = bass.RuntimeValue.of_register_unchecked(earlier[k], min_val=0, max_val=NE - 1) if (k := (u - TURN0) % XR) < 2 else expert[(u - 2) % XR]
                    pe.wait_ge(sem("hhT_made"), i + 1)
                    after(pe, sem("y_made"), i - 1)
                    yb = bank[6 + w]
                    pe.matmul(yb[:, 0:C], sel3[:, bass.ds(e, 1)].to_broadcast([3 * NE, P]),
                              bias3[:, 2 * FF:], start=True, stop=False)
                    for c in range(FC):
                        last = pe.matmul(yb[:, 0:C], hhT[:, w, c, :],
                                         wd[:, bass.ds(e, 1), c, :].rearrange("p a n -> p (a n)"),
                                         start=False, stop=(c == FC - 1))
                    last.then_inc(sem("y_out"), 1)
                i = j - 1
                if live(i, NTILE):
                    w = (u - 1) % 2
                    pe.wait_ge(sem("hh_made"), i + 1)
                    after(pe, sem("hhT_made"), i - 1)
                    for c in range(FC):
                        last = pe.transpose(bank[4 + w][:, c * P:(c + 1) * P], hh[:, w, c * P:(c + 1) * P], ident[:, :])
                    last.then_inc(sem("hh_turned"), 1)
                i = j + 2
                if live(i, NTILE):
                    w = (u + 2) % XR
                    pe.wait_ge(sem(f"x_in{w}"), 16 * (i // XR + 1) if isinstance(i, int) else 2 * (i - w) + 16)
                    after(pe, sem("xgT_made"), i - 1)
                    pe.transpose(bank[2 + w % 2][:, 0:P], xg[:, w, 0:C], ident[:, :]).then_inc(sem("x_turned"), 1)
                if not isinstance(j, int) and (u + 1 - TURN0) % XR == 0:
                    for k in range(2):
                        pe.reg_mov(earlier[k], expert[(u - 1 + k) % XR])

            for k in range(2):
                pe.reg_load(earlier[k], tmap[0:1, TURN0 - 2 + k:TURN0 - 1 + k])
            steps(pe, -2, TURN0, 11, XR, NTILE + 1, expert_tile)

        @block.scalar
        def _(act):
            act.wait_ge(sem("cols_made"), 1)

            def embed(s, u):
                b, v = s, u
                if live(b):
                    act.wait_ge(sem("grams_used"), b + 1)
                    after(act, sem("projected"), b - 1)
                    act.activation(gramsT[:, v, 2, 2:S - 1], bank[2 * v + 1][:, 2:S - 1], ACT.Copy)\
                        .then_inc(sem("gramsT_b"), 1)
                b, v = s - 1, 1 - u
                if live(b):
                    act.wait_ge(sem("stats_made"), b + 1)
                    act.activation(sd[:, v, :], mv[:, v, :, 1], ACT.Sqrt, bias=eps[:, :]).then_inc(sem("sd_made"), 1)
                    act.wait_ge(sem("nmr_made"), b + 1)
                    after(act, sem("xs_made"), b - 1)
                    for t in range(TPB):
                        last = act.activation(xi[:, v, t, :],
                                              h_all[:, bass.ds(b * TPB + t, 1), :].rearrange("p a c -> p (a c)"),
                                              ACT.Relu, scale=rstd[:, v, t:t + 1], bias=nmr[:, v, t:t + 1])
                    last.then_inc(sem("xi_made"), 1)
                b = s - 2
                if live(b):
                    act.wait_ge(sem("xs_turned"), b + 1)
                    act.activation(xsT[:, bass.ds(b * S, S)], bank[6][:, 0:S // 2].bitcast(BF16), ACT.Copy)\
                        .then_inc(sem("xsT_made"), 1)

            steps(act, 0, 4, 6, 2, B + 1, embed)

            act.wait_ge(sem("bn_var"), 1)
            act.activation(bn_sd[:, :], muvar[:, 1, :], ACT.Sqrt, bias=eps[:, :]).then_inc(sem("bn_sd"), 1)
            act.wait_ge(sem("bn_made"), 1)

            def att_upper(b, v, q):
                act.wait_ge(sem("scored1"), 4 * b + (q + 1))
                if q == 0:
                    after(act, sem("attended"), b - 1)
                act.activation(att[:, v, 2 * (q // 2) + 1, q % 2].rearrange("p a n -> p (a n)"), bank[2 + q % 2][:, :],
                               ACT.Relu, scale=-1.0, bias=four[:, :]).then_inc(sem("att_made1"), 1)

            def attend(s, u):
                if live(s):
                    att_upper(s, u % 2, 0)
                b, v = s - 3, (u - 3) % 2
                if live(b):
                    act.wait_ge(sem("stats2_made"), b + 1)
                    act.activation(sd[:, v, :], mv[:, v, :, 1], ACT.Sqrt, bias=eps[:, :]).then_inc(sem("sd2_made"), 1)
                b, v = s, u % 2
                if live(b):
                    act.wait_ge(sem("v_out"), b + 1)
                    after(act, sem("v_made"), b - 1)
                    act.activation(vi[:, v].rearrange("p t c -> p (t c)"), bank[5][:, 0:S], ACT.Relu).then_inc(sem("v_read"), 1)
                if live(s):
                    att_upper(s, u % 2, 1)
                b, v, w = s - 3, (u - 3) % 2, (u - 3) % RR
                if live(b):
                    act.wait_ge(sem("nmr2_made"), b + 1)
                    after(act, sem(f"rows_sent{w}"), rows_sent(b, w))
                    for t in range(TPB):
                        last = act.activation(row[:, w, t, 0:C],
                                              h_all[:, bass.ds(b * TPB + t, 1), :].rearrange("p a c -> p (a c)"),
                                              ACT.Identity, scale=rstd[:, v, t:t + 1], bias=nmr[:, v, t:t + 1])
                    last.then_inc(sem("row_made"), 1)
                b, v = s + 1, (u + 1) % 2
                if live(b):
                    act.wait_ge(sem("qk_out"), b + 1)
                    after(act, sem("qk_made"), b - 1)
                    act.activation(qi[:, v, :], bank[4][:, 0:S], ACT.Relu, scale=bn_a[:, 0:1], bias=bn_bh[:, 0:1])
                    act.activation(ki[:, v, :], bank[4][:, S:2 * S], ACT.Relu, scale=bn_a[:, 1:2], bias=bn_bh[:, 1:2])\
                        .then_inc(sem("qk_read"), 1)
                if live(s):
                    att_upper(s, u % 2, 2)
                if live(s):
                    att_upper(s, u % 2, 3)
                b = s - 3
                if live(b):
                    act.wait_ge(sem("x2_turned"), b + 1)
                    after(act, sem("routed"), b)
                    act.activation(x2T[:, :], bank[7][:, 0:S], ACT.Copy).then_inc(sem("x2T_made"), 1)
                b, v = s - 1, (u - 1) % 2
                if live(b):
                    act.wait_ge(sem("attended"), b + 1)
                    act.wait_ge(sem("o_bias_made"), b + 1)
                    after(act, sem("oT_made"), b - 1)
                    act.activation(oi[:, v, :], bank[6][:, 0:S], ACT.Identity, scale=o_scale[:, :], bias=o_bias[:, v:v + 1])\
                        .then_inc(sem("o_read"), 1)

            steps(act, -1, 5, 2, 4, B + 2, attend)

            act.wait_ge(sem("shifted"), 1)
            act.activation(e_all[:, :, :], e_all[:, :, :], ACT.Exp)
            act.activation(e2[:, :], e2[:, :], ACT.Exp).then_inc(sem("exps_made"), 1)

            def expert_tile(j, u):
                if live(j, NTILE):
                    act.wait_ge(sem("gu_out"), j + 1)
                    after(act, sem("hh_made"), j - 1)
                    act.activation(sg[:, u % 2, :], bank[u % 2][:, 0:FF], ACT.Silu).then_inc(sem("silu_made"), 1)
                i, w = j - 1, (u - 1) % 2
                if live(i, NTILE):
                    act.wait_ge(sem("hh_turned"), i + 1)
                    after(act, sem("y_out"), i - 1)
                    act.activation(hhT[:, w].rearrange("p c n -> p (c n)"), bank[4 + w][:, 0:FF], ACT.Copy)\
                        .then_inc(sem("hhT_made"), 1)

            steps(act, 0, 4, 11, XR, NTILE, expert_tile)

            o = out.rearrange("b (t p) c -> p (b t) c", p=P)
            for g in range(NFG):
                act.wait_ge(sem("fin_made"), g + 1)
                act.dma_start(o[:, g * FG:(g + 1) * FG, :], h_all[:, g * FG:(g + 1) * FG, :]).then_inc(sem("out_written"), 16)
            act.wait_ge(sem("out_written"), 16 * NFG)

        @block.vector
        def _(dve):
            chained = [0]

            def chain(ins):
                chained[0] += 1
                ins.then_inc(sem("dve_chain"), 1)
                dve.wait_ge(sem("dve_chain"), chained[0])

            dve.memset(onesb[:, :], 1.0)
            dve.memset(onesf[:, :], 1.0)
            dve.memset(eps[:, :], EPS)
            dve.memset(four[:, :], CAP)
            dve.memset(gramsT[:, :, :, :], 0.0)
            dve.memset(xs[:, :, :, :], 1.0)
            dve.memset(veo[:, :, :, :, :], 0.0)
            dve.memset(row[:, :, :, :], 0.0)
            dve.memset(seen[:, :, :, :], 0.0)
            chain(dve.memset(picks[:, :, :, :], 0.0))
            dve.wait_ge(sem("tok_in"), 48)
            chain(dve.tensor_copy(tok_f[:, :], tok_i[:, :]))

            def push(dst, h, j):
                n = dst.shape[-1]
                t, q = h_t[:, 0:n], h_q[:, 0, 0:n]
                token = tok_f[:, HALO + P + j - n:HALO + P + j]
                chain(dve.scalar_tensor_tensor(out=t, in0=h, scalar=float(VOCAB), in1=token, op0=ALU.mult, op1=ALU.add))
                chain(dve.tensor_scalar(q, t, 1.0 / HASHED, BIG, ALU.mult, ALU.add))
                chain(dve.tensor_scalar(q, q, -BIG, -float(HASHED), ALU.add, ALU.mult))
                chain(dve.tensor_tensor(dst, t, q, ALU.add))

            push(hsh[:, 0, :], tok_f[:, HALO - 2:HALO - 2 + P + 1], 0)
            push(hsh[:, 1, :], hsh[:, 0, :], 1)
            push(hsh[:, 2, 1:], hsh[:, 1, 0:P], 1)
            chain(dve.tensor_scalar(h_q[:, :, 1:], hsh[:, :, 1:], 0.0, float(HASHED), ALU.is_lt, ALU.mult))
            chain(dve.tensor_tensor(hsh[:, :, 1:], hsh[:, :, 1:], h_q[:, :, 1:], ALU.add))
            dve.sem_inc(sem("hashed"), 1)
            dve.wait_ge(sem("ids_turned"), 1)
            dve.tensor_copy(ids[:, :, :].rearrange("p t n -> p n t"),
                            bank[0][:, 0:NG * NT].rearrange("p (n t) -> p n t", n=NG)).then_inc(sem("ids_made"), 1)

            dve.wait_ge(sem("ident_made"), 1)
            dve.tensor_copy(identb[:, :], ident[:, :]).then_inc(sem("identb_made"), 1)
            dve.wait_ge(sem("before_made"), 1)
            dve.tensor_copy(beforeb[:, :], before[:, :])
            dve.wait_ge(sem("iotas"), 4)
            chain(dve.tensor_copy(part_f[:, :], part_i[:, :]))
            chain(dve.tensor_scalar(head_i[:, :], part_i[:, :], 48, None, ALU.bitwise_and))
            for j in range(4):
                dve.tensor_scalar(head[:, j:j + 1], head_i[:, :], 16.0 * j, None, ALU.is_equal)
            chain(dve.tensor_scalar(upper[:, :], part_f[:, :], float(P // 2), None, ALU.is_ge))
            chain(dve.tensor_scalar(o_scale[:, :], upper[:, :], -0.5, 0.25, ALU.mult, ALU.add))

            def split(part0, part1, part2, w, r1, r2):
                chain(dve.tensor_copy(part0, w))
                chain(dve.tensor_tensor(r1, w, part0, ALU.subtract))
                chain(dve.tensor_copy(part1, r1))
                chain(dve.tensor_tensor(r2, r1, part1, ALU.subtract))
                chain(dve.tensor_copy(part2, r2))

            dve.wait_ge(sem("wemb_turned"), 1)
            dve.tensor_copy(wembT[:, :, :].rearrange("p n c -> p (n c)"), bank[1][:, 0:NG * C])
            dve.wait_ge(sem("wattn_turned"), 1)
            dve.tensor_copy(wT[:, :], bank[2][:, 0:3 * C])
            dve.tensor_copy(wprojT[:, :], bank[3][:, 0:C])
            chain(dve.tensor_copy(cols7[:, :], bank[3][:, C:C + 7]))
            split(qkT3[:, 0, :], qkT3[:, 1, :], qkT3[:, 2, :], wT[:, 0:2 * C], rest[:, :], rest2[:, :])
            split(prT3[:, 0, :], prT3[:, 1, :], prT3[:, 2, :], wprojT[:, :], rest[:, 0:C], rest2[:, 0:C])
            split(col3[:, 0, 0:1], col3[:, 0, 1:2], col3[:, 0, 2:3], cols7[:, 6:7], rest_c[:, 0, 0:1], rest_c[:, 0, 1:2])
            dve.sem_inc(sem("bp_split"), 1)
            dve.wait_ge(sem("bp_turned"), 1)
            chain(dve.tensor_copy(bp3[:, :], bank[4][0:3, 0:C // 2].bitcast(BF16)))
            dve.sem_inc(sem("setup_done"), 1)
            dve.sem_inc(sem("cols_made"), 1)
            dve.wait_ge(sem("bias_in"), 48)
            chain(dve.tensor_copy(bias3[0:NE, :], bias_f[:, :]))
            chain(dve.tensor_tensor(bias_r[:, :], bias_f[:, :], bias3[0:NE, :], ALU.subtract))
            chain(dve.tensor_copy(bias_m[:, :], bias_r[:, :]))
            chain(dve.tensor_copy(bias3[NE:2 * NE, :], bias_m[:, :]))
            chain(dve.tensor_tensor(bias_r[:, :], bias_r[:, :], bias_m[:, :], ALU.subtract))
            chain(dve.tensor_copy(bias3[2 * NE:3 * NE, :], bias_r[:, :]))
            for i in range(3):
                chain(dve.tensor_copy(sel3[i * NE:(i + 1) * NE, :], identb[0:NE, 0:NE]))
            dve.sem_inc(sem("bias3_made"), 1)

            dve.wait_ge(sem("projb_in"), 16)

            def embed(s, u):
                b, v = s - 2, u
                if live(b):
                    dve.wait_ge(sem("xi_made"), b + 1)
                    after(dve, sem("xs_turned"), b - 1)
                    dve.tensor_scalar(xs[:, v, :, 0:C], xi[:, v], CAP, None, ALU.min).then_inc(sem("xs_made"), 1)
                b, v = s, u
                if live(b):
                    dve.wait_ge(sem("grams_used"), b + 1)
                    after(dve, sem("projected"), b - 1)
                    dve.tensor_copy(gramsT[:, v, 0, 1:S], bank[2 * v][:, 1:S])
                    dve.tensor_copy(gramsT[:, v, 1, 1:S - 1], bank[2 * v][:, S + 1:2 * S - 1]).then_inc(sem("gramsT_a"), 1)
                b, v = s - 1, 1 - u
                if live(b):
                    dve.wait_ge(sem("projected"), b + 1)
                    hb = h_all[:, bass.ds(b * TPB, TPB), :]
                    dve.tensor_tensor(hb, bank[4 + v][:, 0:S].rearrange("p (t c) -> p t c", c=C),
                                      projb_bc[:, :].rearrange("p (a c) -> p a c", a=1).to_broadcast([P, TPB, C]),
                                      ALU.add).then_inc(sem("h_made"), 1)
                    hold(dve, sem("h_made"), b + 1)
                    for t in range(TPB):
                        last = dve.bn_stats(st[:, v, t, :], h_all[:, bass.ds(b * TPB + t, 1), :].rearrange("p a c -> p (a c)"))
                    last.then_inc(sem("halves_made"), 1)
                    hold(dve, sem("halves_made"), b + 1)
                    for t in range(TPB):
                        last = dve.bn_aggr(mv[:, v, t, :], st[:, v, t, :])
                    last.then_inc(sem("stats_made"), 1)
                    dve.wait_ge(sem("sd_made"), b + 1)
                    dve.reciprocal(rstd[:, v, :], sd[:, v, :]).then_inc(sem("rstd_made"), 1)
                    dve.wait_ge(sem("rstd_made"), b + 1)
                    dve.scalar_tensor_tensor(out=nmr[:, v, :], in0=mv[:, v, :, 0], scalar=-1.0, in1=rstd[:, v, :],
                                             op0=ALU.mult, op1=ALU.mult).then_inc(sem("nmr_made"), 1)

            steps(dve, 0, 4, 6, 2, B + 1, embed)

            dve.wait_ge(sem("xs_turned"), B)
            dve.tensor_scalar(gn[:, :], bank[7][:, 0:C + 1], 1.0 / NTOK, None, ALU.mult).then_inc(sem("mean_made"), 1)
            dve.wait_ge(sem("mean_turned"), 1)
            dve.tensor_copy(mrow[:, :], bank[0][0:1, 0:P]).then_inc(sem("mrow_made"), 1)
            dve.wait_ge(sem("mm_made"), 1)
            dve.tensor_tensor(cov[:, :], gn[:, 0:C], bank[1][:, 0:C], ALU.subtract).then_inc(sem("cov_made"), 1)
            dve.wait_ge(sem("covw"), 1)
            dve.tensor_tensor(wtc[:, :], wT[:, :], bank[2][:, 0:3 * C], ALU.mult).then_inc(sem("wtc_made"), 1)
            dve.wait_ge(sem("muvar_made"), 1)
            dve.tensor_copy(muvar[:, :, :].rearrange("p a g -> p (a g)"), bank[3][:, 0:6]).then_inc(sem("bn_var"), 1)
            dve.wait_ge(sem("bn_sd"), 1)
            chain(dve.reciprocal(bn_r[:, :], bn_sd[:, :]))
            chain(dve.tensor_tensor(bn_a[:, :], bn_r[:, :], cols7[:, 0:3], ALU.mult))
            chain(dve.tensor_tensor(bn_ma[:, :], muvar[:, 0, :], bn_a[:, :], ALU.mult))
            chain(dve.tensor_tensor(bn_b[:, :], cols7[:, 3:6], bn_ma[:, :], ALU.subtract))
            chain(dve.tensor_scalar(bn_bh[:, :], bn_b[:, :], HALF_UP, None, ALU.add))
            dve.sem_inc(sem("bn_made"), 1)
            dve.tensor_scalar(wv[:, :], wqkv[:, 2, :], bn_a[:, 2:3], None, ALU.mult)
            split(col3[:, 1, 0:1], col3[:, 1, 1:2], col3[:, 1, 2:3], bn_bh[:, 2:3], rest_c[:, 1, 0:1], rest_c[:, 1, 1:2])
            dve.sem_inc(sem("wv_made"), 1)
            dve.wait_ge(sem("wv_turned"), 1)
            dve.tensor_copy(bv3[:, :], bank[1][0:3, 0:C // 2].bitcast(BF16))
            split(vT3[:, 0, :], vT3[:, 1, :], vT3[:, 2, :], bank[0][:, 0:C], rest[:, 0:C], rest2[:, 0:C])
            dve.sem_inc(sem("vT_made"), 1)
            dve.wait_ge(sem("wgate_in"), 32)

            def att_lower(b, v, q):
                dve.wait_ge(sem("scored0"), 4 * b + (q + 1))
                if q == 0:
                    after(dve, sem("attended"), b - 1)
                dve.tensor_scalar(att[:, v, 2 * (q // 2), q % 2].rearrange("p a n -> p (a n)"), bank[q % 2][:, :],
                                  CAP, None, ALU.min).then_inc(sem("att_made0"), 1)

            def attend(s, u):
                if live(s):
                    att_lower(s, u % 2, 0)
                b, v = s - 2, (u - 2) % 2
                if live(b):
                    dve.wait_ge(sem("o_read"), b + 1)
                    after(dve, sem("proj_out"), b - 1)
                    dve.tensor_scalar(oT[:, v, :], oi[:, v, :], CAP, None, ALU.min).then_inc(sem("oT_made"), 1)
                b, v = s - 3, (u - 3) % 2
                if live(b):
                    dve.wait_ge(sem("sd2_made"), b + 1)
                    dve.reciprocal(rstd[:, v, :], sd[:, v, :]).then_inc(sem("rstd2_made"), 1)
                    dve.wait_ge(sem("rstd2_made"), b + 1)
                    dve.scalar_tensor_tensor(out=nmr[:, v, :], in0=mv[:, v, :, 0], scalar=-1.0, in1=rstd[:, v, :],
                                             op0=ALU.mult, op1=ALU.mult).then_inc(sem("nmr2_made"), 1)
                if live(s):
                    att_lower(s, u % 2, 1)
                b = s - 5
                if live(b):
                    dve.wait_ge(sem("ranked"), b + 1)
                    after(dve, sem("placed_made"), b)
                    dve.tensor_tensor(place[:, :, :], bank[7][:, TPB * NE:2 * TPB * NE].rearrange("p (t e) -> p t e", e=NE),
                                      region0[:, :].rearrange("p (a e) -> p a e", a=1).to_broadcast([P, TPB, NE]),
                                      ALU.add).then_inc(sem("slot_read"), 1)
                b = s - 4
                if live(b):
                    dve.wait_ge(sem("routed"), b + 1)
                    after(dve, sem("lg_kept"), b)
                    dve.tensor_tensor(lg[:, :, 0:NE],
                                      bank[7][:, 0:TPB * NE].rearrange("p (t e) -> p t e", e=NE),
                                      bgate_bc[:, :].rearrange("p (a e) -> p a e", a=1).to_broadcast([P, TPB, NE]),
                                      ALU.add).then_inc(sem("logits_made"), 1)
                b, v = s - 1, (u - 1) % 2
                if live(b):
                    dve.wait_ge(sem("v_summed"), b + 1)
                    after(dve, sem("o_read"), b - 1)
                    dve.tensor_scalar(o_bias[:, v:v + 1], bank[6][:, S:S + 1], upper[:, 0:1], 0.0625, ALU.mult, ALU.add)\
                        .then_inc(sem("o_bias_made"), 1)
                b = s - 4
                if live(b):
                    hold(dve, sem("logits_made"), b + 1)
                    for t in range(TPB):
                        last = dve.max(lg[:, t, NE:], lg[:, t, 0:NE])
                    last.then_inc(sem("top_made"), 1)
                b, v = s - 5, (u - 5) % 2
                if live(b):
                    dve.wait_ge(sem("slot_read"), b + 1)
                    for k in range(TOPK):
                        last = dve.tensor_tensor(placed[:, :, k, :], place[:, :, :], chosen[:, v, :, k, :], ALU.mult)
                    last.then_inc(sem("placed_made"), 1)
                if live(s):
                    att_lower(s, u % 2, 2)
                b, w = s - 5, (u - 5) % RR
                if live(b):
                    dve.wait_ge(sem("placed_made"), b + 1)
                    after(dve, sem(f"rows_sent{w}"), rows_sent(b, w))
                    with nc.allow_low_precision(reason="one term of a sum isn't zero, an integer below 2^24"):
                        dve.tensor_reduce(slot[:, w, :], placed[:, :, :, :].rearrange("p t k e -> p (t k) e"), AX, ALU.add)\
                            .then_inc(sem("slot_made"), 1)
                b = s - 4
                if live(b):
                    hold(dve, sem("top_made"), b + 1)
                    for t in range(TPB):
                        last = dve.max_index(topi[:, t, :], lg[:, t, NE:], lg[:, t, 0:NE])
                    last.then_inc(sem("topi_made"), 1)
                b, v = s, u % 2
                if live(b):
                    dve.wait_ge(sem("v_read"), b + 1)
                    after(dve, sem("attended"), b - 1)
                    vh = vi[:, v].rearrange("p t (g a d) -> p (t g) a d", a=2, d=16)
                    for par in range(2):
                        dst = veo[:, v, par].rearrange("p t (g a d) -> p (t g) a d", a=2, d=16)
                        last = dve.tensor_scalar(dst[:, :, par, :], vh[:, :, par, :], CAP, None, ALU.min)
                    last.then_inc(sem("v_made"), 1)
                b = s - 2
                if live(b):
                    dve.wait_ge(sem("proj_out"), b + 1)
                    hb = h_all[:, bass.ds(b * TPB, TPB), :]
                    dve.tensor_tensor(hb, bank[5][:, 0:S].rearrange("p (t c) -> p t c", c=C), hb, ALU.add)\
                        .then_inc(sem("h2_made"), 1)
                b, v = s + 1, (u + 1) % 2
                if live(b):
                    dve.wait_ge(sem("qk_read"), b + 1)
                    after(dve, sem("scored1"), 4 * (b - 1))
                    for j in range(4):
                        dve.tensor_scalar(qh[:, v, j, :], qi[:, v, :], CAP, head[:, j:j + 1], ALU.min, ALU.mult)
                    dve.tensor_scalar(kT[:, v, :], ki[:, v, :], CAP, None, ALU.min).then_inc(sem("qk_made"), 1)
                if live(s):
                    att_lower(s, u % 2, 3)
                b, w = s - 4, (u - 4) % RR
                if live(b):
                    dve.wait_ge(sem("topi_made"), b + 1)
                    dve.tensor_copy(topf[:, :, :], topi[:, :, 0:TOPK]).then_inc(sem("topf_made"), 1)
                    dve.tensor_copy(row[:, w, :, C + 1:C + 2], topi[:, :, 0:1])
                b, v = s - 2, (u - 2) % 2
                if live(b):
                    hold(dve, sem("h2_made"), b + 1)
                    for t in range(TPB):
                        last = dve.bn_stats(st[:, v, t, :], h_all[:, bass.ds(b * TPB + t, 1), :].rearrange("p a c -> p (a c)"))
                    last.then_inc(sem("halves2_made"), 1)
                b, v = s - 4, (u - 4) % 2
                if live(b):
                    dve.wait_ge(sem("topf_made"), b + 1)
                    dve.tensor_tensor(chosen[:, v].rearrange("p t k e -> p (t k) e"),
                                      iota_e[:, :].rearrange("p (a e) -> p a e", a=1).to_broadcast([P, TPB * TOPK, NE]),
                                      topf[:, :, :].rearrange("p t (k a) -> p (t k) a", a=1).to_broadcast([P, TPB * TOPK, NE]),
                                      ALU.is_equal).then_inc(sem("chosen_made"), 1)
                b, v = s - 2, (u - 2) % 2
                if live(b):
                    after(dve, sem("row_made"), b - 1)
                    hold(dve, sem("halves2_made"), b + 1)
                    for t in range(TPB):
                        last = dve.bn_aggr(mv[:, v, t, :], st[:, v, t, :])
                    last.then_inc(sem("stats2_made"), 1)
                b, v = s - 4, (u - 4) % 2
                if live(b):
                    dve.wait_ge(sem("chosen_made"), b + 1)
                    after(dve, sem("ranked"), b)
                    dve.tensor_tensor(seen[:, v, 0, :], seen[:, 1 - v, 1, :], picks[:, 1 - v, 1, :], ALU.add)
                    dve.tensor_tensor(picks[:, v], chosen[:, v, :, 0, :], chosen[:, v, :, 1, :], ALU.add)\
                        .then_inc(sem("picked"), 1)
                b, v = s - 4, (u - 4) % 2
                if live(b):
                    dve.wait_ge(sem("picked"), b + 1)
                    dve.tensor_tensor(seen[:, v, 1, :], seen[:, v, 0, :], picks[:, v, 0, :], ALU.add)\
                        .then_inc(sem("picks_made"), 1)
                    dve.tensor_copy(lg_all[:, bass.ds(b * TPB, TPB), :], lg[:, :, :]).then_inc(sem("lg_kept"), 1)

            steps(dve, -1, 5, 2, 4, B + 4, attend)

            v = (B - 1) % 2
            chain(dve.tensor_tensor(total[:, :], seen[:, v, 1, :], picks[:, v, 1, :], ALU.add))
            dve.sem_inc(sem("total_made"), 1)
            dve.tensor_tensor(e2[:, :], lg_all[:, :, NE + 1], lg_all[:, :, NE], ALU.subtract)
            chain(dve.tensor_tensor(e_all[:, :, :], lg_all[:, :, 0:NE], lg_all[:, :, NE:NE + 1].to_broadcast([P, NT, NE]), ALU.subtract))
            dve.sem_inc(sem("shifted"), 1)
            dve.wait_ge(sem("counted"), 1)
            chain(dve.tensor_copy(count[:, :], bank[0][:, 0:NE]))
            chain(dve.tensor_scalar(ntile_i[:, :], count[:, :], P / 2 - 0.5, 1.0 / P, ALU.add, ALU.mult))
            chain(dve.tensor_copy(ntile[:, :], ntile_i[:, :]))
            chain(dve.tensor_tensor_scan(upto_t[:, :], onesf[:, :], ntile[:, :], 0.0, ALU.mult, ALU.add))
            chain(dve.tensor_tensor(prev_t[:, :], upto_t[:, :], ntile[:, :], ALU.subtract))
            chain(dve.scalar_tensor_tensor(out=origin[:, :], in0=prev_t[:, :], scalar=float(P), in1=count[:, :],
                                           op0=ALU.mult, op1=ALU.add))
            chain(dve.scalar_tensor_tensor(out=origin[:, :], in0=region0[:, :], scalar=-float(P), in1=origin[:, :],
                                           op0=ALU.add, op1=ALU.add))
            chain(dve.tensor_scalar(passed[:, :], upto_t[:, :], part_f[:, 0:1], None, ALU.is_le))
            chain(dve.tensor_reduce(mapc[:, 0:1], passed[:, :], AX, ALU.add))
            chain(dve.tensor_scalar(owner[:, :], iota_e[:, :], mapc[:, 0:1], None, ALU.is_equal))
            chain(dve.tensor_tensor(owner[:, :], owner[:, :], origin[:, :], ALU.mult))
            chain(dve.tensor_reduce(mapc[:, 1:2], owner[:, :], AX, ALU.add))
            chain(dve.scalar_tensor_tensor(out=mapf[:, 1:2], in0=part_f[:, :], scalar=-float(P), in1=mapc[:, 1:2],
                                           op0=ALU.mult, op1=ALU.add))
            chain(dve.tensor_scalar(mapf[:, 1:2], mapf[:, 1:2], 0.0, None, ALU.max))
            chain(dve.tensor_scalar(mapf[:, 0:1], mapc[:, 0:1], float(NE - 1), None, ALU.min))
            dve.sem_inc(sem("map_cols"), 1)
            dve.wait_ge(sem("map_turned"), 1)
            dve.tensor_copy(tmap[:, :], bank[1][0:1, 0:2 * P]).then_inc(sem("map_made"), 1)
            chain(dve.tensor_copy(tile_e, bank[1][:, 2 * P:3 * P]))

            def sent(i, u):
                return 16 * (i // XR + 1) if isinstance(i, int) else 2 * (i - u) + 16

            def expert_tile(j, u):
                if isinstance(j, int) and j == 1:
                    dve.wait_ge(sem("exps_made"), 1)
                    chain(dve.tensor_reduce(den[:, :], e_all[:, :, :], AX, ALU.add))
                    chain(dve.reciprocal(w12[:, 0, :], den[:, :]))
                    chain(dve.tensor_tensor(w12[:, 1, :], w12[:, 0, :], e2[:, :], ALU.mult))
                i = j - 1
                if live(i, NTILE):
                    w = (u - 1) % 2
                    dve.wait_ge(sem("silu_made"), i + 1)
                    after(dve, sem("hh_turned"), i - 1)
                    dve.tensor_tensor(hh[:, w, :], sg[:, w, :], bank[w][:, FF:2 * FF], ALU.mult).then_inc(sem("hh_made"), 1)
                i = j - 3
                if live(i, NTILE):
                    w = (u - 3) % YR
                    dve.wait_ge(sem("y_out"), i + 1)
                    q = (u - 3 - YR) % XR
                    after(dve, sem(f"y_sent{q}"), sent(i - YR, q))
                    dve.tensor_copy(yy[:, w, :], bank[6 + w % 2][:, 0:C]).then_inc(sem("y_made"), 1)
                i = j + 1
                if live(i, NTILE):
                    w = (u + 1) % XR
                    dve.wait_ge(sem("x_turned"), i + 1)
                    after(dve, sem("gu_out"), i - 1)
                    dve.tensor_copy(xgT[:, w % 2, :], bank[2 + w % 2][:, 0:P]).then_inc(sem("xgT_made"), 1)
                    after(dve, sem(f"y_sent{w}"), sent(i - XR, w))
                    dve.scalar_tensor_tensor(out=pair_i[:, w, :], in0=xg[:, w, C + 1:C + 2], scalar=tile_e[:, bass.ds(i, 1)],
                                             in1=xg[:, w, C:C + 1], op0=ALU.not_equal, op1=ALU.add)\
                        .then_inc(sem("pair_kept"), 1)

            steps(dve, -1, 7, 11, XR, NTILE + 2, expert_tile)

            for g in range(NFG):
                dve.wait_ge(sem(f"fin_in{g}"), 16)
                for k in range(TOPK):
                    for t in range(FG):
                        tt = g * FG + t
                        last = dve.scalar_tensor_tensor(out=h_all[:, tt, :], in0=y_fin[:, g, t, k, :],
                                                        scalar=w12[:, k, tt:tt + 1], in1=h_all[:, tt, :],
                                                        op0=ALU.mult, op1=ALU.add)
                    last.then_inc(sem("fin_part"), 1)
                    dve.wait_ge(sem("fin_part"), TOPK * g + k + 1)
                dve.sem_inc(sem("fin_made"), 1)


_INS = ['x', 'L0_tok_emb_2', 'L0_tok_emb_3', 'L0_tok_emb_4', 'L0_tok_proj_w', 'L0_tok_proj_b', 'L0_attn_Wqkv',
        'L0_attn_gamma', 'L0_attn_beta', 'L0_attn_Wproj', 'L0_attn_bproj', 'L0_ffn_Wgate', 'L0_ffn_bgate',
        'L0_ffn_Wg', 'L0_ffn_bg', 'L0_ffn_Wu', 'L0_ffn_bu', 'L0_ffn_Wd', 'L0_ffn_bd']


def kernel(**inputs):
    import numpy as _np
    import concourse.bacc as _bacc
    from concourse import mybir as _mybir
    from concourse.bass_utils import run_bass_kernel_spmd as _run

    nc = _bacc.Bacc("TRN2", target_bir_lowering=False, num_devices=1)
    arrays, aps = {}, {}
    for name in _INS:
        a = _np.ascontiguousarray(inputs[name])
        arrays[f"in_{name}"] = a
        aps[name] = nc.dram_tensor(f"in_{name}", a.shape, _mybir.dt.from_np(a.dtype), kind="ExternalInput").ap()
    out = nc.dram_tensor("out_h", (B, S, C), F32, kind="ExternalOutput").ap()
    a = [aps[n] for n in _INS]
    build(nc, a[0], a[1:4], *a[4:], out)
    r = _run(nc, [arrays], core_ids=[0])
    return r.results[0]["out_h"]
```

```python
from contextlib import ExitStack

import concourse.bass as bass
from concourse import mybir

F32 = mybir.dt.float32
BF16 = mybir.dt.bfloat16
I16 = mybir.dt.int16
I32 = mybir.dt.int32
U32 = mybir.dt.uint32
ALU = mybir.AluOpType
ACT = mybir.ActivationFunctionType
AX = mybir.AxisListType.X

P = 128
B, S = 16, 256
NTOK = B * S
TPB = S // P
NT = NTOK // P
C = 128
NG = 3
VOCAB = 64
HASHED = 25000
HALO = 2
EPS = 1e-5
CAP = 4.0
HALF_UP = 2.0 ** -22
NE = 32
TOPK = 2
EPR = NE // B
FF = 256
FC = FF // P
REGION = NTOK + P
ROW = C + 4
NPAIR = TOPK * NTOK
NTILE = (NPAIR + NE * (P - 1)) // P
NO_PAIR = 2.0 ** 30
ROUNDS = 4
RR = 4
BIG = 1.5 * 2.0 ** 23
FG = 4
NFG = NT // FG
POOL_GROUPS = (2, 5)
EARLY = (4, 7)
FILL = (2, 4, 8, 7, 12)
KEEP = 1


def live(b, n=B):
    return not isinstance(b, int) or 0 <= b < n


def last_gather(s):
    return isinstance(s, int) and s == B - 1


def upto(b, n=B):
    return min(b, n) if isinstance(b, int) else b


def after(eng, sem, count):
    if not isinstance(count, int) or count > 0:
        eng.wait_ge(sem, count)


def hold(eng, sem, count):
    if not isinstance(count, int) or count > 0:
        eng.wait_ge(sem, count)
        eng.nop(nofuse=True)


def steps(eng, first, steady, pairs, unroll, last, step):
    for b in range(first, steady):
        step(b, b % unroll)
    with eng.Fori(0, pairs) as i:
        for u in range(unroll):
            step(unroll * i + (steady + u), (steady + u) % unroll)
    for b in range(steady + pairs * unroll, last + 1):
        step(b, b % unroll)


def build(nc, x, emb, proj_w, proj_b, Wqkv, gamma, beta, Wproj, bproj, Wgate, bgate,
          Wg, bg, Wu, bu, Wd, bd, out):
    ctx = ExitStack()
    with ctx:
        def sb(name, shape, dt):
            return ctx.enter_context(nc.sbuf_tensor(name, shape, dt))

        sems = {}

        def sem(name):
            if name not in sems:
                sems[name] = ctx.enter_context(nc.semaphore(name))
            return sems[name]

        regions = nc.dram_tensor("regions", [NE * REGION, ROW], F32, kind="Internal").ap()
        results = nc.dram_tensor("results", [NPAIR, C], F32, kind="Internal").ap()

        ident = sb("ident", [P, P], F32)
        identb = sb("identb", [P, P], BF16)
        before = sb("before", [P, P], F32)
        beforeb = sb("beforeb", [P, P], BF16)
        onesb = sb("onesb", [P, P], BF16)
        onesf = sb("onesf", [P, NE], F32)
        iota_e = sb("iota_e", [P, NE], F32)
        region0 = sb("region0", [P, NE], F32)
        region_hi = sb("region_hi", [P, NE], BF16)
        region_lo = sb("region_lo", [P, NE], BF16)
        part_i = sb("part_i", [P, 1], I32)
        part_f = sb("part_f", [P, 1], F32)
        head_i = sb("head_i", [P, 1], I32)
        head = sb("head", [P, 4], F32)
        upper = sb("upper", [P, 1], F32)
        o_scale = sb("o_scale", [P, 1], F32)
        eps = sb("eps", [P, 1], F32)
        four = sb("four", [P, 1], F32)
        number = sb("number", [P, NT], F32)
        pad_row = sb("pad_row", [P, ROW], F32)
        projb_bc = sb("projb_bc", [P, C], F32)
        bgate_bc = sb("bgate_bc", [P, NE], F32)
        wgate = sb("wgate", [P, NE], F32)
        wqkv = sb("wqkv", [P, 3, C], F32)
        wproj = sb("wproj", [P, C], F32)
        wemb = sb("wemb", [P, NG * C], F32)
        rows7 = sb("rows7", [7, C], F32)
        cols7 = sb("cols7", [P, 7], F32)
        wembT = sb("wembT", [P, NG, C], F32)
        wT = sb("wT", [P, 3 * C], F32)
        wprojT = sb("wprojT", [P, C], F32)
        qkT3 = sb("qkT3", [P, 3, 2 * C], BF16)
        vT3 = sb("vT3", [P, 3, C], BF16)
        prT3 = sb("prT3", [P, 3, C], BF16)
        rest = sb("rest", [P, 2 * C], F32)
        rest2 = sb("rest2", [P, 2 * C], F32)
        col3 = sb("col3", [P, 2, 3], BF16)
        rest_c = sb("rest_c", [P, 2, 2], F32)
        bp3 = sb("bp3", [3, C], BF16)
        bv3 = sb("bv3", [3, C], BF16)

        tok_i = sb("tok_i", [NT, HALO + P + 2], I32)
        tok_f = sb("tok_f", [NT, HALO + P + 2], F32)
        hsh = sb("hsh", [NT, NG, P + 1], F32)
        h_t = sb("h_t", [NT, P + 1], F32)
        h_q = sb("h_q", [NT, NG, P + 1], F32)
        ids = sb("ids", [P, NT, NG], U32)
        id_ring = sb("id_ring", [P, 2, TPB * NG], U32)

        grams_mem = sb("grams_mem", [P, 2 * TPB * NG * C], F32)
        grams = grams_mem[:, :].rearrange("p (v t n c) -> p v t n c", v=2, t=TPB, n=NG)
        gramsT_mem = sb("gramsT_mem", [P, 2 * NG * S], F32)
        gramsT = gramsT_mem[:, :].rearrange("p (v n s) -> p v n s", v=2, n=NG)
        h_all = sb("h_all", [P, NT, C], F32)
        st = sb("st", [P, 2, TPB, 6], F32)
        mv = sb("mv", [P, 2, TPB, 2], F32)
        sd = sb("sd", [P, 2, TPB], F32)
        rstd = sb("rstd", [P, 2, TPB], F32)
        nmr = sb("nmr", [P, 2, TPB], F32)
        xi = sb("xi", [P, 2, TPB, C], I16)
        xs = sb("xs", [P, 2, TPB, C + 1], BF16)
        xsT = sb("xsT", [P, NTOK], BF16)

        gn = sb("gn", [P, C + 1], F32)
        mrow = sb("mrow", [1, C], F32)
        cov = sb("cov", [P, C], F32)
        wtc = sb("wtc", [P, 3 * C], F32)
        muvar = sb("muvar", [P, 2, 3], F32)
        bn_sd = sb("bn_sd", [P, 3], F32)
        bn_r = sb("bn_r", [P, 3], F32)
        bn_a = sb("bn_a", [P, 3], F32)
        bn_ma = sb("bn_ma", [P, 3], F32)
        bn_b = sb("bn_b", [P, 3], F32)
        bn_bh = sb("bn_bh", [P, 3], F32)
        wv = sb("wv", [P, C], F32)

        qi = sb("qi", [P, 2, S], I16)
        ki = sb("ki", [P, 2, S], I16)
        vi = sb("vi", [P, 2, TPB, C], I16)
        qh = gramsT_mem[:, 0:4 * S].bitcast(BF16).rearrange("p (v j s) -> p v j s", v=2, j=4)
        kT = sb("kT", [P, 2, S], BF16)
        veo = sb("veo", [P, 2, 2, TPB, C], BF16)
        att_mem = sb("att_mem", [P, 2 * ROUNDS * 4 * S], BF16)
        att = att_mem[:, :].rearrange("p (v r i a n) -> p v r i a n", v=2, r=ROUNDS, i=2, a=2)
        o_bias = sb("o_bias", [P, 2], F32)
        oi = sb("oi", [P, 2, S], I16)
        oT = sb("oT", [P, 2, S], BF16)
        row_mem = sb("row_mem", [P, RR * TPB * ROW], F32)
        row = row_mem[:, :].rearrange("p (v t c) -> p v t c", v=RR, t=TPB)
        x2T = sb("x2T", [P, S], F32)
        lg = sb("lg", [P, TPB, NE + 8], F32)
        lg_all = sb("lg_all", [P, NT, NE + 8], F32)
        topi = sb("topi", [P, TPB, 8], U32)
        topf = sb("topf", [P, TPB, TOPK], F32)
        chosen = sb("chosen", [P, 2, TPB, TOPK, NE], F32)
        picks = sb("picks", [P, 2, TPB, NE], BF16)
        seen = sb("seen", [P, 2, TPB, NE], BF16)
        placed = sb("placed", [P, TPB, TOPK, NE], F32)
        slot = sb("slot", [P, RR, TPB * TOPK], U32)

        GU = 2 * FF + 2 * FC
        wgu_mem = sb("wgu_mem", [P, NE * GU], F32)
        wgu = wgu_mem[:, :].rearrange("p (e n) -> p e n", n=GU)
        wd = sb("wd", [P, NE, FC, C], F32)
        bias_f = sb("bias_f", [NE, 2 * FF + C], F32)
        bias3 = sb("bias3", [3 * NE, C], BF16)
        sel3 = sb("sel3", [3 * NE, NE], BF16)
        total = sb("total", [P, NE], BF16)
        count = sb("count", [P, NE], F32)
        ntile_i = sb("ntile_i", [P, NE], I16)
        ntile = sb("ntile", [P, NE], F32)
        upto_t = sb("upto_t", [P, NE], F32)
        prev_t = sb("prev_t", [P, NE], F32)
        origin = sb("origin", [P, NE], F32)
        passed = sb("passed", [P, NE], F32)
        owner = sb("owner", [P, NE], F32)
        mapc = sb("mapc", [P, 2], F32)
        mapf = sb("mapf", [P, 2], F32)
        tmap = sb("tmap", [1, 2 * P], I32)
        den = sb("den", [P, NT], F32)
        e2 = sb("e2", [P, NT], F32)
        w12 = sb("w12", [P, TOPK, NT], F32)
        XR = 8
        YR = 4
        WR = 4
        pair_i = sb("pair_i", [P, XR, 1], U32)
        xg = grams_mem[:, 0:XR * ROW].rearrange("p (r c) -> p r c", r=XR)
        tile_e = grams_mem[:, XR * ROW:XR * ROW + P]
        yy = row_mem[:, 0:YR * C].rearrange("p (r c) -> p r c", r=YR)
        xgT = row_mem[:, YR * C:YR * C + 2 * P].rearrange("p (r c) -> p r c", r=2)
        sg, hhT = [gramsT_mem[:, i * 2 * FF:(i + 1) * 2 * FF] for i in range(2)]
        sg = sg.rearrange("p (r n) -> p r n", r=2)
        hhT = hhT.rearrange("p (r n) -> p r n", r=2)
        y_fin = wgu_mem[:, 0:NPAIR * C // P].rearrange("p (g t k c) -> p g t k c", g=NFG, k=TOPK, t=FG)
        late = att_mem[:, :].bitcast(F32)
        e_all = late[:, 0:NT * NE].rearrange("p (t e) -> p t e", e=NE)
        spare = NT * NE
        wr = late[:, spare:spare + WR * GU].rearrange("p (r n) -> p r n", r=WR)
        bias_r = late[0:NE, spare:spare + C]
        bias_m = att_mem[0:NE, 2 * (spare + C):2 * (spare + C) + C]

        bank = [ctx.enter_context(nc.psum_tensor(f"bank{i}", [P, 512], F32)) for i in range(8)]

        def rows_sent(b, w):
            return 16 * TPB * TOPK * (b - w) // RR if isinstance(b, int) else 16 * TPB * TOPK // RR * (b - w)

        block = ctx.enter_context(nc.Block())

        @block.sync
        def _(sp):
            xr = x.rearrange("b (t p) -> (b t) p", p=P)
            sp.wait_ge(sem("tok_clear"), 1)
            sp.dma_start(tok_i[:, HALO:HALO + P], xr).then_inc(sem("tok_in"), 16)
            sp.dma_start(tok_i[1:NT, 0:HALO], xr[0:NT - 1, P - HALO:P]).then_inc(sem("tok_in"), 16)
            sp.dma_start(tok_i[0:NT - 1, HALO + P:], xr[1:NT, 0:2]).then_inc(sem("tok_in"), 16)
            sp.dma_start(wemb[:, :], proj_w).then_inc(sem("wemb_in"), 16)
            sp.dma_start(projb_bc[:, :], proj_b.rearrange("(a n) -> a n", a=1).to_broadcast([P, C]))\
                .then_inc(sem("projb_in"), 16)
            sp.dma_start(wqkv[:, :, :], Wqkv.rearrange("(g p) c -> p g c", p=P)).then_inc(sem("wattn_in"), 16)
            sp.dma_start(wproj[:, :], Wproj).then_inc(sem("wattn_in"), 16)
            sp.dma_start(rows7[0:3, :], gamma.rearrange("(g p) -> g p", p=P)).then_inc(sem("wattn_in"), 16)
            sp.dma_start(rows7[3:6, :], beta.rearrange("(g p) -> g p", p=P)).then_inc(sem("wattn_in"), 16)
            sp.dma_start(rows7[6:7, :], bproj.rearrange("(a p) -> a p", a=1)).then_inc(sem("wattn_in"), 16)
            sp.dma_start(wgate[:, :], Wgate).then_inc(sem("wgate_in"), 16)
            sp.dma_start(bgate_bc[:, :], bgate.rearrange("(a n) -> a n", a=1).to_broadcast([P, NE]))\
                .then_inc(sem("wgate_in"), 16)
            sp.dma_start(bias_f[:, 0:FF], bg).then_inc(sem("bias_in"), 16)
            sp.dma_start(bias_f[:, FF:2 * FF], bu).then_inc(sem("bias_in"), 16)
            sp.dma_start(bias_f[:, 2 * FF:], bd).then_inc(sem("bias_in"), 16)
            with sp.Fori(0, B) as b:
                sp.wait_ge(sem("grams_used"), b + 1)
                e = b * EPR
                sp.dma_start(wgu[:, bass.ds(e, EPR), 0:FF], Wg[bass.ds(e, EPR)].rearrange("e h i -> h e i"))\
                    .then_inc(sem("experts_in"), 16)
                sp.dma_start(wgu[:, bass.ds(e, EPR), FF:2 * FF], Wu[bass.ds(e, EPR)].rearrange("e h i -> h e i"))\
                    .then_inc(sem("experts_in"), 16)
                sp.dma_start(wd[:, bass.ds(e, EPR)], Wd[bass.ds(e, EPR)].rearrange("e (c p) h -> p e c h", p=P))\
                    .then_inc(sem("experts_in"), 16)
            sp.wait_ge(sem("pad_made"), 1)
            sp.dma_start(regions.rearrange("(e r) c -> r e c", e=NE)[0:P],
                         pad_row[:, :].rearrange("p (a c) -> p a c", a=1).to_broadcast([P, NE, ROW]))\
                .then_inc(sem("pads_in"), 16)

            sp.wait_ge(sem("map_made"), 1)
            for w in range(RR):
                sp.wait_ge(sem(f"rows_sent{w}"), 16 * TPB * TOPK * B // RR)

            def load_tile(j, u):
                start = sp.value_load(tmap[0:1, bass.ds(P + j, 1)], min_val=0, max_val=NE * REGION - P)
                after(sp, sem("pair_kept"), j - XR + 1)
                sp.dma_start(xg[:, u, :], regions[bass.ds(start, P), :]).then_inc(sem(f"x_in{u}"), 16)

            steps(sp, 0, 8, 10, XR, NTILE - 1, load_tile)

            for u in range(XR):
                sp.wait_ge(sem(f"y_sent{u}"), 16 * len(range(u, NTILE, XR)))
            res = results.rearrange("(t p k) c -> p t k c", k=TOPK, p=P)
            for g in range(NFG):
                sp.dma_start(y_fin[:, g], res[:, g * FG:(g + 1) * FG]).then_inc(sem(f"fin_in{g}"), 16)

        @block.gpsimd
        def _(pool):
            pool.memset(tok_i[:, :], 0).then_inc(sem("tok_clear"), 1)
            pool.memset(ident[:, :], 0.0).then_inc(sem("pool_c"), 1)
            pool.memset(before[:, :], 0.0).then_inc(sem("pool_c"), 1)
            pool.memset(pad_row[:, :], 0.0).then_inc(sem("pool_c"), 1)
            pool.wait_ge(sem("pool_c"), 3)
            pool.affine_select(out=ident[:, :], in_=ident[:, :], compare_op=ALU.not_equal, fill=1.0,
                               base=0, pattern=[[-1, P]], channel_multiplier=1).then_inc(sem("ident_made"), 1)
            pool.affine_select(out=before[:, :], in_=before[:, :], compare_op=ALU.is_ge, fill=1.0,
                               base=0, pattern=[[-1, P]], channel_multiplier=1).then_inc(sem("before_made"), 1)
            pool.memset(pad_row[:, C:C + 1], NO_PAIR).then_inc(sem("pad_made"), 1)
            pool.iota(part_i[:, :], pattern=[[0, 1]], base=0, channel_multiplier=1).then_inc(sem("iotas"), 1)
            pool.iota(number[:, :], pattern=[[TOPK * P, NT]], base=0, channel_multiplier=TOPK,
                      allow_small_or_imprecise_dtypes=True).then_inc(sem("iotas"), 1)
            pool.iota(iota_e[:, :], pattern=[[1, NE]], base=0, channel_multiplier=0,
                      allow_small_or_imprecise_dtypes=True).then_inc(sem("iotas"), 1)
            pool.iota(region0[:, :], pattern=[[REGION, NE]], base=P, channel_multiplier=0,
                      allow_small_or_imprecise_dtypes=True).then_inc(sem("iotas"), 1)

            pool.wait_ge(sem("ids_made"), 1)

            def gather(b, u):
                hold(pool, sem(f"grams_in{u}"), 16 * TPB * NG * ((b - u) // 2) if isinstance(b, int)
                      else 8 * TPB * NG * (b - u))
                pool.tensor_copy(id_ring[:, u, :].rearrange("p (t n) -> p t n", n=NG),
                                 ids[:, bass.ds(b * TPB, TPB), :]).then_inc(sem("ids_staged"), 1)
                hold(pool, sem("ids_staged"), b + 1)
                hold(pool, sem("grams_used"), b - 1)
                for t in range(TPB):
                    for n in range(NG):
                        k = t * NG + n
                        pool.indirect_dma_start(grams[:, u, t, n, :], None, emb[n],
                                                bass.IndirectOffsetOnAxis(ap=id_ring[:, u, k:k + 1], axis=0))\
                            .then_inc(sem(f"grams_in{u}"), 16)

            steps(pool, 0, 2, 7, 2, B - 1, gather)

            pool.wait_ge(sem("pads_in"), 16)

            def dispatch(s, u):
                b, w = s - 3, (u - 3) % RR
                if live(b):
                    hold(pool, sem(f"rows_sent{w}"), rows_sent(b, w))
                    pool.tensor_copy(row[:, w, :, C:C + 1],
                                     number[:, bass.ds(b * TPB, TPB)].rearrange("p (t a) -> p t a", a=1))\
                        .then_inc(sem("numbered"), 1)
                b, v = s, u % 2
                if live(b):
                    hold(pool, sem("v_read"), b + 1)
                    hold(pool, sem("attended"), b - 1)
                    vh = vi[:, v].rearrange("p t (g a d) -> p (t g) a d", a=2, d=16)
                    for par in range(2):
                        dst = veo[:, v, par].rearrange("p t (g a d) -> p (t g) a d", a=2, d=16)
                        last = pool.tensor_scalar(dst[:, :, par, :], vh[:, :, par, :], CAP, None, ALU.min)
                    last.then_inc(sem("v_made"), 1)
                b = s - 4
                if live(b):
                    if live(s):
                        hold(pool, sem("top_made"), b + 1)
                        pool.tensor_copy(lg_all[:, bass.ds(b * TPB, TPB), :], lg[:, :, :]).then_inc(sem("lg_kept"), 1)
                b, w = s - 5, (u - 5) % RR
                if live(b):
                    hold(pool, sem("numbered"), b + 1)
                    hold(pool, sem("slot_made"), b + 1)
                    for i in range(TPB * TOPK):
                        pool.indirect_dma_start(
                            regions, bass.IndirectOffsetOnAxis(ap=slot[:, w, i:i + 1], axis=0),
                            row[:, w, i // TOPK, :], None).then_inc(sem(f"rows_sent{w}"), 16)

            steps(pool, 0, 7, 2, 4, B + 4, dispatch)

            def collect(j, u):
                hold(pool, sem("y_made"), j + 1)
                pool.indirect_dma_start(
                    results, bass.IndirectOffsetOnAxis(ap=pair_i[:, u, :], axis=0), yy[:, u % YR, :], None,
                    bounds_check=NPAIR - 1, oob_is_err=False).then_inc(sem(f"y_sent{u}"), 16)

            steps(pool, 0, 4, 11, XR, NTILE - 1, collect)

            pool.wait_ge(sem("weights_made"), 1)
            done = 0
            for g in POOL_GROUPS:
                pool.wait_ge(sem(f"fin_in{g}"), 16)
                hg = h_all[:, g * FG:(g + 1) * FG, :]
                for k in range(TOPK):
                    w = w12[:, k, g * FG:(g + 1) * FG].rearrange("p (t a) -> p t a", a=1).to_broadcast([P, FG, C])
                    pool.tensor_tensor(y_fin[:, g, :, k, :], y_fin[:, g, :, k, :], w, ALU.mult)\
                        .then_inc(sem("fin_made_pool"), 1)
                    pool.wait_ge(sem("fin_made_pool"), done + 1)
                    pool.tensor_tensor(hg, hg, y_fin[:, g, :, k, :], ALU.add).then_inc(sem("fin_made_pool"), 1)
                    done += 2
                    if k < TOPK - 1:
                        pool.wait_ge(sem("fin_made_pool"), done)

        @block.tensor
        def _(pe):
            pe.wait_ge(sem("ident_made"), 1)
            pe.wait_ge(sem("hashed"), 1)
            for n in range(NG):
                last = pe.transpose(bank[0][:, n * NT:(n + 1) * NT], hsh[:, n, 1:], ident[0:NT, 0:NT])
            last.then_inc(sem("ids_turned"), 1)
            pe.wait_ge(sem("wemb_in"), 16)
            for n in range(NG):
                last = pe.transpose(bank[1][:, n * C:(n + 1) * C], wemb[:, n * C:(n + 1) * C], ident[:, :])
            last.then_inc(sem("wemb_turned"), 1)
            pe.wait_ge(sem("wattn_in"), 80)
            for g in range(3):
                pe.transpose(bank[2][:, g * C:(g + 1) * C], wqkv[:, g, :], ident[:, :])
            pe.transpose(bank[3][:, 0:C], wproj[:, :], ident[:, :])
            pe.transpose(bank[3][:, C:C + 7], rows7[:, :], ident[0:7, 0:7]).then_inc(sem("wattn_turned"), 1)
            pe.wait_ge(sem("identb_made"), 1)
            pe.wait_ge(sem("bp_split"), 1)
            pe.transpose(bank[5][0:3, 0:C // 2].bitcast(BF16), col3[:, 0, :], identb[:, :]).then_inc(sem("bp_turned"), 1)
            pe.wait_ge(sem("bias_in"), 48)
            for c in range(2 * FC):
                last = pe.transpose(bank[4][:, P + c * NE:P + (c + 1) * NE], bias_f[:, c * P:(c + 1) * P], ident[0:NE, 0:NE])
            last.then_inc(sem("bias_turned"), 1)
            pe.wait_ge(sem("setup_done"), 1)

            def keep_clock(n, to=5):
                for _ in range(n):
                    pe.matmul(bank[to][:, :], onesb[:, :], xsT[:, 0:512], start=True, stop=True)

            def turn(s, u):
                b, v = s, u
                if live(b):
                    pe.wait_ge(sem(f"grams_in{v}"), 8 * TPB * NG * (b - v) + 16 * TPB * NG)
                    after(pe, sem("gramsT_a"), b - 1)
                    after(pe, sem("gramsT_b"), b - 1)
                    for n in range(NG):
                        for t in range(TPB):
                            dst = bank[2 * v + n // 2][:, (n % 2) * S + t * P:(n % 2) * S + (t + 1) * P]
                            last = pe.transpose(dst, grams[:, v, t, n, :], ident[:, :])
                    last.then_inc(sem("grams_used"), 1)

            def embed(s, u):
                if not last_gather(s):
                    turn(s, u)
                b, v = s - 1, 1 - u
                if live(b):
                    pe.wait_ge(sem("gramsT_a"), b + 1)
                    pe.wait_ge(sem("gramsT_b"), b + 1)
                    after(pe, sem("h_made"), b - 1)
                    for t in range(TPB):
                        for n in range(NG):
                            last = pe.matmul(bank[4 + v][:, t * C:(t + 1) * C], gramsT[:, v, n, t * P:(t + 1) * P],
                                             wembT[:, n, :], start=(n == 0), stop=(n == NG - 1))
                    last.then_inc(sem("projected"), 1)
                    if isinstance(b, int) and b == B - 1:
                        keep_clock(EARLY[1], to=0)
                b, v = s - 2, u
                if live(b):
                    pe.wait_ge(sem("xs_made"), b + 1)
                    after(pe, sem("xsT_made"), b)
                    for t in range(TPB):
                        pe.transpose(bank[6][:, t * C // 2:(t + 1) * C // 2].bitcast(BF16), xs[:, v, t, 0:C], identb[:, :])
                    for t in range(TPB):
                        last = pe.matmul(bank[7][:, 0:C + 1], xs[:, v, t, 0:C], xs[:, v, t, :],
                                         start=(isinstance(b, int) and b == 0 and t == 0),
                                         stop=(isinstance(b, int) and b == B - 1 and t == TPB - 1))
                    last.then_inc(sem("xs_turned"), 1)
                if last_gather(s):
                    turn(s, u)
                    keep_clock(EARLY[0], to=0)

            steps(pe, 0, 4, 5, 2, B + 1, embed)

            pe.wait_ge(sem("mean_made"), 1)
            pe.transpose(bank[0][0:1, 0:P], gn[:, C:C + 1], ident[:, :]).then_inc(sem("mean_turned"), 1)
            keep_clock(FILL[0])
            pe.wait_ge(sem("mrow_made"), 1)
            pe.matmul(bank[1][:, 0:C], mrow[:, :], mrow[:, :], start=True, stop=True).then_inc(sem("mm_made"), 1)
            for g in range(3):
                last = pe.matmul(bank[3][:, g:g + 1], wT[:, g * C:(g + 1) * C], gn[:, C:C + 1], start=True, stop=True)
            pe.wait_ge(sem("cov_made"), 1)
            pe.matmul(bank[2][:, 0:3 * C], cov[:, :], wT[:, :], start=True, stop=True).then_inc(sem("covw"), 1)
            keep_clock(FILL[1])
            pe.wait_ge(sem("wtc_made"), 1)
            for g in range(3):
                last = pe.matmul(bank[3][:, 3 + g:4 + g], wtc[:, g * C:(g + 1) * C], onesf[:, 0:1], start=True, stop=True)
            last.then_inc(sem("muvar_made"), 1)
            def value_weights():
                keep_clock(FILL[2])
                pe.wait_ge(sem("wv_made"), 1)
                pe.transpose(bank[0][:, 0:C], wv[:, :], ident[:, :])
                pe.transpose(bank[1][0:3, 0:C // 2].bitcast(BF16), col3[:, 1, :], identb[:, :]).then_inc(sem("wv_turned"), 1)

                keep_clock(FILL[3])
                pe.wait_ge(sem("vT_made"), 1)

            def scores(b, v, q):
                c, i = q // 2, q % 2
                if q == 0:
                    pe.wait_ge(sem("qk_made"), b + 1)
                for half in range(2):
                    after(pe, sem(f"att_made{half}"), 4 * b + (q - 1))
                    g = half * (P // 2)
                    for par in range(2):
                        last = pe.matmul(bank[2 * half + i][:, par * S:(par + 1) * S],
                                         kT[g:g + P // 2, v, c * P:(c + 1) * P], qh[g:g + P // 2, v, 2 * i + par, :],
                                         start=True, stop=True)
                    last.then_inc(sem(f"scored{half}"), 1)

            def attend(s, u):
                if live(s):
                    scores(s, u % 2, 0)
                b = s - 4
                if live(b):
                    pe.wait_ge(sem("x2T_made"), b + 1)
                    for t in range(TPB):
                        last = pe.matmul(bank[7][:, t * NE:(t + 1) * NE], x2T[:, t * P:(t + 1) * P], wgate[:, :],
                                         start=True, stop=True)
                    last.then_inc(sem("routed"), 1)
                b, v = s - 1, (u - 1) % 2
                if live(b):
                    pe.wait_ge(sem("v_made"), b + 1)
                    after(pe, sem("o_read"), b)
                    for i, (par, c) in enumerate([(0, 0), (0, 1), (1, 0), (1, 1)]):
                        last = pe.matmul(bank[6][:, S:S + 1], veo[:, v, par, c, :], onesb[:, 0:1], start=(i == 0), stop=(i == 3))
                    last.then_inc(sem("v_summed"), 1)
                if live(s):
                    pe.wait_ge(sem("qk_read"), s + 1)
                    keep_clock(KEEP, to=4)
                    scores(s, u % 2, 1)
                b = s + 1
                if live(b):
                    after(pe, sem("qk_read"), b)
                    for g in range(2):
                        for part in range(3):
                            last = pe.matmul(bank[4][:, g * S:(g + 1) * S], qkT3[:, part, g * C:(g + 1) * C],
                                             xsT[:, bass.ds(b * S, S)], start=(part == 0), stop=(part == 2))
                    last.then_inc(sem("qk_out"), 1)
                b, v = s - 5, (u - 5) % 2
                if live(b):
                    pe.wait_ge(sem("picks_made"), b + 1)
                    ranks = bank[7][:, TPB * NE:2 * TPB * NE]
                    pe.matmul(ranks, beforeb[:, :], picks[:, v].rearrange("p t e -> p (t e)"), start=True, stop=False)
                    pe.matmul(ranks, onesb[:, :], seen[:, v].rearrange("p t e -> p (t e)"), start=False, stop=False)
                    for i, first in enumerate((region_hi, region_lo)):
                        last = pe.matmul(ranks.rearrange("p (t e) -> p t e", e=NE), onesb[0:1, :],
                                         first[0:1, :].rearrange("p (a e) -> p a e", a=1).to_broadcast([1, TPB, NE]),
                                         start=False, stop=(i == 1))
                    last.then_inc(sem("ranked"), 1)
                if live(s):
                    scores(s, u % 2, 2)
                b, v = s - 2, (u - 2) % 2
                if live(b):
                    pe.wait_ge(sem("oT_made"), b + 1)
                    pe.wait_ge(sem("v_read"), upto(b + 3))
                    for t in range(TPB):
                        for part in range(3):
                            pe.matmul(bank[5][:, t * C:(t + 1) * C], oT[:, v, t * P:(t + 1) * P], prT3[:, part, :],
                                      start=(part == 0), stop=False)
                        pe.matmul(bank[5][:, t * C:(t + 1) * C], onesb[0:3, :], bp3[:, :], start=False, stop=False)
                        last = pe.matmul(bank[5][:, t * C:(t + 1) * C], ident[:, :],
                                         h_all[:, bass.ds(b * TPB + t, 1), :].rearrange("p a c -> p (a c)"),
                                         start=False, stop=True)
                    last.then_inc(sem("proj_out"), 1)
                b, v = s - 1, (u - 1) % 2
                if live(b):
                    pe.wait_ge(sem("att_made0"), 4 * b + 4)
                    pe.wait_ge(sem("att_made1"), 4 * b + 4)
                    pe.wait_ge(sem("o_bias_made"), b + 1)
                    for i, (par, c) in enumerate([(0, 0), (0, 1), (1, 0), (1, 1)]):
                        for g in range(4):
                            last = pe.matmul(bank[6][32 * g:32 * g + 32, 0:S], veo[:, v, par, c, 32 * g:32 * g + 32],
                                             att[:, v, 2 * c + g // 2, g % 2, par, :],
                                             start=(i == 0), stop=(i == 3))
                    last.then_inc(sem("attended"), 1)
                b, w = s - 3, (u - 3) % RR
                if live(b):
                    pe.wait_ge(sem("row_made"), b + 1)
                    after(pe, sem("logits_made"), b)
                    after(pe, sem("slot_read"), b - 1)
                    for t in range(TPB):
                        last = pe.transpose(bank[7][:, t * P:(t + 1) * P], row[:, w, t, 0:C], ident[:, :])
                    last.then_inc(sem("x2_turned"), 1)
                if live(s):
                    scores(s, u % 2, 3)
                if isinstance(s, int) and s == -1:
                    value_weights()
                b = s + 1
                if live(b):
                    after(pe, sem("v_read"), b)
                    after(pe, sem("h2_made"), b - 2)
                    for t in range(TPB):
                        for part in range(3):
                            pe.matmul(bank[5][:, t * C:(t + 1) * C], xsT[:, bass.ds(b * S + t * P, P)],
                                      vT3[:, part, :], start=(part == 0), stop=False)
                        last = pe.matmul(bank[5][:, t * C:(t + 1) * C], onesb[0:3, :], bv3[:, :], start=False, stop=True)
                    last.then_inc(sem("v_out"), 1)

            steps(pe, -1, 7, 2, 4, B + 4, attend)

            pe.wait_ge(sem("total_made"), 1)
            pe.matmul(bank[0][:, 0:NE], onesb[:, :], total[:, :], start=True, stop=True).then_inc(sem("counted"), 1)
            pe.wait_ge(sem("map_cols"), 1)
            for i in range(2):
                pe.matmul(bank[1][0:1, i * P:(i + 1) * P], mapf[:, i:i + 1], ident[:, :], start=True, stop=True)
            pe.matmul(bank[1][:, 2 * P:3 * P], mapf[:, 0:1].to_broadcast([P, P]), ident[:, :], start=True, stop=True)\
                .then_inc(sem("map_turned"), 1)
            keep_clock(FILL[4])

            pe.wait_ge(sem("map_made"), 1)
            pe.wait_ge(sem("bias3_made"), 1)
            pe.wait_ge(sem("experts_in"), 16 * 3 * B)
            pe.wait_ge(sem("slot_read"), B)

            def expert_tile(j, u):
                if live(j, NTILE):
                    pe.wait_ge(sem("xgT_made"), j + 1)
                    pe.wait_ge(sem("weights_staged"), j + 1)
                    for c in range(2 * FC):
                        last = pe.matmul(bank[u % 2][:, c * P:(c + 1) * P], wr[:, u % WR, c * P:(c + 1) * P],
                                         xgT[:, u % 2, :], start=True, stop=True)
                    last.then_inc(sem("gu_out"), 1)
                i = j - 2
                if live(i, NTILE):
                    w = u % 2
                    e = pe.value_load(tmap[0:1, bass.ds(i, 1)], min_val=0, max_val=NE - 1)
                    if isinstance(j, int) and not live(j, NTILE):
                        pe.wait_ge(sem("hh_made"), i + 1)
                        pe.wait_ge(sem("y_made"), i - 1)
                    yb = bank[6 + w]
                    pe.matmul(yb[:, 0:C], sel3[:, bass.ds(e, 1)].to_broadcast([3 * NE, P]),
                              bias3[:, :], start=True, stop=False)
                    for c in range(FC):
                        last = pe.matmul(yb[:, 0:C], hhT[:, w, c * P:(c + 1) * P],
                                         wd[:, bass.ds(e, 1), c, :].rearrange("p a n -> p (a n)"),
                                         start=False, stop=(c == FC - 1))
                    last.then_inc(sem("y_out"), 1)
                i = j + 2
                if live(i, NTILE):
                    w = (u + 2) % XR
                    pe.wait_ge(sem(f"x_in{w}"), 16 * (i // XR + 1) if isinstance(i, int) else 2 * (i - w) + 16)
                    pe.transpose(bank[2 + w % 2][:, 0:P], xg[:, w, 0:C], ident[:, :]).then_inc(sem("x_turned"), 1)

            steps(pe, -2, 3, 11, XR, NTILE + 1, expert_tile)

        @block.scalar
        def _(act):
            act.wait_ge(sem("cols_made"), 1)

            def turn(s, u):
                b, v = s, u
                if live(b):
                    act.wait_ge(sem("grams_used"), b + 1)
                    after(act, sem("projected"), b - 1)
                    act.activation(gramsT[:, v, 2, 2:S - 1], bank[2 * v + 1][:, 2:S - 1], ACT.Copy)\
                        .then_inc(sem("gramsT_b"), 1)

            def embed(s, u):
                if not last_gather(s):
                    turn(s, u)
                b, v = s - 1, 1 - u
                if live(b):
                    act.wait_ge(sem("stats_made"), b + 1)
                    act.activation(sd[:, v, :], mv[:, v, :, 1], ACT.Sqrt, bias=eps[:, :]).then_inc(sem("sd_made"), 1)
                    act.wait_ge(sem("nmr_made"), b + 1)
                    after(act, sem("xs_made"), b - 1)
                    for t in range(TPB):
                        last = act.activation(xi[:, v, t, :],
                                              h_all[:, bass.ds(b * TPB + t, 1), :].rearrange("p a c -> p (a c)"),
                                              ACT.Relu, scale=rstd[:, v, t:t + 1], bias=nmr[:, v, t:t + 1])
                    last.then_inc(sem("xi_made"), 1)
                b = s - 2
                if live(b):
                    act.wait_ge(sem("xs_turned"), b + 1)
                    act.activation(xsT[:, bass.ds(b * S, S)], bank[6][:, 0:S // 2].bitcast(BF16), ACT.Copy)\
                        .then_inc(sem("xsT_made"), 1)
                if last_gather(s):
                    turn(s, u)

            steps(act, 0, 4, 5, 2, B + 1, embed)

            act.wait_ge(sem("bn_var"), 1)
            act.activation(bn_sd[:, :], muvar[:, 1, :], ACT.Sqrt, bias=eps[:, :]).then_inc(sem("bn_sd"), 1)
            act.wait_ge(sem("bn_made"), 1)

            def att_upper(b, v, q):
                act.wait_ge(sem("scored1"), 4 * b + (q + 1))
                if q == 0:
                    after(act, sem("attended"), b - 1)
                act.activation(att[:, v, 2 * (q // 2) + 1, q % 2].rearrange("p a n -> p (a n)"), bank[2 + q % 2][:, :],
                               ACT.Relu, scale=-1.0, bias=four[:, :]).then_inc(sem("att_made1"), 1)

            def attend(s, u):
                if live(s):
                    att_upper(s, u % 2, 0)
                b, v = s - 3, (u - 3) % 2
                if live(b):
                    act.wait_ge(sem("stats2_made"), b + 1)
                    act.activation(sd[:, v, :], mv[:, v, :, 1], ACT.Sqrt, bias=eps[:, :]).then_inc(sem("sd2_made"), 1)
                b, v = s, u % 2
                if live(b):
                    act.wait_ge(sem("v_out"), b + 1)
                    after(act, sem("v_made"), b - 1)
                    act.activation(vi[:, v].rearrange("p t c -> p (t c)"), bank[5][:, 0:S], ACT.Relu).then_inc(sem("v_read"), 1)
                if live(s):
                    att_upper(s, u % 2, 1)
                b, v, w = s - 3, (u - 3) % 2, (u - 3) % RR
                if live(b):
                    act.wait_ge(sem("nmr2_made"), b + 1)
                    hold(act, sem(f"rows_sent{w}"), rows_sent(b, w))
                    for t in range(TPB):
                        last = act.activation(row[:, w, t, 0:C],
                                              h_all[:, bass.ds(b * TPB + t, 1), :].rearrange("p a c -> p (a c)"),
                                              ACT.Identity, scale=rstd[:, v, t:t + 1], bias=nmr[:, v, t:t + 1])
                    last.then_inc(sem("row_made"), 1)
                b, v = s + 1, (u + 1) % 2
                if live(b):
                    act.wait_ge(sem("qk_out"), b + 1)
                    after(act, sem("qk_made"), b - 1)
                    act.activation(qi[:, v, :], bank[4][:, 0:S], ACT.Relu, scale=bn_a[:, 0:1], bias=bn_bh[:, 0:1])
                    act.activation(ki[:, v, :], bank[4][:, S:2 * S], ACT.Relu, scale=bn_a[:, 1:2], bias=bn_bh[:, 1:2])\
                        .then_inc(sem("qk_read"), 1)
                b = s - 2
                if live(b):
                    hold(act, sem("proj_out"), b + 1)
                    act.activation(h_all[:, bass.ds(b * TPB, TPB), :].rearrange("p t c -> p (t c)"), bank[5][:, 0:S], ACT.Copy)\
                        .then_inc(sem("h2_made"), 1)
                if live(s):
                    att_upper(s, u % 2, 2)
                if live(s):
                    att_upper(s, u % 2, 3)
                b = s - 3
                if live(b):
                    act.wait_ge(sem("x2_turned"), b + 1)
                    after(act, sem("routed"), b)
                    act.activation(x2T[:, :], bank[7][:, 0:S], ACT.Copy).then_inc(sem("x2T_made"), 1)
                b, v = s - 1, (u - 1) % 2
                if live(b):
                    act.wait_ge(sem("attended"), b + 1)
                    act.wait_ge(sem("o_bias_made"), b + 1)
                    after(act, sem("oT_made"), b - 1)
                    act.activation(oi[:, v, :], bank[6][:, 0:S], ACT.Identity, scale=o_scale[:, :], bias=o_bias[:, v:v + 1])\
                        .then_inc(sem("o_read"), 1)

            steps(act, -1, 7, 2, 4, B + 2, attend)

            act.wait_ge(sem("shifted"), 1)
            act.activation(e_all[:, :, :], e_all[:, :, :], ACT.Exp)
            act.activation(e2[:, :], e2[:, :], ACT.Exp).then_inc(sem("exps_made"), 1)

            act.wait_ge(sem("map_made"), 1)
            act.wait_ge(sem("experts_in"), 16 * 3 * B)
            act.wait_ge(sem("biases_made"), 1)

            def expert_tile(j, u):
                if live(j + 2, NTILE):
                    e = act.value_load(tmap[0:1, bass.ds(j + 2, 1)], min_val=0, max_val=NE - 1)
                if live(j, NTILE):
                    act.wait_ge(sem("gu_out"), j + 1)
                    for c in range(FC):
                        last = act.activation(sg[:, u % 2, c * P:(c + 1) * P], bank[u % 2][:, c * P:(c + 1) * P],
                                              ACT.Silu, bias=wr[:, u % WR, 2 * FF + c:2 * FF + c + 1])
                    last.then_inc(sem("silu_made"), 1)
                i = j + 2
                if live(i, NTILE):
                    if not live(j, NTILE) or isinstance(j, int):
                        after(act, sem("hh_made"), i - WR + 1)
                    act.activation(wr[:, (u + 2) % WR, :], wgu[:, bass.ds(e, 1), :].rearrange("p a n -> p (a n)"),
                                   ACT.Copy).then_inc(sem("weights_staged"), 1)

            steps(act, -2, 4, 11, XR, NTILE - 1, expert_tile)

            o = out.rearrange("b (t p) c -> p (b t) c", p=P)
            for g in range(NFG):
                if g in POOL_GROUPS:
                    act.wait_ge(sem("fin_made_pool"), 2 * TOPK * (POOL_GROUPS.index(g) + 1))
                else:
                    act.wait_ge(sem("fin_made"), TOPK * (g + 1 - sum(q < g for q in POOL_GROUPS)))
                act.dma_start(o[:, g * FG:(g + 1) * FG, :], h_all[:, g * FG:(g + 1) * FG, :]).then_inc(sem("out_written"), 16)
            act.wait_ge(sem("out_written"), 16 * NFG)

        @block.vector
        def _(dve):
            chained = [0]

            def chain(ins):
                chained[0] += 1
                ins.then_inc(sem("dve_chain"), 1)
                dve.wait_ge(sem("dve_chain"), chained[0])

            dve.memset(onesb[:, :], 1.0)
            dve.memset(onesf[:, :], 1.0)
            dve.memset(eps[:, :], EPS)
            dve.memset(four[:, :], CAP)
            dve.memset(gramsT[:, :, :, :], 0.0)
            dve.memset(xs[:, :, :, :], 1.0)
            dve.memset(veo[:, :, :, :, :], 0.0)
            dve.memset(row[:, :, :, :], 0.0)
            dve.memset(seen[:, :, :, :], 0.0)
            chain(dve.memset(picks[:, :, :, :], 0.0))
            dve.wait_ge(sem("tok_in"), 48)
            chain(dve.tensor_copy(tok_f[:, :], tok_i[:, :]))

            def push(dst, h, j):
                n = dst.shape[-1]
                t, q = h_t[:, 0:n], h_q[:, 0, 0:n]
                token = tok_f[:, HALO + P + j - n:HALO + P + j]
                chain(dve.scalar_tensor_tensor(out=t, in0=h, scalar=float(VOCAB), in1=token, op0=ALU.mult, op1=ALU.add))
                chain(dve.tensor_scalar(q, t, 1.0 / HASHED, BIG, ALU.mult, ALU.add))
                chain(dve.tensor_scalar(q, q, -BIG, -float(HASHED), ALU.add, ALU.mult))
                chain(dve.tensor_tensor(dst, t, q, ALU.add))

            push(hsh[:, 0, :], tok_f[:, HALO - 2:HALO - 2 + P + 1], 0)
            push(hsh[:, 1, :], hsh[:, 0, :], 1)
            push(hsh[:, 2, 1:], hsh[:, 1, 0:P], 1)
            chain(dve.tensor_scalar(h_q[:, :, 1:], hsh[:, :, 1:], 0.0, float(HASHED), ALU.is_lt, ALU.mult))
            chain(dve.tensor_tensor(hsh[:, :, 1:], hsh[:, :, 1:], h_q[:, :, 1:], ALU.add))
            dve.sem_inc(sem("hashed"), 1)
            dve.wait_ge(sem("ids_turned"), 1)
            dve.tensor_copy(ids[:, :, :].rearrange("p t n -> p n t"),
                            bank[0][:, 0:NG * NT].rearrange("p (n t) -> p n t", n=NG)).then_inc(sem("ids_made"), 1)

            dve.wait_ge(sem("ident_made"), 1)
            dve.tensor_copy(identb[:, :], ident[:, :]).then_inc(sem("identb_made"), 1)
            dve.wait_ge(sem("before_made"), 1)
            dve.tensor_copy(beforeb[:, :], before[:, :])
            dve.wait_ge(sem("iotas"), 4)
            chain(dve.tensor_copy(region_hi[:, :], region0[:, :]))
            dve.tensor_tensor(region_lo[:, :], region0[:, :], region_hi[:, :], ALU.subtract)
            chain(dve.tensor_copy(part_f[:, :], part_i[:, :]))
            chain(dve.tensor_scalar(head_i[:, :], part_i[:, :], 48, None, ALU.bitwise_and))
            for j in range(4):
                dve.tensor_scalar(head[:, j:j + 1], head_i[:, :], 16.0 * j, None, ALU.is_equal)
            chain(dve.tensor_scalar(upper[:, :], part_f[:, :], float(P // 2), None, ALU.is_ge))
            chain(dve.tensor_scalar(o_scale[:, :], upper[:, :], -0.5, 0.25, ALU.mult, ALU.add))

            def split(part0, part1, part2, w, r1, r2):
                chain(dve.tensor_copy(part0, w))
                chain(dve.tensor_tensor(r1, w, part0, ALU.subtract))
                chain(dve.tensor_copy(part1, r1))
                chain(dve.tensor_tensor(r2, r1, part1, ALU.subtract))
                chain(dve.tensor_copy(part2, r2))

            dve.wait_ge(sem("wemb_turned"), 1)
            dve.tensor_copy(wembT[:, :, :].rearrange("p n c -> p (n c)"), bank[1][:, 0:NG * C])
            dve.wait_ge(sem("wattn_turned"), 1)
            dve.tensor_copy(wT[:, :], bank[2][:, 0:3 * C])
            dve.tensor_copy(wprojT[:, :], bank[3][:, 0:C])
            chain(dve.tensor_copy(cols7[:, :], bank[3][:, C:C + 7]))
            split(qkT3[:, 0, :], qkT3[:, 1, :], qkT3[:, 2, :], wT[:, 0:2 * C], rest[:, :], rest2[:, :])
            split(prT3[:, 0, :], prT3[:, 1, :], prT3[:, 2, :], wprojT[:, :], rest[:, 0:C], rest2[:, 0:C])
            split(col3[:, 0, 0:1], col3[:, 0, 1:2], col3[:, 0, 2:3], cols7[:, 6:7], rest_c[:, 0, 0:1], rest_c[:, 0, 1:2])
            dve.sem_inc(sem("bp_split"), 1)
            dve.wait_ge(sem("bp_turned"), 1)
            chain(dve.tensor_copy(bp3[:, :], bank[5][0:3, 0:C // 2].bitcast(BF16)))
            dve.wait_ge(sem("bias_turned"), 1)
            dve.tensor_copy(wgu[:, :, 2 * FF:].rearrange("p e c -> p c e"),
                            bank[4][:, P:P + 2 * FC * NE].rearrange("p (c e) -> p c e", e=NE)).then_inc(sem("biases_made"), 1)
            dve.sem_inc(sem("setup_done"), 1)
            dve.sem_inc(sem("cols_made"), 1)
            dve.wait_ge(sem("bias_in"), 48)
            chain(dve.tensor_copy(bias3[0:NE, :], bias_f[:, 2 * FF:]))
            chain(dve.tensor_tensor(bias_r[:, :], bias_f[:, 2 * FF:], bias3[0:NE, :], ALU.subtract))
            chain(dve.tensor_copy(bias_m[:, :], bias_r[:, :]))
            chain(dve.tensor_copy(bias3[NE:2 * NE, :], bias_m[:, :]))
            chain(dve.tensor_tensor(bias_r[:, :], bias_r[:, :], bias_m[:, :], ALU.subtract))
            chain(dve.tensor_copy(bias3[2 * NE:3 * NE, :], bias_r[:, :]))
            for i in range(3):
                chain(dve.tensor_copy(sel3[i * NE:(i + 1) * NE, :], identb[0:NE, 0:NE]))
            dve.sem_inc(sem("bias3_made"), 1)

            dve.wait_ge(sem("projb_in"), 16)

            def turn(s, u):
                b, v = s, u
                if live(b):
                    dve.wait_ge(sem("grams_used"), b + 1)
                    after(dve, sem("projected"), b - 1)
                    dve.tensor_copy(gramsT[:, v, 0, 1:S], bank[2 * v][:, 1:S])
                    dve.tensor_copy(gramsT[:, v, 1, 1:S - 1], bank[2 * v][:, S + 1:2 * S - 1]).then_inc(sem("gramsT_a"), 1)

            def embed(s, u):
                b, v = s - 2, u
                if live(b):
                    dve.wait_ge(sem("xi_made"), b + 1)
                    after(dve, sem("xs_turned"), b - 1)
                    dve.tensor_scalar(xs[:, v, :, 0:C], xi[:, v], CAP, None, ALU.min).then_inc(sem("xs_made"), 1)
                if not last_gather(s):
                    turn(s, u)
                b, v = s - 1, 1 - u
                if live(b):
                    dve.wait_ge(sem("projected"), b + 1)
                    hb = h_all[:, bass.ds(b * TPB, TPB), :]
                    dve.tensor_tensor(hb, bank[4 + v][:, 0:S].rearrange("p (t c) -> p t c", c=C),
                                      projb_bc[:, :].rearrange("p (a c) -> p a c", a=1).to_broadcast([P, TPB, C]),
                                      ALU.add).then_inc(sem("h_made"), 1)
                    hold(dve, sem("h_made"), b + 1)
                    for t in range(TPB):
                        last = dve.bn_stats(st[:, v, t, :], h_all[:, bass.ds(b * TPB + t, 1), :].rearrange("p a c -> p (a c)"))
                    last.then_inc(sem("halves_made"), 1)
                    hold(dve, sem("halves_made"), b + 1)
                    for t in range(TPB):
                        last = dve.bn_aggr(mv[:, v, t, :], st[:, v, t, :])
                    last.then_inc(sem("stats_made"), 1)
                    dve.wait_ge(sem("sd_made"), b + 1)
                    dve.reciprocal(rstd[:, v, :], sd[:, v, :]).then_inc(sem("rstd_made"), 1)
                    dve.wait_ge(sem("rstd_made"), b + 1)
                    dve.scalar_tensor_tensor(out=nmr[:, v, :], in0=mv[:, v, :, 0], scalar=-1.0, in1=rstd[:, v, :],
                                             op0=ALU.mult, op1=ALU.mult).then_inc(sem("nmr_made"), 1)
                if last_gather(s):
                    turn(s, u)

            steps(dve, 0, 4, 5, 2, B + 1, embed)

            dve.wait_ge(sem("xs_turned"), B)
            dve.tensor_scalar(gn[:, :], bank[7][:, 0:C + 1], 1.0 / NTOK, None, ALU.mult).then_inc(sem("mean_made"), 1)
            dve.wait_ge(sem("mean_turned"), 1)
            dve.tensor_copy(mrow[:, :], bank[0][0:1, 0:P]).then_inc(sem("mrow_made"), 1)
            dve.wait_ge(sem("mm_made"), 1)
            dve.tensor_tensor(cov[:, :], gn[:, 0:C], bank[1][:, 0:C], ALU.subtract).then_inc(sem("cov_made"), 1)
            dve.wait_ge(sem("covw"), 1)
            dve.tensor_tensor(wtc[:, :], wT[:, :], bank[2][:, 0:3 * C], ALU.mult).then_inc(sem("wtc_made"), 1)
            dve.wait_ge(sem("muvar_made"), 1)
            dve.tensor_copy(muvar[:, :, :].rearrange("p a g -> p (a g)"), bank[3][:, 0:6]).then_inc(sem("bn_var"), 1)
            dve.wait_ge(sem("bn_sd"), 1)
            chain(dve.reciprocal(bn_r[:, :], bn_sd[:, :]))
            chain(dve.tensor_tensor(bn_a[:, :], bn_r[:, :], cols7[:, 0:3], ALU.mult))
            chain(dve.tensor_tensor(bn_ma[:, :], muvar[:, 0, :], bn_a[:, :], ALU.mult))
            chain(dve.tensor_tensor(bn_b[:, :], cols7[:, 3:6], bn_ma[:, :], ALU.subtract))
            chain(dve.tensor_scalar(bn_bh[:, :], bn_b[:, :], HALF_UP, None, ALU.add))
            dve.sem_inc(sem("bn_made"), 1)
            dve.tensor_scalar(wv[:, :], wqkv[:, 2, :], bn_a[:, 2:3], None, ALU.mult)
            split(col3[:, 1, 0:1], col3[:, 1, 1:2], col3[:, 1, 2:3], bn_bh[:, 2:3], rest_c[:, 1, 0:1], rest_c[:, 1, 1:2])
            dve.sem_inc(sem("wv_made"), 1)
            dve.wait_ge(sem("wgate_in"), 32)

            def att_lower(b, v, q):
                dve.wait_ge(sem("scored0"), 4 * b + (q + 1))
                if q == 0:
                    after(dve, sem("attended"), b - 1)
                dve.tensor_scalar(att[:, v, 2 * (q // 2), q % 2].rearrange("p a n -> p (a n)"), bank[q % 2][:, :],
                                  CAP, None, ALU.min).then_inc(sem("att_made0"), 1)

            def attend(s, u):
                if live(s):
                    att_lower(s, u % 2, 0)
                b, v = s - 2, (u - 2) % 2
                if live(b):
                    dve.wait_ge(sem("o_read"), b + 1)
                    after(dve, sem("proj_out"), b - 1)
                    dve.tensor_scalar(oT[:, v, :], oi[:, v, :], CAP, None, ALU.min).then_inc(sem("oT_made"), 1)
                b, v = s - 3, (u - 3) % 2
                if live(b):
                    dve.wait_ge(sem("sd2_made"), b + 1)
                    dve.reciprocal(rstd[:, v, :], sd[:, v, :]).then_inc(sem("rstd2_made"), 1)
                    dve.wait_ge(sem("rstd2_made"), b + 1)
                    dve.scalar_tensor_tensor(out=nmr[:, v, :], in0=mv[:, v, :, 0], scalar=-1.0, in1=rstd[:, v, :],
                                             op0=ALU.mult, op1=ALU.mult).then_inc(sem("nmr2_made"), 1)
                if live(s):
                    att_lower(s, u % 2, 1)
                b, v = s - 5, (u - 5) % 2
                if live(b):
                    dve.wait_ge(sem("ranked"), b + 1)
                    dve.tensor_tensor(placed[:, :, :, :], chosen[:, v],
                                      bank[7][:, TPB * NE:2 * TPB * NE].rearrange("p (t a e) -> p t a e", a=1, e=NE)
                                      .to_broadcast([P, TPB, TOPK, NE]), ALU.mult).then_inc(sem("slot_read"), 1)
                b = s - 4
                if live(b):
                    dve.wait_ge(sem("routed"), b + 1)
                    after(dve, sem("lg_kept"), b)
                    dve.tensor_tensor(lg[:, :, 0:NE],
                                      bank[7][:, 0:TPB * NE].rearrange("p (t e) -> p t e", e=NE),
                                      bgate_bc[:, :].rearrange("p (a e) -> p a e", a=1).to_broadcast([P, TPB, NE]),
                                      ALU.add).then_inc(sem("logits_made"), 1)
                b, v = s - 1, (u - 1) % 2
                if live(b):
                    dve.wait_ge(sem("v_summed"), b + 1)
                    after(dve, sem("o_read"), b - 1)
                    dve.tensor_scalar(o_bias[:, v:v + 1], bank[6][:, S:S + 1], upper[:, 0:1], 0.0625, ALU.mult, ALU.add)\
                        .then_inc(sem("o_bias_made"), 1)
                b = s - 4
                if live(b):
                    hold(dve, sem("logits_made"), b + 1)
                    for t in range(TPB):
                        last = dve.max(lg[:, t, NE:], lg[:, t, 0:NE])
                    last.then_inc(sem("top_made"), 1)
                if live(s):
                    att_lower(s, u % 2, 2)
                b, w = s - 5, (u - 5) % RR
                if live(b):
                    dve.wait_ge(sem("slot_read"), b + 1)
                    with nc.allow_low_precision(reason="one term of a sum isn't zero, an integer below 2^24"):
                        dve.tensor_reduce(slot[:, w, :], placed[:, :, :, :].rearrange("p t k e -> p (t k) e"), AX, ALU.add)\
                            .then_inc(sem("slot_made"), 1)
                b = s - 4
                if live(b):
                    hold(dve, sem("top_made"), b + 1)
                    for t in range(TPB):
                        last = dve.max_index(topi[:, t, :], lg[:, t, NE:], lg[:, t, 0:NE])
                    last.then_inc(sem("topi_made"), 1)
                    if not live(s):
                        dve.tensor_copy(lg_all[:, bass.ds(b * TPB, TPB), :], lg[:, :, :]).then_inc(sem("lg_kept"), 1)
                b, v = s + 1, (u + 1) % 2
                if live(b):
                    dve.wait_ge(sem("qk_read"), b + 1)
                    after(dve, sem("scored1"), 4 * (b - 1))
                    for j in range(4):
                        dve.tensor_scalar(qh[:, v, j, :], qi[:, v, :], CAP, head[:, j:j + 1], ALU.min, ALU.mult)
                    dve.tensor_scalar(kT[:, v, :], ki[:, v, :], CAP, None, ALU.min).then_inc(sem("qk_made"), 1)
                if live(s):
                    att_lower(s, u % 2, 3)
                b, w = s - 4, (u - 4) % RR
                if live(b):
                    dve.wait_ge(sem("topi_made"), b + 1)
                    dve.tensor_copy(topf[:, :, :], topi[:, :, 0:TOPK]).then_inc(sem("topf_made"), 1)
                    dve.tensor_copy(row[:, w, :, C + 1:C + 2], topi[:, :, 0:1])
                b, v = s - 2, (u - 2) % 2
                if live(b):
                    hold(dve, sem("h2_made"), b + 1)
                    for t in range(TPB):
                        last = dve.bn_stats(st[:, v, t, :], h_all[:, bass.ds(b * TPB + t, 1), :].rearrange("p a c -> p (a c)"))
                    last.then_inc(sem("halves2_made"), 1)
                b, v = s - 4, (u - 4) % 2
                if live(b):
                    dve.wait_ge(sem("topf_made"), b + 1)
                    dve.tensor_tensor(chosen[:, v].rearrange("p t k e -> p (t k) e"),
                                      iota_e[:, :].rearrange("p (a e) -> p a e", a=1).to_broadcast([P, TPB * TOPK, NE]),
                                      topf[:, :, :].rearrange("p t (k a) -> p (t k) a", a=1).to_broadcast([P, TPB * TOPK, NE]),
                                      ALU.is_equal).then_inc(sem("chosen_made"), 1)
                b, v = s - 2, (u - 2) % 2
                if live(b):
                    after(dve, sem("row_made"), b - 1)
                    hold(dve, sem("halves2_made"), b + 1)
                    for t in range(TPB):
                        last = dve.bn_aggr(mv[:, v, t, :], st[:, v, t, :])
                    last.then_inc(sem("stats2_made"), 1)
                b, v = s - 4, (u - 4) % 2
                if live(b):
                    dve.wait_ge(sem("chosen_made"), b + 1)
                    after(dve, sem("ranked"), b)
                    dve.tensor_tensor(seen[:, v, 0, :], seen[:, 1 - v, 1, :], picks[:, 1 - v, 1, :], ALU.add)
                    dve.tensor_tensor(picks[:, v], chosen[:, v, :, 0, :], chosen[:, v, :, 1, :], ALU.add)\
                        .then_inc(sem("picked"), 1)
                b, v = s - 4, (u - 4) % 2
                if live(b):
                    dve.wait_ge(sem("picked"), b + 1)
                    dve.tensor_tensor(seen[:, v, 1, :], seen[:, v, 0, :], picks[:, v, 0, :], ALU.add)\
                        .then_inc(sem("picks_made"), 1)

            attend(-1, 3)
            dve.wait_ge(sem("wv_turned"), 1)
            dve.tensor_copy(bv3[:, :], bank[1][0:3, 0:C // 2].bitcast(BF16))
            split(vT3[:, 0, :], vT3[:, 1, :], vT3[:, 2, :], bank[0][:, 0:C], rest[:, 0:C], rest2[:, 0:C])
            dve.sem_inc(sem("vT_made"), 1)
            steps(dve, 0, 7, 2, 4, B + 4, attend)

            v = (B - 1) % 2
            chain(dve.tensor_tensor(total[:, :], seen[:, v, 1, :], picks[:, v, 1, :], ALU.add))
            dve.sem_inc(sem("total_made"), 1)
            dve.wait_ge(sem("counted"), 1)
            chain(dve.tensor_copy(count[:, :], bank[0][:, 0:NE]))
            chain(dve.tensor_scalar(ntile_i[:, :], count[:, :], P / 2 - 0.5, 1.0 / P, ALU.add, ALU.mult))
            chain(dve.tensor_copy(ntile[:, :], ntile_i[:, :]))
            chain(dve.tensor_tensor_scan(upto_t[:, :], onesf[:, :], ntile[:, :], 0.0, ALU.mult, ALU.add))
            chain(dve.tensor_tensor(prev_t[:, :], upto_t[:, :], ntile[:, :], ALU.subtract))
            chain(dve.scalar_tensor_tensor(out=origin[:, :], in0=prev_t[:, :], scalar=float(P), in1=count[:, :],
                                           op0=ALU.mult, op1=ALU.add))
            chain(dve.scalar_tensor_tensor(out=origin[:, :], in0=region0[:, :], scalar=-float(P), in1=origin[:, :],
                                           op0=ALU.add, op1=ALU.add))
            chain(dve.tensor_scalar(passed[:, :], upto_t[:, :], part_f[:, 0:1], None, ALU.is_le))
            chain(dve.tensor_reduce(mapc[:, 0:1], passed[:, :], AX, ALU.add))
            chain(dve.tensor_scalar(owner[:, :], iota_e[:, :], mapc[:, 0:1], None, ALU.is_equal))
            chain(dve.tensor_tensor(owner[:, :], owner[:, :], origin[:, :], ALU.mult))
            chain(dve.tensor_reduce(mapc[:, 1:2], owner[:, :], AX, ALU.add))
            chain(dve.scalar_tensor_tensor(out=mapf[:, 1:2], in0=part_f[:, :], scalar=-float(P), in1=mapc[:, 1:2],
                                           op0=ALU.mult, op1=ALU.add))
            chain(dve.tensor_scalar(mapf[:, 1:2], mapf[:, 1:2], 0.0, None, ALU.max))
            chain(dve.tensor_scalar(mapf[:, 0:1], mapc[:, 0:1], float(NE - 1), None, ALU.min))
            dve.sem_inc(sem("map_cols"), 1)
            dve.wait_ge(sem("lg_kept"), B)
            dve.tensor_tensor(e2[:, :], lg_all[:, :, NE + 1], lg_all[:, :, NE], ALU.subtract)
            chain(dve.tensor_tensor(e_all[:, :, :], lg_all[:, :, 0:NE], lg_all[:, :, NE:NE + 1].to_broadcast([P, NT, NE]), ALU.subtract))
            dve.sem_inc(sem("shifted"), 1)
            dve.wait_ge(sem("map_turned"), 1)
            dve.tensor_copy(tmap[:, :], bank[1][0:1, 0:2 * P]).then_inc(sem("map_made"), 1)
            chain(dve.tensor_copy(tile_e, bank[1][:, 2 * P:3 * P]))

            def sent(i, u):
                return 16 * (i // XR + 1) if isinstance(i, int) else 2 * (i - u) + 16

            def expert_tile(j, u):
                if isinstance(j, int) and j == 1:
                    dve.wait_ge(sem("exps_made"), 1)
                    chain(dve.tensor_reduce(den[:, :], e_all[:, :, :], AX, ALU.add))
                    chain(dve.reciprocal(w12[:, 0, :], den[:, :]))
                    chain(dve.tensor_tensor(w12[:, 1, :], w12[:, 0, :], e2[:, :], ALU.mult))
                    dve.sem_inc(sem("weights_made"), 1)
                i = j - 1
                if live(i, NTILE):
                    w = (u - 1) % 2
                    dve.wait_ge(sem("silu_made"), i + 1)
                    after(dve, sem("y_out"), i - 1)
                    for c in range(FC):
                        last = dve.scalar_tensor_tensor(out=hhT[:, w, c * P:(c + 1) * P],
                                                        in0=bank[w][:, FF + c * P:FF + (c + 1) * P],
                                                        scalar=wr[:, (u - 1) % WR, 2 * FF + FC + c:2 * FF + FC + c + 1],
                                                        in1=sg[:, w, c * P:(c + 1) * P], op0=ALU.add, op1=ALU.mult)
                    last.then_inc(sem("hh_made"), 1)
                i = j - 3
                if live(i, NTILE):
                    w = (u - 3) % YR
                    if not live(j - 1, NTILE):
                        dve.wait_ge(sem("y_out"), i + 1)
                    q = (u - 3 - YR) % XR
                    after(dve, sem(f"y_sent{q}"), sent(i - YR, q))
                    dve.tensor_copy(yy[:, w, :], bank[6 + w % 2][:, 0:C]).then_inc(sem("y_made"), 1)
                i = j + 1
                if live(i, NTILE):
                    w = (u + 1) % XR
                    dve.wait_ge(sem("x_turned"), i + 1)
                    dve.tensor_copy(xgT[:, w % 2, :], bank[2 + w % 2][:, 0:P]).then_inc(sem("xgT_made"), 1)
                    dve.scalar_tensor_tensor(out=pair_i[:, w, :], in0=xg[:, w, C + 1:C + 2], scalar=tile_e[:, bass.ds(i, 1)],
                                             in1=xg[:, w, C:C + 1], op0=ALU.not_equal, op1=ALU.add)\
                        .then_inc(sem("pair_kept"), 1)

            steps(dve, -1, 7, 10, XR, NTILE + 2, expert_tile)

            for n, g in enumerate(g for g in range(NFG) if g not in POOL_GROUPS):
                dve.wait_ge(sem(f"fin_in{g}"), 16)
                for k in range(TOPK):
                    for t in range(g * FG, (g + 1) * FG):
                        last = dve.scalar_tensor_tensor(out=h_all[:, t, :], in0=y_fin[:, g, t - g * FG, k, :],
                                                        scalar=w12[:, k, t:t + 1], in1=h_all[:, t, :],
                                                        op0=ALU.mult, op1=ALU.add)
                    last.then_inc(sem("fin_made"), 1)
                    if k < TOPK - 1:
                        dve.wait_ge(sem("fin_made"), TOPK * n + k + 1)


_INS = ['x', 'L0_tok_emb_2', 'L0_tok_emb_3', 'L0_tok_emb_4', 'L0_tok_proj_w', 'L0_tok_proj_b', 'L0_attn_Wqkv',
        'L0_attn_gamma', 'L0_attn_beta', 'L0_attn_Wproj', 'L0_attn_bproj', 'L0_ffn_Wgate', 'L0_ffn_bgate',
        'L0_ffn_Wg', 'L0_ffn_bg', 'L0_ffn_Wu', 'L0_ffn_bu', 'L0_ffn_Wd', 'L0_ffn_bd']


def kernel(**inputs):
    import numpy as _np
    import concourse.bacc as _bacc
    from concourse import mybir as _mybir
    from concourse.bass_utils import run_bass_kernel_spmd as _run

    nc = _bacc.Bacc("TRN2", target_bir_lowering=False, num_devices=1)
    arrays, aps = {}, {}
    for name in _INS:
        a = _np.ascontiguousarray(inputs[name])
        arrays[f"in_{name}"] = a
        aps[name] = nc.dram_tensor(f"in_{name}", a.shape, _mybir.dt.from_np(a.dtype), kind="ExternalInput").ap()
    out = nc.dram_tensor("out_h", (B, S, C), F32, kind="ExternalOutput").ap()
    a = [aps[n] for n in _INS]
    build(nc, a[0], a[1:4], *a[4:], out)
    r = _run(nc, [arrays], core_ids=[0])
    return r.results[0]["out_h"]
```
